# Optimizing a Trainium2 kernel written in Bass

```python
import numpy as np
import jax
import jax.numpy as jnp

def _softmax(x, axis=-1):
    return jax.nn.softmax(x, axis=axis)
def _gelu(x):
    return jax.nn.gelu(x, approximate=True)
def _silu(x):
    return jax.nn.silu(x)
def _sigmoid(x):
    return jax.nn.sigmoid(x)
def _layernorm(x, axis=-1, eps=1e-5):
    m = jnp.mean(x, axis=axis, keepdims=True)
    v = jnp.var(x, axis=axis, keepdims=True)
    return (x - m) / jnp.sqrt(v + eps)
def _scatter_add(tgt, idx, src, axis=0):
    return tgt.at[idx].add(src)
def _segment_sum(src, seg, n):
    return jax.ops.segment_sum(src, seg, n)

kernel_name = 'mk_conv_preact_d2_conv_nhwc128_a2a4be'

def setup_inputs(seed: int = 0):
    np.random.seed(seed)
    _w = jnp.asarray
    def _rec_inputs():
        import jax
        import jax.numpy as jnp
        _gk = jax.random.key(seed)
        x = 7.22e-05 + 1 * jax.random.normal(jax.random.fold_in(_gk, 1), (1, 256, 256, 128), jnp.float32)
        return x
    x = _rec_inputs()
    def _L0_conv_setup():
        import jax, jax.numpy as jnp
        import numpy as np
        H = 4
        C = 32
        CZ = 128
        N = 256
        B = 1
        EPS = 1e-05
        key = jax.random.key(seed)
        ks = jax.random.split(key, 8)
        hc = H * C
        return {'z': jax.random.normal(ks[0], (B, N, N, CZ), dtype=jnp.float32), 'ln_scale': jnp.ones((CZ,), dtype=jnp.float32), 'ln_bias': jnp.zeros((CZ,), dtype=jnp.float32), 'Wq': jax.random.normal(ks[1], (CZ, hc), dtype=jnp.float32) * 0.02, 'Wk': jax.random.normal(ks[2], (CZ, hc), dtype=jnp.float32) * 0.02, 'Wv': jax.random.normal(ks[3], (CZ, hc), dtype=jnp.float32) * 0.02, 'Wb': jax.random.normal(ks[4], (CZ, H), dtype=jnp.float32) * 0.02, 'Wg': jax.random.normal(ks[5], (CZ, hc), dtype=jnp.float32) * 0.02, 'Wo': jax.random.normal(ks[6], (hc, CZ), dtype=jnp.float32) * 0.02}
    _L0_conv_all = _L0_conv_setup()
    _L0_conv_in = {k: v for k, v in _L0_conv_all.items() if k in ('ln_scale', 'ln_bias', 'Wq', 'Wk', 'Wv', 'Wb', 'Wg', 'Wo', )}
    del _L0_conv_all

    def _L1_conv_setup():
        import jax, jax.numpy as jnp
        import numpy as np
        D_MODEL = 128
        D_STATE = 16
        D_INNER = 256
        DT_RANK = 8
        K = 4
        B, H, W = (2, 64, 64)

        def silu(x):
            return x * jax.nn.sigmoid(x)

        def selective_scan(xs, dts, As, Bs, Cs, Ds, dt_bias):
            delta = jax.nn.softplus(dts + dt_bias[None, :, :, None])
            d_l = jnp.moveaxis(delta, -1, 0)
            x_l = jnp.moveaxis(xs, -1, 0)
            B_l = jnp.moveaxis(Bs, -1, 0)
            C_l = jnp.moveaxis(Cs, -1, 0)

            def step(h, inp):
                d_t, x_t, B_t, C_t = inp
                dA = jnp.exp(d_t[..., None] * As)
                h = dA * h + (d_t * x_t)[..., None] * B_t[:, :, None, :]
                y = jnp.einsum('bkdn,bkn->bkd', h, C_t)
                return (h, y)
            h0 = jnp.zeros((xs.shape[0], K, As.shape[1], As.shape[2]), xs.dtype)
            _, ys = jax.lax.scan(step, h0, (d_l, x_l, B_l, C_l))
            ys = jnp.moveaxis(ys, 0, -1)
            return ys + Ds[None, :, :, None] * xs
        key = jax.random.key(seed)
        ks = jax.random.split(key, 8)
        f = lambda k, s, scale=0.02: jax.random.normal(k, s, dtype=jnp.float32) * scale
        A = jnp.tile(jnp.arange(1, D_STATE + 1, dtype=jnp.float32)[None, :], (K * D_INNER, 1))
        return {'x': jax.random.normal(ks[0], (B, H, W, D_MODEL), dtype=jnp.float32), 'w_in': f(ks[1], (2 * D_INNER, D_MODEL)), 'conv_w': f(ks[2], (D_INNER, 1, 3, 3)), 'conv_b': jnp.zeros((D_INNER,), jnp.float32), 'x_proj_w': f(ks[3], (K, DT_RANK + 2 * D_STATE, D_INNER)), 'dt_w': f(ks[4], (K, D_INNER, DT_RANK)), 'dt_b': f(ks[5], (K, D_INNER), 0.1), 'A_logs': jnp.log(A), 'Ds': jnp.ones((K * D_INNER,), jnp.float32), 'ln_w': jnp.ones((D_INNER,), jnp.float32), 'ln_b': jnp.zeros((D_INNER,), jnp.float32), 'w_out': f(ks[6], (D_MODEL, D_INNER))}
    _L1_conv_all = _L1_conv_setup()
    _L1_conv_in = {k: v for k, v in _L1_conv_all.items() if k in ('w_in', 'conv_w', 'conv_b', 'x_proj_w', 'dt_w', 'dt_b', 'A_logs', 'Ds', 'ln_w', 'ln_b', 'w_out', )}
    del _L1_conv_all

    return {
        "x": x,
        "L0_conv_ln_scale": _L0_conv_in["ln_scale"],
        "L0_conv_ln_bias": _L0_conv_in["ln_bias"],
        "L0_conv_Wq": _L0_conv_in["Wq"],
        "L0_conv_Wk": _L0_conv_in["Wk"],
        "L0_conv_Wv": _L0_conv_in["Wv"],
        "L0_conv_Wb": _L0_conv_in["Wb"],
        "L0_conv_Wg": _L0_conv_in["Wg"],
        "L0_conv_Wo": _L0_conv_in["Wo"],
        "L1_conv_w_in": _L1_conv_in["w_in"],
        "L1_conv_conv_w": _L1_conv_in["conv_w"],
        "L1_conv_conv_b": _L1_conv_in["conv_b"],
        "L1_conv_x_proj_w": _L1_conv_in["x_proj_w"],
        "L1_conv_dt_w": _L1_conv_in["dt_w"],
        "L1_conv_dt_b": _L1_conv_in["dt_b"],
        "L1_conv_A_logs": _L1_conv_in["A_logs"],
        "L1_conv_Ds": _L1_conv_in["Ds"],
        "L1_conv_ln_w": _L1_conv_in["ln_w"],
        "L1_conv_ln_b": _L1_conv_in["ln_b"],
        "L1_conv_w_out": _L1_conv_in["w_out"],
    }

def reference(x, L0_conv_ln_scale, L0_conv_ln_bias, L0_conv_Wq, L0_conv_Wk, L0_conv_Wv, L0_conv_Wb, L0_conv_Wg, L0_conv_Wo, L1_conv_w_in, L1_conv_conv_w, L1_conv_conv_b, L1_conv_x_proj_w, L1_conv_dt_w, L1_conv_dt_b, L1_conv_A_logs, L1_conv_Ds, L1_conv_ln_w, L1_conv_ln_b, L1_conv_w_out):
    import jax
    import jax.numpy as jnp
    def _L0_conv_ref(z, ln_scale, ln_bias, Wq, Wk, Wv, Wb, Wg, Wo):
        import jax, jax.numpy as jnp
        import numpy as np
        H = 4
        C = 32
        CZ = 128
        N = 256
        B = 1
        EPS = 1e-05
        b, n = (z.shape[0], z.shape[1])
        mu = jnp.mean(z, axis=-1, keepdims=True)
        var = jnp.mean(jnp.square(z - mu), axis=-1, keepdims=True)
        zn = (z - mu) * jax.lax.rsqrt(var + EPS) * ln_scale + ln_bias
        q = (zn @ Wq).reshape(b, n, n, H, C)
        k = (zn @ Wk).reshape(b, n, n, H, C)
        v = (zn @ Wv).reshape(b, n, n, H, C)
        bias = zn @ Wb
        g = jax.nn.sigmoid(zn @ Wg).reshape(b, n, n, H, C)
        scores = jnp.einsum('bijhd,bikhd->bijkh', q, k) * (1.0 / C ** 0.5)
        scores = scores + bias[:, None, :, :, :]
        a = jax.nn.softmax(scores, axis=-2)
        o = jnp.einsum('bijkh,bikhd->bijhd', a, v)
        o = (g * o).reshape(b, n, n, H * C)
        return o @ Wo

    def _L1_conv_ref(x, w_in, conv_w, conv_b, x_proj_w, dt_w, dt_b, A_logs, Ds, ln_w, ln_b, w_out):
        import jax, jax.numpy as jnp
        import numpy as np
        D_MODEL = 128
        D_STATE = 16
        D_INNER = 256
        DT_RANK = 8
        K = 4
        B, H, W = (2, 64, 64)

        def silu(x):
            return x * jax.nn.sigmoid(x)

        def selective_scan(xs, dts, As, Bs, Cs, Ds, dt_bias):
            delta = jax.nn.softplus(dts + dt_bias[None, :, :, None])
            d_l = jnp.moveaxis(delta, -1, 0)
            x_l = jnp.moveaxis(xs, -1, 0)
            B_l = jnp.moveaxis(Bs, -1, 0)
            C_l = jnp.moveaxis(Cs, -1, 0)

            def step(h, inp):
                d_t, x_t, B_t, C_t = inp
                dA = jnp.exp(d_t[..., None] * As)
                h = dA * h + (d_t * x_t)[..., None] * B_t[:, :, None, :]
                y = jnp.einsum('bkdn,bkn->bkd', h, C_t)
                return (h, y)
            h0 = jnp.zeros((xs.shape[0], K, As.shape[1], As.shape[2]), xs.dtype)
            _, ys = jax.lax.scan(step, h0, (d_l, x_l, B_l, C_l))
            ys = jnp.moveaxis(ys, 0, -1)
            return ys + Ds[None, :, :, None] * xs
        xz = x @ w_in.T
        xi, z = jnp.split(xz, 2, axis=-1)
        z = silu(z)
        xc = jnp.transpose(xi, (0, 3, 1, 2))
        xc = jax.lax.conv_general_dilated(xc, conv_w, (1, 1), 'SAME', feature_group_count=D_INNER, dimension_numbers=('NCHW', 'OIHW', 'NCHW')) + conv_b[None, :, None, None]
        xc = silu(xc)
        b, d, h, w = xc.shape
        L = h * w
        x_flat = xc.reshape(b, d, L)
        x_t = jnp.transpose(xc, (0, 1, 3, 2)).reshape(b, d, L)
        x_hwwh = jnp.stack([x_flat, x_t], axis=1)
        xs = jnp.concatenate([x_hwwh, jnp.flip(x_hwwh, axis=-1)], axis=1)
        x_dbl = jnp.einsum('bkdl,kcd->bkcl', xs, x_proj_w)
        dts, Bs, Cs = jnp.split(x_dbl, [DT_RANK, DT_RANK + D_STATE], axis=2)
        dts = jnp.einsum('bkrl,kdr->bkdl', dts, dt_w)
        As = -jnp.exp(A_logs).reshape(K, d, D_STATE)
        out_y = selective_scan(xs, dts, As, Bs, Cs, Ds.reshape(K, d), dt_b)
        inv_y = jnp.flip(out_y[:, 2:4], axis=-1)
        wh_y = jnp.transpose(out_y[:, 1].reshape(b, d, w, h), (0, 1, 3, 2)).reshape(b, d, L)
        invwh_y = jnp.transpose(inv_y[:, 1].reshape(b, d, w, h), (0, 1, 3, 2)).reshape(b, d, L)
        y = out_y[:, 0] + inv_y[:, 0] + wh_y + invwh_y
        y = jnp.transpose(y, (0, 2, 1))
        mu = y.mean(-1, keepdims=True)
        var = ((y - mu) ** 2).mean(-1, keepdims=True)
        y = (y - mu) / jnp.sqrt(var + 1e-05) * ln_w + ln_b
        y = y.reshape(b, h, w, d) * z
        return y @ w_out.T

    def _gn(v, G=32, eps=1e-5):
        B_, H_, W_, C_ = v.shape
        g = v.reshape(B_, H_, W_, G, C_ // G)
        m = jnp.mean(g, axis=(1, 2, 4), keepdims=True)
        s = jnp.var(g, axis=(1, 2, 4), keepdims=True)
        return ((g - m) / jnp.sqrt(s + eps)).reshape(v.shape)

    def _ln_c(v, eps=1e-6):
        m = jnp.mean(v, axis=-1, keepdims=True)
        s = jnp.var(v, axis=-1, keepdims=True)
        return (v - m) / jnp.sqrt(s + eps)

    def _ln_t(v, eps=1e-5):
        m = jnp.mean(v, axis=-1, keepdims=True)
        s = jnp.var(v, axis=-1, keepdims=True)
        return (v - m) / jnp.sqrt(s + eps)

    def _to_tokens(v):
        B_, H_, W_, C_ = v.shape
        return v.reshape(B_, H_ * W_, C_)
    def _from_tokens(t, like):
        return t.reshape(like.shape)

    x = x + _L0_conv_ref(_gn(x), L0_conv_ln_scale, L0_conv_ln_bias, L0_conv_Wq, L0_conv_Wk, L0_conv_Wv, L0_conv_Wb, L0_conv_Wg, L0_conv_Wo)
    x = x + _L1_conv_ref(_gn(x), L1_conv_w_in, L1_conv_conv_w, L1_conv_conv_b, L1_conv_x_proj_w, L1_conv_dt_w, L1_conv_dt_b, L1_conv_A_logs, L1_conv_Ds, L1_conv_ln_w, L1_conv_ln_b, L1_conv_w_out)
    return x


_drawn_inputs = setup_inputs


def setup_inputs(seed=0):
    import zlib

    import numpy as np

    out = dict(_drawn_inputs(seed))
    spreads = {'L0_conv_ln_scale': (1.0, 0.6),
     'L0_conv_ln_bias': (0.0, 0.8),
     'L1_conv_conv_b': (0.0, 0.1),
     'L1_conv_Ds': (1.0, 0.6),
     'L1_conv_ln_w': (1.0, 0.6),
     'L1_conv_ln_b': (0.0, 0.8)}
    factors = {'L0_conv_Wq': 8.0,
     'L0_conv_Wk': 8.0,
     'L0_conv_Wv': 8.0,
     'L0_conv_Wb': 8.0,
     'L0_conv_Wg': 8.0,
     'L0_conv_Wo': 8.0,
     'L1_conv_conv_w': 8.0,
     'L1_conv_x_proj_w': 8.0,
     'L1_conv_dt_w': 8.0,
     'L1_conv_dt_b': 8.0,
     'L1_conv_A_logs': 8.0}
    for name, (base, spread) in spreads.items():
        noise = np.random.default_rng([zlib.crc32(name.encode()), seed]).standard_normal(out[name].shape)
        drawn = base * np.exp(spread * noise) if base else spread * noise
        out[name] = jnp.asarray(drawn.astype(out[name].dtype))
    for name, factor in factors.items():
        out[name] = (out[name] * factor).astype(out[name].dtype)
    return out
```

```python
from contextlib import ExitStack

import numpy as np
import concourse.bass as bass
from concourse import mybir

F32 = mybir.dt.float32
BF16 = mybir.dt.bfloat16
ALU = mybir.AluOpType
ACT = mybir.ActivationFunctionType
AX_X = mybir.AxisListType.X

P = 128
SIDE = 256
TOKENS = SIDE * SIDE
C = 128
GROUPS = 32
PER_GROUP = C // GROUPS
HEADS, HEAD_DIM = 4, 32
JB = SIDE // P
D_INNER = 256
HALVES = D_INNER // P
D_STATE = 16
DT_RANK = 8
DIRECTIONS = 4
BANK = 512

ENGINES = ("tensor", "vector", "scalar", "gpsimd", "sync")


class Body:

    def __init__(self, nc, semaphores):
        self.nc, self.semaphores = nc, semaphores
        self.named, self.counts, self.owner = {}, {}, {}
        self.queues = {e: [] for e in ENGINES}

    def do(self, engine, issue, after=(), signal=None):
        mark, step = None, 1
        if signal is not None:
            if signal not in self.named:
                self.named[signal] = self.semaphores[len(self.named)]
                self.counts[signal], self.owner[signal] = 0, engine
            assert self.owner[signal] == engine
            self.counts[signal] += 1
            mark = (signal, self.counts[signal])
        self.queues[engine].append((issue, [m for m in after if m], signal, step))
        return mark

    def dma(self, engine, issue, after=(), signal=None):
        mark = self.do(engine, issue, after, signal)
        queue = self.queues[engine]
        queue[-1] = queue[-1][:3] + (16,)
        return (mark[0], mark[1] * 16)

    def run(self):
        nc = self.nc
        with nc.Block() as block:
            for name in ENGINES:
                def program(engine, queue=self.queues[name]):
                    for issue, after, signal, step in queue:
                        for what, count in after:
                            engine.wait_ge(self.named[what], count)
                        last = issue(engine)
                        if signal is not None:
                            last.then_inc(self.named[signal], step)
                start = {"tensor": block.tensor, "vector": block.vector, "scalar": block.scalar,
                         "gpsimd": block.gpsimd, "sync": block.sync}
                start[name](program)
        first = self.semaphores[0].num
        nc.vector.sem_clear(range(first, first + len(self.semaphores)))
        nc.all_engine_barrier()


class Memory:

    def __init__(self, nc, stack):
        self.nc, self.stack = nc, stack

    def sb(self, name, shape, dtype=F32):
        return self.stack.enter_context(self.nc.sbuf_tensor(name, shape, dtype))

    def ps(self, name, shape, dtype=F32):
        return self.stack.enter_context(self.nc.psum_tensor(name, shape, dtype))


def group_stats(nc, sems, name, x, eps, const, scale_row, shift_row, columns=None):
    CHUNK = BANK // PER_GROUP
    per_part = TOKENS // P
    chunks = per_part // CHUNK
    with ExitStack() as stack:
        m = Memory(nc, stack)
        xt = m.sb(f"{name}_x", [P, 2, CHUNK, C])
        st = m.sb(f"{name}_st", [P, GROUPS, chunks, 6])
        mv = m.sb(f"{name}_mv", [P, GROUPS, 2])
        avg = m.sb(f"{name}_avg", [P, GROUPS, 2])
        dev = m.sb(f"{name}_dev", [P, GROUPS])
        var = m.sb(f"{name}_var", [P, GROUPS])
        std = m.sb(f"{name}_std", [P, GROUPS])
        pick = m.sb(f"{name}_pick", [P, 2, GROUPS])
        total = m.ps(f"{name}_total", [P, 2, BANK])
        src = x.rearrange("(p j k) c -> j p k c", p=P, k=CHUNK)
        b = Body(nc, sems)
        stats = [None] * chunks
        for j in range(chunks):
            loaded = b.dma("sync", lambda e, j=j: e.dma_start(xt[:, j % 2], src[j]),
                           [stats[j - 2] if j >= 2 else None], f"load{j % 2}")
            for g in range(GROUPS):
                stats[j] = b.do("vector", lambda e, j=j, g=g: e.bn_stats(
                    st[:, g, j, :], xt[:, j % 2, :, g * PER_GROUP:(g + 1) * PER_GROUP]), [loaded], "stats")
        for g in range(GROUPS):
            aggr = b.do("vector", lambda e, g=g: e.bn_aggr(mv[:, g, :], st[:, g]), [stats[-1]], "aggr")
        t0 = b.do("tensor", lambda e: e.matmul(total[:, 0, 0:2 * GROUPS], const["mean"][:, :],
                  mv[:, :, :].rearrange("p g s -> p (g s)"), start=True, stop=True), [aggr], "t")
        a0 = b.do("vector", lambda e: e.tensor_copy(avg[:, :, :].rearrange("p g s -> p (g s)"),
                  total[:, 0, 0:2 * GROUPS]), [t0], "v")
        d0 = b.do("vector", lambda e: e.tensor_tensor(dev[:, :], mv[:, :, 0], avg[:, :, 0], ALU.subtract), [a0], "v")
        d1 = b.do("vector", lambda e: e.tensor_tensor(dev[:, :], dev[:, :], dev[:, :], ALU.mult), [d0], "v")
        t1 = b.do("tensor", lambda e: e.matmul(total[:, 1, 0:GROUPS], const["mean"][:, :], dev[:, :],
                  start=True, stop=True), [d1], "t")
        v0 = b.do("vector", lambda e: e.tensor_tensor(var[:, :], avg[:, :, 1], total[:, 1, 0:GROUPS], ALU.add), [t1], "v")
        v1 = b.do("vector", lambda e: e.tensor_scalar(var[:, :], var[:, :], eps, None, ALU.add), [v0], "v")
        s0 = b.do("scalar", lambda e: e.activation(std[:, :], var[:, :], ACT.Sqrt), [v1], "s")
        r0 = b.do("vector", lambda e: e.reciprocal(scale_row[:, :], std[:, :]), [s0], "v")
        r1 = b.do("vector", lambda e: e.scalar_tensor_tensor(out=shift_row[:, :], in0=avg[:, :, 0], scalar=-1.0,
                  in1=scale_row[:, :], op0=ALU.mult, op1=ALU.mult), [r0], "v")
        if columns:
            for i, (row, column) in enumerate(zip((scale_row, shift_row), columns)):
                p0 = b.do("vector", lambda e, i=i, row=row: e.tensor_tensor(
                    pick[:, i, :], row[:, :], const["group_of"][:, :], ALU.mult), [r1], "v")
                b.do("vector", lambda e, i=i, column=column: e.tensor_reduce(
                    column[:, 0:1], pick[:, i, :], AX_X, ALU.add), [p0], "v")
        b.run()


def norm_phase(nc, sems, x, zn_t, bias_d, wts, const, scale_row, shift_row):
    ROWS = 8
    CT = ROWS * SIDE
    BLOCKS = CT // P
    PER_BODY = 4
    with ExitStack() as stack:
        m = Memory(nc, stack)
        xt = m.sb("n_x", [P, 2, BLOCKS, C])
        gt = m.sb("n_g", [P, 2, BLOCKS, C])
        st = m.sb("n_st", [P, 2, BLOCKS, 6])
        mv = m.sb("n_mv", [P, 2, BLOCKS, 2])
        std = m.sb("n_std", [P, 2, BLOCKS])
        rstd = m.sb("n_rstd", [P, 2, BLOCKS])
        nmr = m.sb("n_nmr", [P, 2, BLOCKS])
        zt = m.sb("n_zt", [P, 2, CT])
        bt = m.sb("n_bt", [HEADS, 2, CT])
        tp = m.ps("n_tp", [P, 4, BANK])
        bp = m.ps("n_bp", [P, 2, BANK])
        src = x.rearrange("(i q b p) c -> i q p b c", q=PER_BODY, b=BLOCKS, p=P)
        dst = zn_t.rearrange("(i q) c t -> i q c t", q=PER_BODY)
        bdst = bias_d.rearrange("h (i q t) -> i q h t", q=PER_BODY, t=CT)
        four = lambda v: v.rearrange("p b (g c) -> p b g c", c=PER_GROUP)
        row = lambda v: v[:, :].unsqueeze(1).unsqueeze(3).to_broadcast([P, BLOCKS, GROUPS, PER_GROUP])
        with nc.Fori(0, TOKENS // (CT * PER_BODY)) as it:
            b = Body(nc, sems)
            turned = [None] * PER_BODY; evac = [None] * (PER_BODY * 4); stored = [None] * PER_BODY
            bevac = [None] * (PER_BODY * 4); bstored = [None] * PER_BODY
            for q in range(PER_BODY):
                s = q % 2
                back = lambda marks, n=2: marks[q - n] if q >= n else None
                for half in (slice(0, BLOCKS // 2), slice(BLOCKS // 2, BLOCKS)):
                    ld = b.dma("sync", lambda e, q=q, s=s, half=half: e.dma_start(xt[:, s, half], src[it, q, :, half]),
                               [back(turned)], f"load{s}")
                g0 = b.do("vector", lambda e, s=s: e.tensor_tensor(four(gt[:, s]), four(xt[:, s]), row(scale_row),
                          ALU.mult), [ld, back(turned)], "v")
                g1 = b.do("gpsimd", lambda e, s=s: e.tensor_tensor(four(gt[:, s]), four(gt[:, s]), row(shift_row),
                          ALU.add), [g0], "p")
                for j in range(BLOCKS):
                    s0 = b.do("vector", lambda e, s=s, j=j: e.bn_stats(st[:, s, j, :], gt[:, s, j, :]), [g1], "v")
                for j in range(BLOCKS):
                    s1 = b.do("vector", lambda e, s=s, j=j: e.bn_aggr(mv[:, s, j, :], st[:, s, j, :]), [s0], "v")
                v0 = b.do("vector", lambda e, s=s: e.tensor_scalar(std[:, s], mv[:, s, :, 1], 1e-5, None, ALU.add), [s1], "v")
                q0 = b.do("scalar", lambda e, s=s: e.activation(std[:, s], std[:, s], ACT.Sqrt), [v0], "s")
                v1 = b.do("vector", lambda e, s=s: e.reciprocal(rstd[:, s], std[:, s]), [q0], "v")
                v2 = b.do("vector", lambda e, s=s: e.scalar_tensor_tensor(
                    out=nmr[:, s], in0=mv[:, s, :, 0], scalar=-1.0, in1=rstd[:, s], op0=ALU.mult, op1=ALU.mult), [v1], "v")
                for j in range(BLOCKS):
                    z0 = b.do("vector", lambda e, s=s, j=j: e.tensor_scalar(
                        gt[:, s, j, :], gt[:, s, j, :], rstd[:, s, j:j + 1], nmr[:, s, j:j + 1], ALU.mult, ALU.add),
                        [v2], "v")
                for f in range(4):
                    k = q * 4 + f
                    def turn(e, s=s, f=f):
                        for j in range(4):
                            last = e.transpose(tp[:, f, j * P:(j + 1) * P], gt[:, s, 4 * f + j, :], const["eye"][:, :])
                        return last
                    turned[q] = b.do("tensor", turn, [z0, evac[k - 4] if q else None], "turn")
                    evac[k] = b.do("scalar", lambda e, s=s, f=f: e.activation(
                        zt[:, s, f * BANK:(f + 1) * BANK], tp[:, f, :], ACT.Identity, bias=wts["ln_bias"][:, 0:1],
                        scale=wts["ln_scale"][:, 0:1]), [turned[q], back(stored)], "evac")
                    pb = b.do("tensor", lambda e, s=s, f=f: e.matmul(
                        bp[0:HEADS, f % 2, :], wts["Wb"][:, :], zt[:, s, f * BANK:(f + 1) * BANK], start=True, stop=True),
                        [evac[k], bevac[k - 2] if k >= 2 else None], "pb")
                    bevac[k] = b.do("scalar", lambda e, s=s, f=f: e.copy(
                        bt[:, s, f * BANK:(f + 1) * BANK], bp[0:HEADS, f % 2, :]), [pb, back(bstored)], "bevac")
                stored[q] = b.dma("sync", lambda e, q=q, s=s: e.dma_start(dst[it, q], zt[:, s]), [evac[4 * q + 3]], f"st{s}")
                bstored[q] = b.dma("sync", lambda e, q=q, s=s: e.dma_start(bdst[it, q], bt[:, s]), [bevac[4 * q + 3]], f"bst{s}")
            b.do("sync", lambda e: e.nop(), [stored[-1], stored[-2], bstored[-1], bstored[-2]])
            b.run()


def attention_phase(nc, sems, x, zn_t, bias_d, x1, wts, const):
    ROWS = 8
    SCALE = float(HEAD_DIM) ** -0.5
    V1 = HEAD_DIM + 1
    with ExitStack() as stack:
        m = Memory(nc, stack)
        zt = m.sb("a_zt", [P, ROWS, SIDE])
        xt = m.sb("a_xt", [P, ROWS, JB, C])
        bias = m.sb("a_bias", [P, JB, HEADS, SIDE])
        qk = m.sb("a_qk", [P, 2, 2, SIDE])
        v1 = m.sb("a_v1", [P, 3, JB, HEADS, V1])
        gate = m.sb("a_gate", [P, 3, JB, C])
        sc = m.sb("a_sc", [P, 2, HEADS, JB, SIDE])
        top = m.sb("a_top", [P, 2, HEADS, JB])
        ntop = m.sb("a_ntop", [P, 2, HEADS, JB])
        pt = m.sb("a_pt", [P, 2, HEADS, JB, SIDE])
        den = m.sb("a_den", [P, 2, JB, HEADS])
        rden = m.sb("a_rden", [P, 2, JB, HEADS])
        go = m.sb("a_go", [P, 2, JB, C])
        gt = m.sb("a_gt", [P, 2, SIDE])
        yt = m.sb("a_yt", [P, ROWS, JB, C])
        scores = m.ps("a_scores", [P, HEADS, BANK])
        proj = m.ps("a_proj", [P, BANK])
        turn = m.ps("a_turn", [P, 2, BANK])
        mix = m.ps("a_mix", [P, BANK])
        xsrc = x.rearrange("(i r b p) c -> i p r b c", r=ROWS, b=JB, p=P)
        xdst = x1.rearrange("(i r b p) c -> i p r b c", r=ROWS, b=JB, p=P)
        zsrc = zn_t.rearrange("i c (r t) -> i c r t", t=SIDE)

        b = Body(nc, sems)
        bsrc = bias_d.rearrange("h (b j k) -> b j h k", b=JB, j=P)
        for jb in range(JB):
            ld = b.dma("sync", lambda e, jb=jb: e.dma_start(bias[:, jb], bsrc[jb]), [], "bias")
        b.do("sync", lambda e: e.nop(), [ld])
        b.do("vector", lambda e: e.memset(v1[:, :, :, :, :].rearrange("p s b h v -> p (s b h v)"), 1.0))
        b.run()

        with nc.Fori(0, SIDE // ROWS) as it:
            b = Body(nc, sems)
            zl = b.dma("sync", lambda e: e.dma_start(zt[:, :, :], zsrc[it]), [], "loadz")
            for half in (slice(0, ROWS // 2), slice(ROWS // 2, ROWS)):
                xl = b.dma("sync", lambda e, half=half: e.dma_start(xt[:, half], xsrc[it, :, half]), [], "loadx")
            N = ROWS
            qk_ev, v_ev, g_ev, bias_ad, exps, t_last, t_ev, pv, gated, gt_ev, y_mm, y_ev, s_mm, s_ev = ({} for _ in range(14))

            def project(r):
                def qk_mm(e):
                    e.matmul(proj[:, 0:SIDE], wts["Wq"][:, :], zt[:, r, :], start=True, stop=True)
                    return e.matmul(proj[:, SIDE:], wts["Wk"][:, :], zt[:, r, :], start=True, stop=True)
                t = b.do("tensor", qk_mm, [zl, g_ev.get(r - 1)], "proj")
                qk_ev[r] = b.do("scalar", lambda e: e.copy(
                    qk[:, r % 2].rearrange("p a t -> p (a t)"), proj[:, :]), [t, s_mm.get(r - 2)], "qkev")
                def vg_mm(e):
                    for jb in range(JB):
                        last = e.matmul(proj[:, jb * SIDE:(jb + 1) * SIDE], zt[:, r, jb * P:(jb + 1) * P],
                                        wts["Wvg"][:, :], start=True, stop=True)
                    return last
                t = b.do("tensor", vg_mm, [qk_ev[r]], "proj")
                pv_view = proj[:, :].rearrange("p (b a n) -> p b a n", b=JB, a=2)
                tan = b.do("scalar", lambda e: e.activation(gate[:, r % 3], pv_view[:, :, 1, :], ACT.Tanh, scale=0.5),
                           [t, gated.get(r - 3)], "gate")
                v_ev[r] = b.do("vector", lambda e: e.tensor_copy(
                    v1[:, r % 3, :, :, 0:HEAD_DIM], pv_view[:, :, 0, :].rearrange("p b (h d) -> p b h d", h=HEADS)),
                    [tan, pv.get(r - 3)], "vev")
                g_ev[r] = v_ev[r]

            def score(r):
                for h in range(HEADS):
                    def mm(e, h=h):
                        rows = slice(h * HEAD_DIM, (h + 1) * HEAD_DIM)
                        for jb in range(JB):
                            last = e.matmul(scores[:, h, jb * SIDE:(jb + 1) * SIDE],
                                            qk[rows, r % 2, 0, jb * P:(jb + 1) * P], qk[rows, r % 2, 1, :],
                                            start=True, stop=True)
                        return last
                    s_mm[r] = t = b.do("tensor", mm, [qk_ev[r], s_ev.get((r - 1, h))], "score")
                    s_ev[r, h] = b.do("vector", lambda e, h=h: e.scalar_tensor_tensor(
                        out=sc[:, r % 2, h, :, :], in0=scores[:, h, :].rearrange("p (b k) -> p b k", b=JB), scalar=SCALE,
                        in1=bias[:, :, h, :], op0=ALU.mult, op1=ALU.add), [t, t_last.get(r - 2)], "sev")
                mx = b.do("vector", lambda e: e.tensor_reduce(
                    top[:, r % 2], sc[:, r % 2], AX_X, ALU.max), [s_ev[r, HEADS - 1]], "v")
                ng = b.do("vector", lambda e: e.tensor_scalar(ntop[:, r % 2], top[:, r % 2], -1.0, None, ALU.mult),
                          [mx, exps.get((r - 2, HEADS - 1))], "v")
                for h in range(HEADS):
                    def ex(e, h=h):
                        for jb in range(JB):
                            last = e.activation(sc[:, r % 2, h, jb, :], sc[:, r % 2, h, jb, :], ACT.Exp,
                                                bias=ntop[:, r % 2, h, jb:jb + 1])
                        return last
                    exps[r, h] = b.do("scalar", ex, [ng], "exp")

            def weigh(r):
                for h in range(HEADS):
                    def tr(e, h=h):
                        for kb in range(JB):
                            for jb in range(JB):
                                last = e.transpose(turn[:, h % 2, kb * SIDE + jb * P:kb * SIDE + (jb + 1) * P],
                                                   sc[:, r % 2, h, jb, kb * P:(kb + 1) * P], const["eye"][:, :])
                        return last
                    t_last[r] = t = b.do("tensor", tr, [exps[r, h], t_ev.get((r, h - 2)), t_ev.get((r - 1, h + 2))], "turn")
                    who = "scalar" if h % 2 else "vector"
                    def ev(e, h=h):
                        dst, src = pt[:, r % 2, h].rearrange("p b k -> p (b k)"), turn[:, h % 2, :]
                        return e.copy(dst, src) if h % 2 else e.tensor_copy(dst, src)
                    t_ev[r, h] = b.do(who, ev, [t, pv.get(r - 2)], f"tev{h % 2}")
                for h in range(HEADS):
                    def mm(e, h=h):
                        for jb in range(JB):
                            for kb in range(JB):
                                at = (jb * HEADS + h) * V1
                                last = e.matmul(mix[:, at:at + V1], pt[:, r % 2, h, kb, jb * P:(jb + 1) * P],
                                                v1[:, r % 3, kb, h, :], start=(kb == 0), stop=(kb == JB - 1))
                        return last
                    pv[r] = b.do("tensor", mm, [t_ev[r, h], v_ev[r], y_ev.get(r - 1)], "pv")
                o = mix[:, 0:JB * HEADS * V1].rearrange("p (b h v) -> p b h v", b=JB, h=HEADS)
                d0 = b.do("vector", lambda e: e.tensor_scalar(den[:, r % 2], o[:, :, :, HEAD_DIM], 2.0, None, ALU.mult), [pv[r]], "v")
                d1 = b.do("vector", lambda e: e.reciprocal(rden[:, r % 2], den[:, r % 2]), [d0], "v")
                g0 = b.do("vector", lambda e: e.scalar_tensor_tensor(
                    out=go[:, r % 2].rearrange("p b (h d) -> p b h d", h=HEADS),
                    in0=gate[:, r % 3].rearrange("p b (h d) -> p b h d", h=HEADS), scalar=1.0,
                    in1=o[:, :, :, 0:HEAD_DIM], op0=ALU.add, op1=ALU.mult), [pv[r], gt_ev.get(r - 2)], "v")
                gated[r] = b.do("vector", lambda e: e.tensor_tensor(
                    go[:, r % 2].rearrange("p b (h d) -> p b h d", h=HEADS),
                    go[:, r % 2].rearrange("p b (h d) -> p b h d", h=HEADS),
                    rden[:, r % 2].unsqueeze(3).broadcast_to([P, JB, HEADS, HEAD_DIM]), ALU.mult), [g0, d1], "v")

            def gate_turn(r):
                def tr(e):
                    for jb in range(JB):
                        last = e.transpose(mix[:, jb * P:(jb + 1) * P], go[:, r % 2, jb, :], const["eye"][:, :])
                    return last
                t = b.do("tensor", tr, [gated[r]], "mix")
                gt_ev[r] = b.do("scalar", lambda e: e.copy(gt[:, r % 2, :], mix[:, 0:SIDE]), [t, y_mm.get(r - 2)], "gtev")

            def output(r):
                def mm(e):
                    for jb in range(JB):
                        last = e.matmul(mix[:, SIDE + jb * P:SIDE + (jb + 1) * P], gt[:, r % 2, jb * P:(jb + 1) * P],
                                        wts["Wo"][:, :], start=True, stop=True)
                    return last
                y_mm[r] = b.do("tensor", mm, [gt_ev[r]], "ymm")
                y_ev[r] = b.do("vector", lambda e: e.tensor_tensor(
                    yt[:, r].rearrange("p b c -> p (b c)"), mix[:, SIDE:2 * SIDE],
                    xt[:, r].rearrange("p b c -> p (b c)"), ALU.add), [y_mm[r], xl], "yev")

            project(0)
            score(0)
            project(1)
            for r in range(N):
                if r >= 1:
                    gate_turn(r - 1)
                if r + 1 < N:
                    score(r + 1)
                if r >= 1:
                    output(r - 1)
                if r + 2 < N:
                    project(r + 2)
                weigh(r)
            gate_turn(N - 1)
            output(N - 1)
            st = b.dma("sync", lambda e: e.dma_start(xdst[it], yt[:, :, :, :]), [y_ev[N - 1]], "store")
            b.do("sync", lambda e: e.nop(), [st])
            b.run()


def conv_phase(nc, sems, x1, xc_tok, wts, const, scale_col, shift_col):
    ROWS = 8
    PAIR = 2
    WIDE = SIDE + 2
    with ExitStack() as stack:
        m = Memory(nc, stack)
        xt = m.sb("c_xt", [P, ROWS, JB, C])
        gn = m.sb("c_gn", [P, 2, BANK])
        xi = m.sb("c_xi", [P, HALVES, ROWS + 2, WIDE])
        acc = m.sb("c_acc", [P, ROWS, SIDE])
        xc = m.sb("c_xc", [P, HALVES, ROWS, SIDE])
        ot = m.sb("c_ot", [P, ROWS, JB, D_INNER])
        tap = m.sb("c_tap", [P, 9, P])
        tp = m.ps("c_tp", [P, BANK])
        xp = m.ps("c_xp", [P, 2, BANK])
        cp = m.ps("c_cp", [P, 2, BANK])
        op = m.ps("c_op", [P, 2, BANK])
        src = x1.rearrange("(h b p) c -> p h b c", b=JB, p=P)
        dst = xc_tok.rearrange("(h b p) d -> p h b d", b=JB, p=P)

        def rows_of(ap, first, count):
            return ap[:, bass.ds(first, count)] if not isinstance(first, int) else ap[:, first:first + count]

        def xi_rows(b, first, slot, count, after=None):
            for at in range(0, count, PAIR):
                ld = b.dma("sync", lambda e, at=at: e.dma_start(xt[:, at:at + PAIR], rows_of(src, first + at, PAIR)), [], "load")
            tev, xev, gmm = {}, {}, {}
            for k in range(count // PAIR):
                def tr(e, k=k):
                    for j in range(4):
                        last = e.transpose(tp[:, j * P:(j + 1) * P], xt[:, PAIR * k + j // 2, j % 2, :], const["eye"][:, :])
                    return last
                t = b.do("tensor", tr, [ld, tev.get(k - 1)], "turn")
                tev[k] = b.do("scalar", lambda e, k=k: e.activation(gn[:, k % 2, :], tp[:, :], ACT.Identity,
                              bias=shift_col[:, 0:1], scale=scale_col[:, 0:1]), [t, gmm.get(k - 2)], "gn")
                for half in range(HALVES):
                    t = gmm[k] = b.do("tensor", lambda e, k=k, half=half: e.matmul(
                        xp[:, half, :], wts["w_in"][:, half * P:(half + 1) * P], gn[:, k % 2, :], start=True, stop=True),
                        [tev[k], xev.get((k - 1, half))], "xmm")
                    def ev(e, k=k, half=half):
                        d = xi[:, half, slot + PAIR * k:slot + PAIR * (k + 1), 1:1 + SIDE]
                        s = xp[:, half, :].rearrange("p (r w) -> p r w", r=PAIR)
                        return e.tensor_copy(d, s) if half else e.copy(d, s)
                    xev[k, half] = b.do("vector" if half else "scalar", ev, [t, after], f"xev{half}")
            return [xev[count // PAIR - 1, 0], xev[count // PAIR - 1, 1]]

        def one_turn(h0, last):
            b = Body(nc, sems)
            ready = []
            if not last:
                ready = xi_rows(b, h0 + 1, 2, ROWS)
            else:
                ready = xi_rows(b, h0 + 1, 2, ROWS - 2)
                ld = b.dma("sync", lambda e: e.dma_start(xt[:, 6:7], src[:, h0 + 7:h0 + 8]), [], "load1")
                def tr(e):
                    for j in range(2):
                        t = e.transpose(tp[:, j * P:(j + 1) * P], xt[:, 6, j, :], const["eye"][:, :])
                    return t
                t = b.do("tensor", tr, [ld, ready[0]], "turn")
                g = b.do("scalar", lambda e: e.activation(gn[:, 1, 0:SIDE], tp[:, 0:SIDE], ACT.Identity,
                         bias=shift_col[:, 0:1], scale=scale_col[:, 0:1]), [t, ready[1]], "gn")
                for half in range(HALVES):
                    t = b.do("tensor", lambda e, half=half: e.matmul(
                        xp[:, half, 0:SIDE], wts["w_in"][:, half * P:(half + 1) * P], gn[:, 1, 0:SIDE],
                        start=True, stop=True), [g, ready[half]], "xmm")
                    def ev(e, half=half):
                        e.memset(xi[:, half, ROWS + 1, :], 0.0)
                        return e.tensor_copy(xi[:, half, ROWS, 1:1 + SIDE], xp[:, half, 0:SIDE])
                    ready.append(b.do("vector", ev, [t], "edge"))
            for t9 in range(9):
                dy, dx = t9 // 3, t9 % 3
                window = xi[:, 1, dy:dy + ROWS, dx:dx + SIDE]
                w = wts["conv_w"][:, 1, t9:t9 + 1]
                if t9 == 0:
                    a = b.do("vector", lambda e, window=window, w=w: e.tensor_scalar(
                        acc[:, :, :], window, w, None, ALU.mult), ready, "acc")
                else:
                    a = b.do("vector", lambda e, window=window, w=w: e.scalar_tensor_tensor(
                        out=acc[:, :, :], in0=window, scalar=w, in1=acc[:, :, :], op0=ALU.mult, op1=ALU.add), [a], "acc")
            cev, oev, csil = {}, {}, {}
            for k in range(ROWS // PAIR):
                def mm(e, k=k):
                    for t9 in range(9):
                        dy, dx = t9 // 3, t9 % 3
                        last = e.matmul(cp[:, k % 2, :].rearrange("p (r w) -> p r w", r=PAIR), tap[:, t9, :],
                                        xi[:, 0, PAIR * k + dy:PAIR * k + dy + PAIR, dx:dx + SIDE],
                                        start=(t9 == 0), stop=(t9 == 8))
                    return last
                t = b.do("tensor", mm, ready + [cev.get(k - 2)], "conv")
                cev[k] = b.do("scalar", lambda e, k=k: e.activation(
                    xc[:, 0, PAIR * k:PAIR * (k + 1), :], cp[:, k % 2, :].rearrange("p (r w) -> p r w", r=PAIR),
                    ACT.Silu, bias=wts["conv_b"][:, 0:1]), [t], "silu")
            c1 = b.do("scalar", lambda e: e.activation(xc[:, 1], acc[:, :, :], ACT.Silu, bias=wts["conv_b"][:, 1:2]), [a], "silu")
            for r in range(ROWS):
                def tr(e, r=r):
                    for jb in range(JB):
                        for half in range(HALVES):
                            last = e.transpose(op[:, r % 2, jb * D_INNER + half * P:jb * D_INNER + (half + 1) * P],
                                               xc[:, half, r, jb * P:(jb + 1) * P], const["eye"][:, :])
                    return last
                t = b.do("tensor", tr, [c1, oev.get(r - 2)], "turn")
                def ev(e, r=r):
                    d, s = ot[:, r].rearrange("p b d -> p (b d)"), op[:, r % 2, :]
                    return e.tensor_copy(d, s) if r % 2 else e.copy(d, s)
                oev[r] = b.do("vector" if r % 2 else "scalar", ev, [t], f"oev{r % 2}")
            st = b.dma("sync", lambda e: e.dma_start(rows_of(dst, h0, ROWS), ot[:, :, :, :]), [oev[ROWS - 1], oev[ROWS - 2]], "store")
            b.do("sync", lambda e: e.nop(), [st])
            b.do("gpsimd", lambda e: e.tensor_copy(xi[:, :, 0:2, :], xi[:, :, ROWS:ROWS + 2, :]), [t, a], None)
            b.run()

        b = Body(nc, sems)
        z = b.do("vector", lambda e: e.memset(xi[:, :, :, :].rearrange("p a r w -> p (a r w)"), 0.0), [], "zero")
        for t9 in range(9):
            b.do("vector", lambda e, t9=t9: e.tensor_scalar(tap[:, t9, :], const["eye"][:, :],
                 wts["conv_w"][:, 0, t9:t9 + 1], None, ALU.mult))
        xi_rows(b, 0, 1, PAIR, z)
        b.run()
        turns = SIDE // ROWS
        with nc.Fori(0, turns - 1) as it:
            one_turn(it * ROWS, False)
        one_turn((turns - 1) * ROWS, True)


def scan_phase(nc, sems, k, xc_tok, y_k, wts, const, turns_limit=None):
    T = BANK
    SUBS = T // P
    TILES = TOKENS // T
    PER_BODY = 8
    NDA, NP_ = 4, 4
    backwards = k >= 2
    by_column = k % 2 == 1
    GUARD = 20.0
    flow = slice(None, None, -1) if backwards else slice(None)
    last_token = 0 if backwards else T - 1
    with ExitStack() as stack:
        m = Memory(nc, stack)
        xt = m.sb(f"s{k}_xt", [P, 2, SUBS, D_INNER])
        xc = m.sb(f"s{k}_xc", [P, 2, HALVES, T])
        rest = m.sb(f"s{k}_rest", [96, 2, T])
        mid = m.sb(f"s{k}_mid", [96, 2, T], BF16)
        parts = m.sb(f"s{k}_parts", [96, 2, 2, T], BF16)
        low = m.sb(f"s{k}_low", [DT_RANK, T])
        e1 = m.sb(f"s{k}_e1", [P, HALVES, T])
        delta = m.sb(f"s{k}_delta", [P, 2, HALVES, T])
        dx = m.sb(f"s{k}_dx", [P, 2, HALVES, T])
        da = m.sb(f"s{k}_da", [P, NDA, T])
        h = m.sb(f"s{k}_h", [P, HALVES, D_STATE, T])
        cb = m.sb(f"s{k}_cb", [P, 3, T])
        prod = m.sb(f"s{k}_prod", [P, NP_, T])
        yt = m.sb(f"s{k}_yt", [P, 2, SUBS, D_INNER])
        pb = m.ps(f"s{k}_pb", [P, 2, BANK])
        pd = m.ps(f"s{k}_pd", [P, BANK])
        pc = m.ps(f"s{k}_pc", [P, BANK])
        py = m.ps(f"s{k}_py", [P, 2, BANK])
        pr = m.ps(f"s{k}_pr", [P, 2, BANK])

        if by_column:
            view = lambda t: t.rearrange("(b p w) d -> w p b d", b=JB, p=P)
        else:
            view = lambda t: t.rearrange("(i b p) d -> i p b d", b=JB, p=P)
        src, dst = view(xc_tok), view(y_k)

        b = Body(nc, sems)
        b.do("vector", lambda e: e.memset(h[:, :, :, last_token], 0.0))
        b.run()

        turns = turns_limit or TILES // PER_BODY
        with nc.Fori(0, turns) as it:
            b = Body(nc, sems)
            loads, turned, xc_ev, xc_used, split, spread_b, spread_c, dts, dx_ready, delta_ready = ({} for _ in range(10))
            exps, b_mm, db, scans, c_mm, c_ev, prods, sums, y_ev, stores = ({} for _ in range(10))
            pr_free = [None, None]

            def line(g, i):
                tile = (TILES - 1 - g) - it * PER_BODY if backwards else it * PER_BODY + g
                return tile * (T // SIDE) + i

            def load(g):
                for i in range(T // SIDE):
                    loads[g] = b.dma("sync", lambda e, i=i: e.dma_start(
                        xt[:, g % 2, i * JB:(i + 1) * JB, :], src[line(g, i)]), [turned.get(g - 2)], f"load{g % 2}")

            def prepare(g):
                s = g % 2
                for half in range(HALVES):
                    def tr(e, half=half):
                        for j in range(SUBS):
                            last = e.transpose(pr[:, half, j * P:(j + 1) * P], xt[:, s, j, half * P:(half + 1) * P],
                                               const["eye"][:, :])
                        return last
                    t = turned[g] = b.do("tensor", tr, [loads[g], pr_free[half]], "prep")
                    xc_ev[g, half] = pr_free[half] = b.do("scalar", lambda e, half=half: e.copy(
                        xc[:, s, half, :], pr[:, half, :]), [t, dx_ready.get(g - 2), xc_used.get(g - 2)], "xcev")
                yield
                for which, name in enumerate(("proj_b", "proj_c")):
                    def mm(e, which=which, name=name):
                        rows = wts[name].shape[-1]
                        for half in range(HALVES):
                            last = e.matmul(pr[0:rows, which, :], wts[name][:, half, :], xc[:, s, half, :],
                                            start=(half == 0), stop=(half == HALVES - 1))
                        return last
                    t = b.do("tensor", mm, [xc_ev[g, 0], xc_ev[g, 1], pr_free[which]], "prep")
                both = lambda v: v.rearrange("p a t -> p (a t)")
                up = b.do("scalar", lambda e: e.copy(both(parts[:, s]), both(pr[0:96])), [t, spread_c.get(g - 2)], "hi")
                lw = b.do("scalar", lambda e: e.copy(low[:, :], pr[96:96 + DT_RANK, 0, :]), [t, dts.get(g - 1)], "hi")
                re = b.do("vector", lambda e: e.tensor_tensor(both(rest[:, :, :]), both(pr[0:96]), both(parts[:, s]), ALU.subtract),
                          [lw, split.get(g - 1)], "rest")
                pr_free[0] = pr_free[1] = re
                yield
                md = b.do("scalar", lambda e: e.copy(both(mid[:, :, :]), both(rest[:, :, :])), [re, split.get(g - 1)], "hi")
                pm = b.do("vector", lambda e: e.tensor_copy(parts[32:64, s], mid[32:64]), [md], "rest")
                split[g] = b.do("vector", lambda e: e.tensor_tensor(parts[64:96, s], rest[64:96], mid[64:96], ALU.subtract), [md], "rest")
                for half in range(HALVES):
                    t = dts[g] = b.do("tensor", lambda e, half=half: e.matmul(
                        pr[:, half, :], wts["dt_w"][:, half * P:(half + 1) * P], low[:, :], start=True, stop=True),
                        [lw, pr_free[half]], "prep")
                    rl = b.do("scalar", lambda e, half=half: e.activation(
                        e1[:, half, :], pr[:, half, :], ACT.Relu, bias=wts["guard_less_dt_b"][:, half:half + 1], scale=-1.0),
                        [t, delta_ready.get((g - 1, half))], "soft")
                yield
                ex = b.do("scalar", lambda e: e.activation(e1[:, :, :], e1[:, :, :], ACT.Exp, scale=-1.0, bias=wts["guard"][:, 0:1]), [rl], "soft")
                ln = b.do("scalar", lambda e: e.activation(e1[:, :, :], e1[:, :, :], ACT.Ln, bias=1.0), [ex], "soft")
                yield
                for half in range(HALVES):
                    delta_ready[g, half] = pr_free[half] = b.do("vector", lambda e, half=half: e.scalar_tensor_tensor(
                        out=delta[:, s, half, :], in0=pr[:, half, :], scalar=wts["dt_b"][:, half:half + 1],
                        in1=e1[:, half, :], op0=ALU.add, op1=ALU.max), [ln, exps.get((g - 2, D_STATE - 1, 1))], "delta")
                dx_ready[g] = b.do("vector", lambda e: e.tensor_tensor(
                    dx[:, s], delta[:, s], xc[:, s], ALU.mult), [delta_ready[g, 1]], "delta")
                yield

            def spread(g, n):
                s = g % 2
                b_mm[g, n] = b.do("tensor", lambda e: e.matmul(pb[:, n % 2, :], const["spread"][:, n, :],
                    parts[:, s, 0, :], start=True, stop=True),
                    [split[g], scans.get((g, n - 2, 1)) if n >= 2 else scans.get((g - 1, D_STATE + n - 2, 1))], "bmm")
                c_mm[g, n] = spread_c[g] = b.do("tensor", lambda e: e.matmul(pc[:, :], const["spread"][:, n, :],
                    parts[:, s, 1, :], start=True, stop=True),
                    [c_ev.get((g, n - 1)) or c_ev.get((g - 1, D_STATE - 1))], "cmm")
                at = (g * D_STATE + n) % 3
                before = (g, n - 3, 1) if n >= 3 else (g - 1, D_STATE + n - 3, 1)
                c_ev[g, n] = b.do("scalar", lambda e: e.copy(cb[:, at, :], pc[:, :]), [c_mm[g, n], prods.get(before)], "cev")
                for half in range(HALVES):
                    slot = (2 * n + half) % NDA
                    before = (g, n - NDA // 2, half) if n >= NDA // 2 else (g - 1, D_STATE + n - NDA // 2, half)
                    exps[g, n, half] = b.do("scalar", lambda e, half=half, slot=slot: e.activation(
                        da[:, slot, :], delta[:, s, half, :], ACT.Exp, scale=wts["a_neg"][:, half, n:n + 1]),
                        [delta_ready[g, half], scans.get(before)], "exp")

            def state(g, n):
                s = g % 2
                dst_of = [pd[:, :], pb[:, n % 2, :]]
                for half in range(HALVES):
                    db[half] = b.do("vector", lambda e, half=half: e.tensor_tensor(
                        dst_of[half], pb[:, n % 2, :], dx[:, s, half, :], ALU.mult),
                        [b_mm[g, n], dx_ready[g], scans.get((g, n - 1, 0) if n else (g - 1, D_STATE - 1, 0))], "v")
                for half in range(HALVES):
                    slot = (2 * n + half) % NDA
                    scans[g, n, half] = b.do("vector", lambda e, half=half, slot=slot: e.tensor_tensor_scan(
                        h[:, half, n, flow], da[:, slot, flow], dst_of[half][:, flow], h[:, half, n, last_token:last_token + 1],
                        ALU.mult, ALU.add), [db[half], exps[g, n, half], prods.get((g - 1, n, half))], "v")
                at = (g * D_STATE + n) % 3
                for half in range(HALVES):
                    slot = (2 * n + half) % NP_
                    before = (g, n - NP_ // 2, half) if n >= NP_ // 2 else (g - 1, D_STATE + n - NP_ // 2, half)
                    prods[g, n, half] = b.do("gpsimd", lambda e, half=half, slot=slot: e.tensor_tensor(
                        prod[:, slot, :], h[:, half, n, :], cb[:, at, :], ALU.mult),
                        [scans[g, n, half], c_ev[g, n], sums.get(before)], "prod")

            def total(g, n):
                for half in range(HALVES):
                    slot = (2 * n + half) % NP_
                    def mm(e, half=half, slot=slot):
                        for j in range(SUBS):
                            out = py[:, j // 2, (j % 2) * D_INNER + half * P:(j % 2) * D_INNER + (half + 1) * P]
                            first = n == 0 and half == 0 and j % 2 == 0
                            last = e.matmul(out, prod[:, slot, j * P:(j + 1) * P], const["eye"][:, :], start=first,
                                            stop=(n == D_STATE - 1), is_transpose=True, skip_group_check=True)
                        return last
                    sums[g, n, half] = b.do("tensor", mm, [prods[g, n, half], y_ev.get(g - 1) if n == 0 else None], "sum")

            def skip(g):
                def mm(e):
                    for j in range(SUBS):
                        for half in range(HALVES):
                            out = py[:, j // 2, (j % 2) * D_INNER + half * P:(j % 2) * D_INNER + (half + 1) * P]
                            last = e.matmul(out, xc[:, g % 2, half, j * P:(j + 1) * P], wts["d_diag"][:, half, :],
                                            start=False, stop=False, skip_group_check=True)
                    return last
                xc_used[g] = b.do("tensor", mm, [], "sum")

            def store(g):
                for bank in range(2):
                    y_ev[g] = b.do("scalar", lambda e, bank=bank: e.copy(
                        yt[:, g % 2, 2 * bank:2 * bank + 2, :].rearrange("p j d -> p (j d)"), py[:, bank, :]),
                        [sums[g, D_STATE - 1, 1], stores.get(g - 2)], "yev")
                for i in range(T // SIDE):
                    stores[g] = b.dma("sync", lambda e, i=i: e.dma_start(
                        dst[line(g, i)], yt[:, g % 2, i * JB:(i + 1) * JB, :]), [y_ev[g]], f"store{g % 2}")

            load(0)
            load(1)
            for _ in prepare(0):
                pass
            AHEAD = (1, 4, 6, 9, 11)
            spread(0, 0)
            for g in range(PER_BODY):
                if g >= 1 and g + 1 < PER_BODY:
                    load(g + 1)
                steps = prepare(g + 1) if g + 1 < PER_BODY else iter(())
                for n in range(D_STATE):
                    if n + 1 < D_STATE:
                        spread(g, n + 1)
                    elif g + 1 < PER_BODY:
                        spread(g + 1, 0)
                    state(g, n)
                    if n >= 1:
                        total(g, n - 1)
                    if n == 2 and k == 0:
                        skip(g)
                    if n in AHEAD:
                        next(steps, None)
                total(g, D_STATE - 1)
                store(g)
            b.do("sync", lambda e: e.nop(), [stores[PER_BODY - 1], stores[PER_BODY - 2]])
            b.run()


def output_phase(nc, sems, ys, x1, out, wts, const, scale_col, shift_col):
    K = 8
    PER_BODY = 4
    with ExitStack() as stack:
        m = Memory(nc, stack)
        yt = m.sb("o_y", [P, 2, DIRECTIONS, K, D_INNER])
        xt = m.sb("o_x", [P, 2, K, C])
        st = m.sb("o_st", [P, 2, K, 6])
        mv = m.sb("o_mv", [P, 2, K, 2])
        std = m.sb("o_std", [P, 2, K])
        rstd = m.sb("o_rstd", [P, 2, K])
        nmr = m.sb("o_nmr", [P, 2, K])
        gn = m.sb("o_gn", [P, 2, BANK])
        zs = m.sb("o_zs", [P, 2, HALVES, BANK])
        yn = m.sb("o_yn", [P, 2, HALVES, BANK])
        ot = m.sb("o_ot", [P, 2, K, C])
        tp = m.ps("o_tp", [P, BANK])
        zp = m.ps("o_zp", [P, 2, BANK])
        yp = m.ps("o_yp", [P, 2, BANK])
        op = m.ps("o_op", [P, 2, BANK])
        view = lambda t: t.rearrange("(i q p j) c -> i q p j c", q=PER_BODY, j=K, p=P)
        ysrc, xsrc, dst = [view(y) for y in ys], view(x1), view(out)
        flat = lambda v: v.rearrange("p j d -> p (j d)")
        with nc.Fori(0, TOKENS // (K * P * PER_BODY)) as it:
            b = Body(nc, sems)
            ynt, tev, zmm, zev, zmul, yev, omm, oev, stored = ({} for _ in range(9))
            for q in range(PER_BODY):
                s = q % 2
                for i in range(DIRECTIONS):
                    ly = b.dma("sync", lambda e, i=i, q=q, s=s: e.dma_start(yt[:, s, i], ysrc[i][it, q]), [ynt.get(q - 2)], f"ly{s}")
                lx = b.dma("sync", lambda e, q=q, s=s: e.dma_start(xt[:, s], xsrc[it, q]), [oev.get((q - 2, 1))], f"lx{s}")
                a1 = b.do("gpsimd", lambda e, s=s: e.tensor_tensor(flat(yt[:, s, 2]), flat(yt[:, s, 2]), flat(yt[:, s, 3]), ALU.add), [ly], "p")
                a0 = b.do("vector", lambda e, s=s: e.tensor_tensor(flat(yt[:, s, 0]), flat(yt[:, s, 0]), flat(yt[:, s, 1]), ALU.add), [ly], "v")
                a2 = b.do("vector", lambda e, s=s: e.tensor_tensor(flat(yt[:, s, 0]), flat(yt[:, s, 0]), flat(yt[:, s, 2]), ALU.add), [a0, a1], "v")
                for j in range(K):
                    s0 = b.do("vector", lambda e, s=s, j=j: e.bn_stats(st[:, s, j, :], yt[:, s, 0, j, :]), [a2], "v")
                for j in range(K):
                    s1 = b.do("vector", lambda e, s=s, j=j: e.bn_aggr(mv[:, s, j, :], st[:, s, j, :]), [s0], "v")
                v0 = b.do("vector", lambda e, s=s: e.tensor_scalar(std[:, s], mv[:, s, :, 1], 1e-5, None, ALU.add), [s1], "v")
                q0 = b.do("scalar", lambda e, s=s: e.activation(std[:, s], std[:, s], ACT.Sqrt), [v0], "sqrt")
                v1 = b.do("vector", lambda e, s=s: e.reciprocal(rstd[:, s], std[:, s]), [q0], "v")
                v2 = b.do("vector", lambda e, s=s: e.scalar_tensor_tensor(
                    out=nmr[:, s], in0=mv[:, s, :, 0], scalar=-1.0, in1=rstd[:, s], op0=ALU.mult, op1=ALU.mult), [v1], "v")
                for j in range(K):
                    z0 = b.do("vector", lambda e, s=s, j=j: e.tensor_scalar(
                        yt[:, s, 0, j, :], yt[:, s, 0, j, :], rstd[:, s, j:j + 1], nmr[:, s, j:j + 1], ALU.mult, ALU.add),
                        [v2], "v")
                for f in range(K // 4):
                    i = q * (K // 4) + f
                    def tr(e, s=s, f=f):
                        for j in range(4):
                            last = e.transpose(tp[:, j * P:(j + 1) * P], xt[:, s, 4 * f + j, :], const["eye"][:, :])
                        return last
                    t = b.do("tensor", tr, [lx, tev.get(i - 1)], "t")
                    tev[i] = b.do("scalar", lambda e, i=i: e.activation(gn[:, i % 2, :], tp[:, :], ACT.Identity,
                                  bias=shift_col[:, 0:1], scale=scale_col[:, 0:1]), [t, zmm.get(i - 2)], "gn")
                    for half in range(HALVES):
                        t = zmm[i] = b.do("tensor", lambda e, i=i, half=half: e.matmul(
                            zp[:, half, :], wts["w_in"][:, D_INNER + half * P:D_INNER + (half + 1) * P], gn[:, i % 2, :],
                            start=True, stop=True), [tev[i], zev.get((i - 1, half))], "t")
                        zev[i, half] = b.do("scalar", lambda e, i=i, half=half: e.activation(
                            zs[:, i % 2, half, :], zp[:, half, :], ACT.Silu), [t, zmul.get((i - 2, half))], "z")
                    for half in range(HALVES):
                        def ty(e, s=s, f=f, half=half):
                            for j in range(4):
                                last = e.transpose(yp[:, half, j * P:(j + 1) * P], yt[:, s, 0, 4 * f + j, half * P:(half + 1) * P],
                                                   const["eye"][:, :])
                            return last
                        t = ynt[q] = b.do("tensor", ty, [z0, yev.get((i - 1, half))], "t")
                        yev[i, half] = b.do("scalar", lambda e, i=i, half=half: e.activation(
                            yn[:, i % 2, half, :], yp[:, half, :], ACT.Identity, bias=wts["ln_b"][:, half:half + 1],
                            scale=wts["ln_w"][:, half:half + 1]), [t, omm.get(i - 2)], "yn")
                        zmul[i, half] = b.do("gpsimd", lambda e, i=i, half=half: e.tensor_tensor(
                            yn[:, i % 2, half, :], yn[:, i % 2, half, :], zs[:, i % 2, half, :], ALU.mult),
                            [yev[i, half], zev[i, half]], "zmul")
                    def mo(e, i=i):
                        for j in range(4):
                            for half in range(HALVES):
                                last = e.matmul(op[:, i % 2, j * P:(j + 1) * P], yn[:, i % 2, half, j * P:(j + 1) * P],
                                                wts["w_out"][:, half, :], start=(half == 0), stop=(half == HALVES - 1))
                        return last
                    t = omm[i] = b.do("tensor", mo, [zmul[i, 1], oev.get((q - 1, f)) if q else None], "t")
                    oev[q, f] = b.do("vector", lambda e, i=i, s=s, f=f: e.tensor_tensor(
                        flat(ot[:, s, 4 * f:4 * f + 4]), op[:, i % 2, :], flat(xt[:, s, 4 * f:4 * f + 4]), ALU.add),
                        [t, stored.get(q - 2)], "oev")
                stored[q] = b.dma("sync", lambda e, q=q, s=s: e.dma_start(dst[it, q], ot[:, s]), [oev[q, 1]], f"store{s}")
            b.do("sync", lambda e: e.nop(), [stored[PER_BODY - 1], stored[PER_BODY - 2]])
            b.run()


_WEIGHTS = {
    "ln_scale": (P, 1), "ln_bias": (P, 1), "Wq": (C, C), "Wk": (C, C), "Wvg": (C, 2 * C), "Wb": (C, HEADS), "Wo": (C, C),
    "w_in": (C, 2 * D_INNER), "conv_w": (P, HALVES, 9), "conv_b": (P, HALVES),
    "proj_b": (DIRECTIONS, P, HALVES, 96 + DT_RANK), "proj_c": (DIRECTIONS, P, HALVES, 96),
    "dt_w": (DIRECTIONS, DT_RANK, D_INNER), "dt_b": (DIRECTIONS, P, HALVES), "A_logs": (DIRECTIONS, P, HALVES, D_STATE),
    "Ds": (P, HALVES, DIRECTIONS), "ln_w": (P, HALVES), "ln_b": (P, HALVES), "w_out": (P, HALVES, C),
}


def build(nc, x, dram, out, eye, mean, group_of, spread, phases="0123456789", outputs=None, scan_turns=None):
    f = lambda name, shape: (outputs or {}).get(name) or nc.dram_tensor(name, shape, F32).ap()
    zn_t = f("zn_t", (SIDE // 8, C, 8 * SIDE))
    bias_d = f("bias_d", (HEADS, TOKENS))
    x1 = f("x1", (TOKENS, C))
    xc_tok = f("xc_tok", (TOKENS, D_INNER))
    ys = [f(f"y{k}", (TOKENS, D_INNER)) for k in range(DIRECTIONS)]
    with ExitStack() as stack:
        m = Memory(nc, stack)
        sems = [stack.enter_context(nc.semaphore(f"s{i}")) for i in range(40)]
        assert all(b.num == a.num + 1 for a, b in zip(sems, sems[1:]))
        const = {"eye": m.sb("eye", [P, P]), "mean": m.sb("mean", [P, P]), "group_of": m.sb("group_of", [P, GROUPS]),
                 "spread": m.sb("spread", [96, D_STATE, P], BF16)}
        spread32 = m.sb("spread32", [96, D_STATE, P])
        scale_row, shift_row = m.sb("scale_row", [P, GROUPS]), m.sb("shift_row", [P, GROUPS])
        scale_col, shift_col = m.sb("scale_col", [P, 1]), m.sb("shift_col", [P, 1])
        per_direction = ("proj_b", "proj_c", "dt_w", "dt_b", "A_logs")
        wts = {}
        for name, shape in _WEIGHTS.items():
            if name in per_direction:
                wts[name] = [m.sb(f"w_{name}{k}", list(shape[1:])) for k in range(DIRECTIONS)]
            else:
                wts[name] = m.sb(f"w_{name}", list(shape))
        whole = lambda t: t[tuple(slice(None) for _ in t.shape)]
        wts["a_neg"] = [m.sb(f"a_neg{k}", [P, HALVES, D_STATE]) for k in range(DIRECTIONS)]
        wts["guard_less_dt_b"] = [m.sb(f"gdt{k}", [P, HALVES]) for k in range(DIRECTIONS)]
        guard = m.sb("guard", [P, 1])
        d_sum, d_diag = m.sb("d_sum", [P, HALVES]), m.sb("d_diag", [P, HALVES, P])

        b = Body(nc, sems)
        for tile, source in ((const["eye"], eye), (const["mean"], mean), (const["group_of"], group_of), (spread32, spread)):
            ld = b.dma("sync", lambda e, tile=tile, source=source: e.dma_start(whole(tile), source), [], "load")
        for name in _WEIGHTS:
            tiles = wts[name] if name in per_direction else [wts[name]]
            for k, tile in enumerate(tiles):
                source = dram[name][k] if name in per_direction else dram[name]
                ld = b.dma("sync", lambda e, tile=tile, source=source: e.dma_start(whole(tile), source), [], "load")
        b.do("vector", lambda e: e.memset(guard[:, :], 20.0))
        b.do("vector", lambda e: e.tensor_copy(const["spread"][:, :, :], spread32[:, :, :]), [ld])
        ds = b.do("vector", lambda e: e.tensor_reduce(d_sum[:, :], wts["Ds"][:, :, :], AX_X, ALU.add), [ld], "v")
        for half in range(HALVES):
            b.do("vector", lambda e, half=half: e.tensor_scalar(d_diag[:, half, :], const["eye"][:, :], d_sum[:, half:half + 1],
                 None, ALU.mult), [ds])
        for k in range(DIRECTIONS):
            b.do("vector", lambda e, k=k: e.tensor_scalar(wts["guard_less_dt_b"][k][:, :], wts["dt_b"][k][:, :], -1.0, 20.0,
                 ALU.mult, ALU.add), [ld])
            ex = b.do("scalar", lambda e, k=k: e.activation(wts["a_neg"][k][:, :, :], wts["A_logs"][k][:, :, :], ACT.Exp), [ld], "a")
            b.do("vector", lambda e, k=k: e.tensor_scalar(wts["a_neg"][k][:, :, :], wts["a_neg"][k][:, :, :], -1.0, None,
                 ALU.mult), [ex])
        b.run()

        if "0" in phases:
            group_stats(nc, sems, "g0", x, 1e-5, const, scale_row, shift_row)
        if "1" in phases:
            norm_phase(nc, sems, x, zn_t, bias_d, wts, const, scale_row, shift_row)
        if "2" in phases:
            attention_phase(nc, sems, x, zn_t, bias_d, x1, wts, const)
        if "3" in phases:
            group_stats(nc, sems, "g1", x1, 1e-5, const, scale_row, shift_row, (scale_col, shift_col))
        if "4" in phases:
            conv_phase(nc, sems, x1, xc_tok, wts, const, scale_col, shift_col)
        for k in range(DIRECTIONS):
            if str(5 + k) in phases:
                own = {n: wts[n][k] for n in per_direction + ("a_neg", "guard_less_dt_b")}
                scan_phase(nc, sems, k, xc_tok, ys[k], {**wts, **own, "guard": guard, "d_diag": d_diag}, const, scan_turns)
        if "9" in phases:
            output_phase(nc, sems, ys, x1, out, wts, const, scale_col, shift_col)


def laid_out(w):
    halves = lambda a: np.ascontiguousarray(np.moveaxis(a.reshape((HALVES, P) + a.shape[1:]), 0, 1))
    xp = w["L1_conv_x_proj_w"]
    proj_b = np.zeros((DIRECTIONS, D_INNER, 96 + DT_RANK), np.float32)
    proj_c = np.zeros((DIRECTIONS, D_INNER, 96), np.float32)
    for k in range(DIRECTIONS):
        for at in (0, 32, 64):
            proj_b[k, :, at:at + D_STATE] = xp[k, DT_RANK:DT_RANK + D_STATE].T
            proj_c[k, :, at:at + D_STATE] = xp[k, DT_RANK + D_STATE:].T
        proj_b[k, :, 96:] = xp[k, :DT_RANK].T
    each = lambda a: np.stack([halves(a[k]) for k in range(DIRECTIONS)])
    return {
        "ln_scale": w["L0_conv_ln_scale"].reshape(P, 1), "ln_bias": w["L0_conv_ln_bias"].reshape(P, 1),
        "Wq": w["L0_conv_Wq"], "Wk": w["L0_conv_Wk"], "Wvg": np.concatenate([w["L0_conv_Wv"], w["L0_conv_Wg"]], 1),
        "Wb": w["L0_conv_Wb"], "Wo": w["L0_conv_Wo"], "w_in": w["L1_conv_w_in"].T,
        "conv_w": halves(w["L1_conv_conv_w"].reshape(D_INNER, 9)), "conv_b": halves(w["L1_conv_conv_b"]),
        "proj_b": each(proj_b), "proj_c": each(proj_c), "dt_w": np.moveaxis(w["L1_conv_dt_w"], 1, 2),
        "dt_b": each(w["L1_conv_dt_b"]), "A_logs": each(w["L1_conv_A_logs"].reshape(DIRECTIONS, D_INNER, D_STATE)),
        "Ds": halves(w["L1_conv_Ds"].reshape(DIRECTIONS, D_INNER).T), "ln_w": halves(w["L1_conv_ln_w"]),
        "ln_b": halves(w["L1_conv_ln_b"]), "w_out": halves(w["L1_conv_w_out"].T),
    }


def constants():
    spread = np.zeros((96, D_STATE, P), np.float32)
    for n in range(D_STATE):
        for at in (0, 32, 64):
            spread[at + n, n, :] = 1.0
    return {"eye": np.eye(P, dtype=np.float32), "mean": np.full((P, P), 1.0 / P, np.float32),
            "group_of": np.repeat(np.eye(GROUPS, dtype=np.float32), PER_GROUP, axis=0), "spread": spread}


def kernel(**inputs):
    import concourse.bacc as bacc
    from concourse.bass_utils import run_bass_kernel_spmd

    w = {n: np.asarray(a) for n, a in inputs.items()}
    arrays = {"x": np.ascontiguousarray(w["x"]).reshape(TOKENS, C)}
    arrays.update({n: np.ascontiguousarray(a) for n, a in laid_out(w).items()})
    arrays.update(constants())
    nc = bacc.Bacc("TRN2", target_bir_lowering=False, num_devices=1)
    dram = {n: nc.dram_tensor(f"in_{n}", a.shape, F32, kind="ExternalInput").ap() for n, a in arrays.items()}
    out = nc.dram_tensor("out", (TOKENS, C), F32, kind="ExternalOutput").ap()
    build(nc, dram["x"], dram, out, dram["eye"], dram["mean"], dram["group_of"], dram["spread"])
    r = run_bass_kernel_spmd(nc, [{f"in_{n}": a for n, a in arrays.items()}], core_ids=[0])
    return r.results[0]["out"].reshape(1, SIDE, SIDE, C)
```

```python
from contextlib import ExitStack

import numpy as np
import concourse.bass as bass
from concourse import mybir

F32 = mybir.dt.float32
BF16 = mybir.dt.bfloat16
ALU = mybir.AluOpType
ACT = mybir.ActivationFunctionType
AX_X = mybir.AxisListType.X

P = 128
SIDE = 256
TOKENS = SIDE * SIDE
C = 128
GROUPS = 32
PER_GROUP = C // GROUPS
HEADS, HEAD_DIM = 4, 32
JB = SIDE // P
D_INNER = 256
HALVES = D_INNER // P
D_STATE = 16
DT_RANK = 8
DIRECTIONS = 4
BANK = 512

ENGINES = ("tensor", "vector", "scalar", "gpsimd", "sync")


class Body:

    def __init__(self, nc, semaphores):
        self.nc, self.semaphores = nc, semaphores
        self.named, self.counts, self.owner = {}, {}, {}
        self.queues = {e: [] for e in ENGINES}

    def do(self, engine, issue, after=(), signal=None):
        mark, step = None, 1
        if signal is not None:
            if signal not in self.named:
                self.named[signal] = self.semaphores[len(self.named)]
                self.counts[signal], self.owner[signal] = 0, engine
            assert self.owner[signal] == engine
            self.counts[signal] += 1
            mark = (signal, self.counts[signal])
        self.queues[engine].append((issue, [m for m in after if m], signal, step))
        return mark

    def dma(self, engine, issue, after=(), signal=None):
        mark = self.do(engine, issue, after, signal)
        queue = self.queues[engine]
        queue[-1] = queue[-1][:3] + (16,)
        return (mark[0], mark[1] * 16)

    def run(self):
        nc = self.nc
        with nc.Block() as block:
            for name in ENGINES:
                def program(engine, queue=self.queues[name]):
                    for issue, after, signal, step in queue:
                        for what, count in after:
                            engine.wait_ge(self.named[what], count)
                        last = issue(engine)
                        if signal is not None:
                            last.then_inc(self.named[signal], step)
                start = {"tensor": block.tensor, "vector": block.vector, "scalar": block.scalar,
                         "gpsimd": block.gpsimd, "sync": block.sync}
                start[name](program)
        first = self.semaphores[0].num
        nc.vector.sem_clear(range(first, first + len(self.semaphores)))
        nc.all_engine_barrier()


class Memory:

    def __init__(self, nc, stack):
        self.nc, self.stack = nc, stack

    def sb(self, name, shape, dtype=F32):
        return self.stack.enter_context(self.nc.sbuf_tensor(name, shape, dtype))

    def ps(self, name, shape, dtype=F32):
        return self.stack.enter_context(self.nc.psum_tensor(name, shape, dtype))


def group_stats(nc, sems, name, x, eps, const, scale_row, shift_row, columns=None):
    CHUNK = BANK // PER_GROUP
    per_part = TOKENS // P
    chunks = per_part // CHUNK
    with ExitStack() as stack:
        m = Memory(nc, stack)
        xt = m.sb(f"{name}_x", [P, 2, CHUNK, C])
        st = m.sb(f"{name}_st", [P, GROUPS, chunks, 6])
        mv = m.sb(f"{name}_mv", [P, GROUPS, 2])
        avg = m.sb(f"{name}_avg", [P, GROUPS, 2])
        dev = m.sb(f"{name}_dev", [P, GROUPS])
        var = m.sb(f"{name}_var", [P, GROUPS])
        std = m.sb(f"{name}_std", [P, GROUPS])
        pick = m.sb(f"{name}_pick", [P, 2, GROUPS])
        total = m.ps(f"{name}_total", [P, 2, BANK])
        src = x.rearrange("(p j k) c -> j p k c", p=P, k=CHUNK)
        b = Body(nc, sems)
        stats = [None] * chunks
        for j in range(chunks):
            loaded = b.dma("sync", lambda e, j=j: e.dma_start(xt[:, j % 2], src[j]),
                           [stats[j - 2] if j >= 2 else None], f"load{j % 2}")
            for g in range(GROUPS):
                stats[j] = b.do("vector", lambda e, j=j, g=g: e.bn_stats(
                    st[:, g, j, :], xt[:, j % 2, :, g * PER_GROUP:(g + 1) * PER_GROUP]), [loaded], "stats")
        for g in range(GROUPS):
            aggr = b.do("vector", lambda e, g=g: e.bn_aggr(mv[:, g, :], st[:, g]), [stats[-1]], "aggr")
        t0 = b.do("tensor", lambda e: e.matmul(total[:, 0, 0:2 * GROUPS], const["mean"][:, :],
                  mv[:, :, :].rearrange("p g s -> p (g s)"), start=True, stop=True), [aggr], "t")
        a0 = b.do("vector", lambda e: e.tensor_copy(avg[:, :, :].rearrange("p g s -> p (g s)"),
                  total[:, 0, 0:2 * GROUPS]), [t0], "v")
        d0 = b.do("vector", lambda e: e.tensor_tensor(dev[:, :], mv[:, :, 0], avg[:, :, 0], ALU.subtract), [a0], "v")
        d1 = b.do("vector", lambda e: e.tensor_tensor(dev[:, :], dev[:, :], dev[:, :], ALU.mult), [d0], "v")
        t1 = b.do("tensor", lambda e: e.matmul(total[:, 1, 0:GROUPS], const["mean"][:, :], dev[:, :],
                  start=True, stop=True), [d1], "t")
        v0 = b.do("vector", lambda e: e.tensor_tensor(var[:, :], avg[:, :, 1], total[:, 1, 0:GROUPS], ALU.add), [t1], "v")
        v1 = b.do("vector", lambda e: e.tensor_scalar(var[:, :], var[:, :], eps, None, ALU.add), [v0], "v")
        s0 = b.do("scalar", lambda e: e.activation(std[:, :], var[:, :], ACT.Sqrt), [v1], "s")
        r0 = b.do("vector", lambda e: e.reciprocal(scale_row[:, :], std[:, :]), [s0], "v")
        r1 = b.do("vector", lambda e: e.scalar_tensor_tensor(out=shift_row[:, :], in0=avg[:, :, 0], scalar=-1.0,
                  in1=scale_row[:, :], op0=ALU.mult, op1=ALU.mult), [r0], "v")
        if columns:
            for i, (row, column) in enumerate(zip((scale_row, shift_row), columns)):
                p0 = b.do("vector", lambda e, i=i, row=row: e.tensor_tensor(
                    pick[:, i, :], row[:, :], const["group_of"][:, :], ALU.mult), [r1], "v")
                b.do("vector", lambda e, i=i, column=column: e.tensor_reduce(
                    column[:, 0:1], pick[:, i, :], AX_X, ALU.add), [p0], "v")
        b.run()


def norm_phase(nc, sems, x, zn_t, bias_d, wts, const, scale_row, shift_row):
    ROWS = 8
    CT = ROWS * SIDE
    BLOCKS = CT // P
    PER_BODY = 8
    with ExitStack() as stack:
        m = Memory(nc, stack)
        xt = m.sb("n_x", [P, 2, BLOCKS, C])
        gt = m.sb("n_g", [P, 2, BLOCKS, C])
        st = m.sb("n_st", [P, 2, BLOCKS, 6])
        mv = m.sb("n_mv", [P, 2, BLOCKS, 2])
        std = m.sb("n_std", [P, 2, BLOCKS])
        rstd = m.sb("n_rstd", [P, 2, BLOCKS])
        nmr = m.sb("n_nmr", [P, 2, BLOCKS])
        zt = m.sb("n_zt", [P, 2, CT])
        bt = m.sb("n_bt", [HEADS, 2, CT])
        tp = m.ps("n_tp", [P, 4, BANK])
        bp = m.ps("n_bp", [P, 2, BANK])
        src = x.rearrange("(i q b p) c -> i q p b c", q=PER_BODY, b=BLOCKS, p=P)
        dst = zn_t.rearrange("(i q) c t -> i q c t", q=PER_BODY)
        bdst = bias_d.rearrange("h (i q t) -> i q h t", q=PER_BODY, t=CT)
        four = lambda v: v.rearrange("p b (g c) -> p b g c", c=PER_GROUP)
        row = lambda v: v[:, :].unsqueeze(1).unsqueeze(3).to_broadcast([P, BLOCKS, GROUPS, PER_GROUP])
        with nc.Fori(0, TOKENS // (CT * PER_BODY)) as it:
            b = Body(nc, sems)
            turned, evac, bevac, stored, bstored, loaded, normed, pb = ({} for _ in range(8))

            def load(q):
                s = q % 2
                for half in (slice(0, BLOCKS // 2), slice(BLOCKS // 2, BLOCKS)):
                    loaded[q] = b.dma("sync", lambda e, half=half: e.dma_start(xt[:, s, half], src[it, q, :, half]),
                                      [turned.get(q - 2)], f"load{s}")

            def normalize(q):
                s = q % 2
                g0 = b.do("vector", lambda e: e.tensor_tensor(four(gt[:, s]), four(xt[:, s]), row(scale_row),
                          ALU.mult), [loaded[q], turned.get(q - 2)], "v")
                g1 = b.do("vector", lambda e: e.tensor_tensor(four(gt[:, s]), four(gt[:, s]), row(shift_row),
                          ALU.add), [g0], "v")
                for j in range(BLOCKS):
                    s0 = b.do("vector", lambda e, j=j: e.bn_stats(st[:, s, j, :], gt[:, s, j, :]), [g1], "v")
                for j in range(BLOCKS):
                    s1 = b.do("vector", lambda e, j=j: e.bn_aggr(mv[:, s, j, :], st[:, s, j, :]), [s0], "v")
                v0 = b.do("vector", lambda e: e.tensor_scalar(std[:, s], mv[:, s, :, 1], 1e-5, None, ALU.add), [s1], "v")
                q0 = b.do("scalar", lambda e: e.activation(std[:, s], std[:, s], ACT.Sqrt), [v0], "s")
                v1 = b.do("vector", lambda e: e.reciprocal(rstd[:, s], std[:, s]), [q0], "v")
                v2 = b.do("vector", lambda e: e.scalar_tensor_tensor(
                    out=nmr[:, s], in0=mv[:, s, :, 0], scalar=-1.0, in1=rstd[:, s], op0=ALU.mult, op1=ALU.mult), [v1], "v")
                for j in range(BLOCKS):
                    normed[q] = b.do("vector", lambda e, j=j: e.tensor_scalar(
                        gt[:, s, j, :], gt[:, s, j, :], rstd[:, s, j:j + 1], nmr[:, s, j:j + 1], ALU.mult, ALU.add),
                        [v2], "v")

            def turn(q, f):
                k, s = q * 4 + f, q % 2
                def tr(e):
                    for j in range(4):
                        last = e.transpose(tp[:, f, j * P:(j + 1) * P], gt[:, s, 4 * f + j, :], const["eye"][:, :])
                    return last
                turned[q] = b.do("tensor", tr, [normed[q], evac.get(k - 4)], "turn")
                evac[k] = b.do("scalar", lambda e: e.activation(
                    zt[:, s, f * BANK:(f + 1) * BANK], tp[:, f, :], ACT.Identity, bias=wts["ln_bias"][:, 0:1],
                    scale=wts["ln_scale"][:, 0:1]), [turned[q], stored.get(q - 2)], "evac")

            def pair_bias(q, f):
                k, s = q * 4 + f, q % 2
                t = b.do("tensor", lambda e: e.matmul(
                    bp[0:HEADS, f % 2, :], wts["Wb"][:, :], zt[:, s, f * BANK:(f + 1) * BANK], start=True, stop=True),
                    [evac[k], bevac.get(k - 2)], "pb")
                bevac[k] = b.do("scalar", lambda e: e.copy(
                    bt[:, s, f * BANK:(f + 1) * BANK], bp[0:HEADS, f % 2, :]), [t, bstored.get(q - 2)], "bevac")

            N = PER_BODY
            load(0)
            load(1)
            normalize(0)
            for q in range(N):
                s = q % 2
                for f in range(4):
                    turn(q, f)
                if q + 2 < N:
                    load(q + 2)
                for f in range(4):
                    pair_bias(q, f)
                if q + 1 < N:
                    normalize(q + 1)
                stored[q] = b.dma("sync", lambda e, q=q, s=s: e.dma_start(dst[it, q], zt[:, s]), [evac[4 * q + 3]], f"st{s}")
                bstored[q] = b.dma("sync", lambda e, q=q, s=s: e.dma_start(bdst[it, q], bt[:, s]), [bevac[4 * q + 3]], f"bst{s}")
            b.do("sync", lambda e: e.nop(), [stored[N - 1], stored[N - 2], bstored[N - 1], bstored[N - 2]])
            b.run()


def attention_phase(nc, sems, x, zn_t, bias_d, x1, wts, const):
    ROWS = 32
    CHUNK = zn_t.shape[2] // SIDE
    SCALE = float(HEAD_DIM) ** -0.5
    V1 = HEAD_DIM + 1
    with ExitStack() as stack:
        m = Memory(nc, stack)
        zt = m.sb("a_zt", [P, ROWS, SIDE])
        xt = m.sb("a_xt", [P, ROWS, JB, C])
        bias = m.sb("a_bias", [P, JB, HEADS, SIDE])
        qk = m.sb("a_qk", [P, 2, 2, SIDE])
        v1 = m.sb("a_v1", [P, 4, JB, HEADS, V1])
        gate = m.sb("a_gate", [P, 4, JB, C])
        sc = m.sb("a_sc", [P, 3, HEADS, JB, SIDE])
        top = m.sb("a_top", [P, 3, HEADS, JB])
        ntop = m.sb("a_ntop", [P, 3, HEADS, JB])
        pt = m.sb("a_pt", [P, 2, HEADS, JB, SIDE])
        den = m.sb("a_den", [P, 2, JB, HEADS])
        rden = m.sb("a_rden", [P, 2, JB, HEADS])
        go = m.sb("a_go", [P, 2, JB, C])
        gt = m.sb("a_gt", [P, 2, SIDE])
        scores = m.ps("a_scores", [P, HEADS, BANK])
        proj = m.ps("a_proj", [P, BANK])
        turn = m.ps("a_turn", [P, 2, BANK])
        mix = m.ps("a_mix", [P, BANK])
        xsrc = x.rearrange("(i r b p) c -> i p r b c", r=ROWS, b=JB, p=P)
        xdst = x1.rearrange("(i r b p) c -> i p r b c", r=ROWS, b=JB, p=P)
        zsrc = zn_t.rearrange("(i q) c (r t) -> i q c r t", q=ROWS // CHUNK, t=SIDE)

        b = Body(nc, sems)
        bsrc = bias_d.rearrange("h (b j k) -> b j h k", b=JB, j=P)
        for jb in range(JB):
            ld = b.dma("sync", lambda e, jb=jb: e.dma_start(bias[:, jb], bsrc[jb]), [], "bias")
        b.do("sync", lambda e: e.nop(), [ld])
        b.do("vector", lambda e: e.memset(v1[:, :, :, :, :].rearrange("p s b h v -> p (s b h v)"), 1.0))
        b.run()

        with nc.Fori(0, SIDE // ROWS) as it:
            b = Body(nc, sems)
            N = ROWS
            zl, xl, stores = {}, {}, []
            for q in range(N // CHUNK):
                zl[q] = b.dma("sync", lambda e, q=q: e.dma_start(zt[:, q * CHUNK:(q + 1) * CHUNK], zsrc[it, q]), [], f"loadz{q}")
            for q in range(N // CHUNK):
                for half in (slice(q * CHUNK, q * CHUNK + CHUNK // 2), slice(q * CHUNK + CHUNK // 2, (q + 1) * CHUNK)):
                    xl[q] = b.dma("sync", lambda e, half=half: e.dma_start(xt[:, half], xsrc[it, :, half]), [], f"loadx{q}")
            qk_ev, v_ev, exps, t_last, t_ev, pv, gated, gt_ev, y_mm, y_ev, s_mm, s_ev, neg = ({} for _ in range(13))

            def project(r):
                def qk_mm(e):
                    e.matmul(proj[:, 0:SIDE], wts["Wq"][:, :], zt[:, r, :], start=True, stop=True)
                    return e.matmul(proj[:, SIDE:], wts["Wk"][:, :], zt[:, r, :], start=True, stop=True)
                t = b.do("tensor", qk_mm, [zl[r // CHUNK], v_ev.get(r - 1)], "proj")
                qk_ev[r] = b.do("scalar", lambda e: e.copy(
                    qk[:, r % 2].rearrange("p a t -> p (a t)"), proj[:, :]), [t, s_mm.get(r - 2)], "qkev")

            def values(r):
                def vg_mm(e):
                    for jb in range(JB):
                        last = e.matmul(proj[:, jb * SIDE:(jb + 1) * SIDE], zt[:, r, jb * P:(jb + 1) * P],
                                        wts["Wvg"][:, :], start=True, stop=True)
                    return last
                t = b.do("tensor", vg_mm, [qk_ev[r]], "proj")
                pv_view = proj[:, :].rearrange("p (b a n) -> p b a n", b=JB, a=2)
                tan = b.do("scalar", lambda e: e.activation(gate[:, r % 4], pv_view[:, :, 1, :], ACT.Tanh, scale=0.5),
                           [t, gated.get(r - 4)], "gate")
                v_ev[r] = b.do("vector", lambda e: e.tensor_copy(
                    v1[:, r % 4, :, :, 0:HEAD_DIM], pv_view[:, :, 0, :].rearrange("p b (h d) -> p b h d", h=HEADS)),
                    [tan, pv.get(r - 4)], "vev")

            def score(r):
                for h in range(HEADS):
                    def mm(e, h=h):
                        rows = slice(h * HEAD_DIM, (h + 1) * HEAD_DIM)
                        for jb in range(JB):
                            last = e.matmul(scores[:, h, jb * SIDE:(jb + 1) * SIDE],
                                            qk[rows, r % 2, 0, jb * P:(jb + 1) * P], qk[rows, r % 2, 1, :],
                                            start=True, stop=True)
                        return last
                    s_mm[r] = t = b.do("tensor", mm, [qk_ev[r], s_ev.get((r - 1, h))], "score")
                    s_ev[r, h] = b.do("vector", lambda e, h=h: e.scalar_tensor_tensor(
                        out=sc[:, r % 3, h, :, :], in0=scores[:, h, :].rearrange("p (b k) -> p b k", b=JB), scalar=SCALE,
                        in1=bias[:, :, h, :], op0=ALU.mult, op1=ALU.add), [t, t_last.get(r - 3)], "sev")

            def maximum(r):
                mx = b.do("vector", lambda e: e.tensor_reduce(
                    top[:, r % 3], sc[:, r % 3], AX_X, ALU.max), [s_ev[r, HEADS - 1]], "v")
                neg[r] = b.do("vector", lambda e: e.tensor_scalar(ntop[:, r % 3], top[:, r % 3], -1.0, None, ALU.mult),
                              [mx, exps.get((r - 3, HEADS - 1))], "v")

            def exponentials(r):
                for h in range(HEADS):
                    def ex(e, h=h):
                        for jb in range(JB):
                            last = e.activation(sc[:, r % 3, h, jb, :], sc[:, r % 3, h, jb, :], ACT.Exp,
                                                bias=ntop[:, r % 3, h, jb:jb + 1])
                        return last
                    exps[r, h] = b.do("scalar", ex, [neg[r]], "exp")

            def turn_weights(r, heads):
                for h in heads:
                    def tr(e, h=h):
                        for kb in range(JB):
                            for jb in range(JB):
                                last = e.transpose(turn[:, h % 2, kb * SIDE + jb * P:kb * SIDE + (jb + 1) * P],
                                                   sc[:, r % 3, h, jb, kb * P:(kb + 1) * P], const["eye"][:, :])
                        return last
                    t_last[r] = t = b.do("tensor", tr, [exps[r, h], t_ev.get((r, h - 2)), t_ev.get((r - 1, h + 2))], "turn")
                    who = "scalar" if h % 2 else "vector"
                    def ev(e, h=h):
                        dst, src = pt[:, r % 2, h].rearrange("p b k -> p (b k)"), turn[:, h % 2, :]
                        return e.copy(dst, src) if h % 2 else e.tensor_copy(dst, src)
                    t_ev[r, h] = b.do(who, ev, [t, pv.get(r - 2)], f"tev{h % 2}")

            def mix_values(r):
                for h in range(HEADS):
                    def mm(e, h=h):
                        for jb in range(JB):
                            for kb in range(JB):
                                at = (jb * HEADS + h) * V1
                                last = e.matmul(mix[:, at:at + V1], pt[:, r % 2, h, kb, jb * P:(jb + 1) * P],
                                                v1[:, r % 4, kb, h, :], start=(kb == 0), stop=(kb == JB - 1))
                        return last
                    pv[r] = b.do("tensor", mm, [t_ev[r, h], v_ev[r], y_ev.get(r - 1)], "pv")
                o = mix[:, 0:JB * HEADS * V1].rearrange("p (b h v) -> p b h v", b=JB, h=HEADS)
                d0 = b.do("vector", lambda e: e.tensor_scalar(den[:, r % 2], o[:, :, :, HEAD_DIM], 2.0, None, ALU.mult), [pv[r]], "v")
                g0 = b.do("vector", lambda e: e.scalar_tensor_tensor(
                    out=go[:, r % 2].rearrange("p b (h d) -> p b h d", h=HEADS),
                    in0=gate[:, r % 4].rearrange("p b (h d) -> p b h d", h=HEADS), scalar=1.0,
                    in1=o[:, :, :, 0:HEAD_DIM], op0=ALU.add, op1=ALU.mult), [pv[r], gt_ev.get(r - 2)], "v")
                d1 = b.do("vector", lambda e: e.reciprocal(rden[:, r % 2], den[:, r % 2]), [d0], "v")
                gated[r] = b.do("vector", lambda e: e.tensor_tensor(
                    go[:, r % 2].rearrange("p b (h d) -> p b h d", h=HEADS),
                    go[:, r % 2].rearrange("p b (h d) -> p b h d", h=HEADS),
                    rden[:, r % 2].unsqueeze(3).broadcast_to([P, JB, HEADS, HEAD_DIM]), ALU.mult), [g0, d1], "v")

            def gate_turn(r):
                def tr(e):
                    for jb in range(JB):
                        last = e.transpose(mix[:, jb * P:(jb + 1) * P], go[:, r % 2, jb, :], const["eye"][:, :])
                    return last
                t = b.do("tensor", tr, [gated[r]], "mix")
                gt_ev[r] = b.do("scalar", lambda e: e.copy(gt[:, r % 2, :], mix[:, 0:SIDE]), [t, y_mm.get(r - 2)], "gtev")

            def output(r):
                def mm(e):
                    for jb in range(JB):
                        last = e.matmul(mix[:, SIDE + jb * P:SIDE + (jb + 1) * P], gt[:, r % 2, jb * P:(jb + 1) * P],
                                        wts["Wo"][:, :], start=True, stop=True)
                    return last
                y_mm[r] = b.do("tensor", mm, [gt_ev[r]], "ymm")
                y_ev[r] = b.do("vector", lambda e: e.tensor_tensor(
                    xt[:, r].rearrange("p b c -> p (b c)"), mix[:, SIDE:2 * SIDE],
                    xt[:, r].rearrange("p b c -> p (b c)"), ALU.add), [y_mm[r], xl[r // CHUNK]], "yev")

            for r in range(-3, N + 1):
                if 0 <= r < N:
                    turn_weights(r, (0, 1))
                if 0 <= r - 1:
                    gate_turn(r - 1)
                if 0 <= r < N:
                    turn_weights(r, (2, 3))
                if 0 <= r - 1:
                    output(r - 1)
                    if r % CHUNK == 0:
                        rows = slice(r - CHUNK, r)
                        stores.append(b.dma("sync", lambda e, rows=rows: e.dma_start(xdst[it, :, rows], xt[:, rows]),
                                            [y_ev[r - 1]], f"store{r // CHUNK}"))
                if 0 <= r + 1 < N:
                    exponentials(r + 1)
                if 0 <= r + 2 < N:
                    score(r + 2)
                if r + 3 < N:
                    project(r + 3)
                if 0 <= r + 2 < N:
                    maximum(r + 2)
                if 0 <= r < N:
                    mix_values(r)
                if r + 3 < N:
                    values(r + 3)
            b.do("sync", lambda e: e.nop(), stores)
            b.run()


def conv_phase(nc, sems, x1, xc_tok, wts, const, scale_col, shift_col):
    ROWS = 16
    PAIR = 2
    STRIP = 4
    WIDE = SIDE + 2
    PAIRS, STRIPS = ROWS // PAIR, ROWS // STRIP
    with ExitStack() as stack:
        m = Memory(nc, stack)
        xt = m.sb("c_xt", [P, ROWS, JB, C])
        gn = m.sb("c_gn", [P, 2, BANK])
        xi = m.sb("c_xi", [P, HALVES, ROWS + 2, WIDE])
        acc = m.sb("c_acc", [P, 2, STRIP, SIDE])
        xc = m.sb("c_xc", [P, HALVES, ROWS, SIDE])
        ot = m.sb("c_ot", [P, ROWS, JB, D_INNER])
        tap = m.sb("c_tap", [P, 9, P])
        tp = m.ps("c_tp", [P, BANK])
        xp = m.ps("c_xp", [P, 2, BANK])
        cp = m.ps("c_cp", [P, 2, BANK])
        op = m.ps("c_op", [P, 2, BANK])
        src = x1.rearrange("(h b p) c -> p h b c", b=JB, p=P)
        dst = xc_tok.rearrange("(h b p) d -> p h b d", b=JB, p=P)

        def rows_of(ap, first, count):
            return ap[:, bass.ds(first, count)] if not isinstance(first, int) else ap[:, first:first + count]

        class Inner:

            def __init__(self, b, first, slot, rows, after=None):
                self.b, self.slot, self.rows, self.after = b, slot, rows, after
                self.loads, self.tev, self.xev, self.mm = {}, {}, {}, {}
                for k in range((rows + 1) // PAIR):
                    count = min(PAIR, rows - PAIR * k)
                    self.loads[k] = b.dma("sync", lambda e, k=k, count=count: e.dma_start(
                        xt[:, PAIR * k:PAIR * k + count], rows_of(src, first + PAIR * k, count)), [], f"load{k}")

            def pair(self, k):
                b = self.b
                count = min(PAIR, self.rows - PAIR * k)
                wide = count * SIDE
                def tr(e):
                    for j in range(count * JB):
                        last = e.transpose(tp[:, j * P:(j + 1) * P], xt[:, PAIR * k + j // JB, j % JB, :], const["eye"][:, :])
                    return last
                t = b.do("tensor", tr, [self.loads[k], self.tev.get(k - 1)], "pe")
                self.tev[k] = b.do("scalar", lambda e: e.activation(gn[:, k % 2, 0:wide], tp[:, 0:wide], ACT.Identity,
                                   bias=shift_col[:, 0:1], scale=scale_col[:, 0:1]), [t, self.mm.get(k - 2)], "gn")

            def product(self, k):
                b = self.b
                count = min(PAIR, self.rows - PAIR * k)
                wide = count * SIDE
                for half in range(HALVES):
                    t = self.mm[k] = b.do("tensor", lambda e, half=half: e.matmul(
                        xp[:, half, 0:wide], wts["w_in"][:, half * P:(half + 1) * P], gn[:, k % 2, 0:wide], start=True, stop=True),
                        [self.tev[k], self.xev.get((k - 1, half))], "pe")
                    def ev(e, half=half):
                        d = xi[:, half, self.slot + PAIR * k:self.slot + PAIR * k + count, 1:1 + SIDE]
                        v = xp[:, half, 0:wide].rearrange("p (r w) -> p r w", r=count)
                        return e.copy(d, v)
                    self.xev[k, half] = b.do("scalar", ev, [t, self.after], f"xev{half}")

        def one_turn(h0, last):
            b = Body(nc, sems)
            rows = ROWS - 1 if last else ROWS
            zero = b.do("vector", lambda e: e.memset(xi[:, :, ROWS + 1, :], 0.0), [], "zero") if last else None
            inner = Inner(b, h0 + 1, 2, rows)
            cev, oev, mark = {}, {}, {}
            sev, acc_used = {}, {}

            def strip(c):
                for t9 in range(9):
                    dy, dx = t9 // 3, t9 % 3
                    window = xi[:, 1, STRIP * c + dy:STRIP * c + dy + STRIP, dx:dx + SIDE]
                    w = wts["conv_w"][:, 1, t9:t9 + 1]
                    if t9 == 0:
                        a = b.do("vector", lambda e, window=window, w=w: e.tensor_scalar(
                            acc[:, c % 2], window, w, None, ALU.mult),
                            [inner.xev[(STRIP * c + STRIP - 1) // PAIR, 1], acc_used.get(c - 2), zero], "acc")
                    else:
                        a = b.do("vector", lambda e, window=window, w=w: e.scalar_tensor_tensor(
                            out=acc[:, c % 2], in0=window, scalar=w, in1=acc[:, c % 2], op0=ALU.mult, op1=ALU.add), [a], "acc")
                mark[c] = a

            def strip_silu(c):
                sev[c] = acc_used[c] = b.do("scalar", lambda e: e.activation(
                    xc[:, 1, STRIP * c:STRIP * (c + 1)], acc[:, c % 2], ACT.Silu, bias=wts["conv_b"][:, 1:2]), [mark[c]], "silu")

            def conv(k):
                def mm(e):
                    for t9 in range(9):
                        dy, dx = t9 // 3, t9 % 3
                        last = e.matmul(cp[:, k % 2, :].rearrange("p (r w) -> p r w", r=PAIR), tap[:, t9, :],
                                        xi[:, 0, PAIR * k + dy:PAIR * k + dy + PAIR, dx:dx + SIDE],
                                        start=(t9 == 0), stop=(t9 == 8))
                    return last
                mark["pe"] = t = b.do("tensor", mm, [inner.xev[k, 0], zero, cev.get(k - 2)], "pe")
                cev[k] = b.do("scalar", lambda e: e.activation(
                    xc[:, 0, PAIR * k:PAIR * (k + 1), :], cp[:, k % 2, :].rearrange("p (r w) -> p r w", r=PAIR),
                    ACT.Silu, bias=wts["conv_b"][:, 0:1]), [t], "silu")

            def turn(r):
                def tr(e):
                    for jb in range(JB):
                        for half in range(HALVES):
                            last = e.transpose(op[:, r % 2, jb * D_INNER + half * P:jb * D_INNER + (half + 1) * P],
                                               xc[:, half, r, jb * P:(jb + 1) * P], const["eye"][:, :])
                    return last
                t = b.do("tensor", tr, [sev[r // STRIP], cev[r // PAIR], oev.get(r - 2)], "pe")
                def ev(e):
                    return e.copy(ot[:, r].rearrange("p b d -> p (b d)"), op[:, r % 2, :])
                oev[r] = b.do("scalar", ev, [t], "oev")

            LAG = 3
            stores = []
            inner.pair(0)
            for k in range(PAIRS + LAG):
                if k + 1 < PAIRS:
                    inner.pair(k + 1)
                if k < PAIRS:
                    inner.product(k)
                if 1 <= k <= PAIRS:
                    conv(k - 1)
                if k < PAIRS and k % 2 == 1:
                    strip(k // 2)
                if k >= LAG and (k - LAG) % 2 == 0:
                    strip_silu((k - LAG) // 2)
                if k >= LAG:
                    for r in (PAIR * (k - LAG), PAIR * (k - LAG) + 1):
                        turn(r)
                    if r % 8 == 7:
                        stores.append(b.dma("sync", lambda e, r=r: e.dma_start(
                            rows_of(dst, h0 + (r - 7), 8), ot[:, r - 7:r + 1]), [oev[r]], f"store{r // 8}"))
            b.do("sync", lambda e: e.nop(), stores)
            b.do("gpsimd", lambda e: e.tensor_copy(xi[:, :, 0:2, :], xi[:, :, ROWS:ROWS + 2, :]), [mark["pe"], mark[STRIPS - 1]], None)
            b.run()

        b = Body(nc, sems)
        z = b.do("vector", lambda e: e.memset(xi[:, :, :, :].rearrange("p a r w -> p (a r w)"), 0.0), [], "zero")
        for t9 in range(9):
            b.do("vector", lambda e, t9=t9: e.tensor_scalar(tap[:, t9, :], const["eye"][:, :],
                 wts["conv_w"][:, 0, t9:t9 + 1], None, ALU.mult))
        top = Inner(b, 0, 1, 1, z)
        top.pair(0)
        top.product(0)
        b.run()
        turns = SIDE // ROWS
        with nc.Fori(0, turns - 1) as it:
            one_turn(it * ROWS, False)
        one_turn((turns - 1) * ROWS, True)


def scan_phase(nc, sems, k, xc_tok, y_before, y_k, wts, const, turns_limit=None):
    T = BANK
    SUBS = T // P
    TILES = TOKENS // T
    PER_BODY = 8
    NDA, NP_, NCB = 8, 8, 4
    backwards = k >= 2
    by_column = k % 2 == 1
    GUARD = 20.0
    flow = slice(None, None, -1) if backwards else slice(None)
    last_token = 0 if backwards else T - 1
    with ExitStack() as stack:
        m = Memory(nc, stack)
        xt = m.sb(f"s{k}_xt", [P, 2, SUBS, D_INNER])
        xc = m.sb(f"s{k}_xc", [P, 2, HALVES, T])
        rest = m.sb(f"s{k}_rest", [96, 2, T])
        mid = m.sb(f"s{k}_mid", [96, 2, T], BF16)
        parts = m.sb(f"s{k}_parts", [96, 2, 2, T], BF16)
        low = m.sb(f"s{k}_low", [DT_RANK, T])
        e1 = m.sb(f"s{k}_e1", [P, HALVES, T])
        delta = m.sb(f"s{k}_delta", [P, 2, HALVES, T])
        dx = m.sb(f"s{k}_dx", [P, 2, HALVES, T])
        da = m.sb(f"s{k}_da", [P, NDA, T])
        h = m.sb(f"s{k}_h", [P, HALVES, D_STATE, T])
        cb = m.sb(f"s{k}_cb", [P, NCB, T])
        prod = m.sb(f"s{k}_prod", [P, NP_, T])
        yt = m.sb(f"s{k}_yt", [P, 2, SUBS, D_INNER])
        yb = m.sb(f"s{k}_yb", [P, 2, SUBS, D_INNER]) if k else None
        pb = m.ps(f"s{k}_pb", [P, 2, BANK])
        pd = m.ps(f"s{k}_pd", [P, BANK])
        pc = m.ps(f"s{k}_pc", [P, BANK])
        py = m.ps(f"s{k}_py", [P, 2, BANK])
        pr = m.ps(f"s{k}_pr", [P, 2, BANK])

        if by_column:
            view = lambda t: t.rearrange("(b p w) d -> w p b d", b=JB, p=P)
        else:
            view = lambda t: t.rearrange("(i b p) d -> i p b d", b=JB, p=P)
        src, dst = view(xc_tok), view(y_k)
        before = view(y_before) if k else None

        b = Body(nc, sems)
        b.do("vector", lambda e: e.memset(h[:, :, :, last_token], 0.0))
        b.do("scalar", lambda e: e.preload_act_table_set("natural_log_exp_and_others"))
        b.run()

        def one_turn(it, first=False, last=False):
            b = Body(nc, sems)
            loads, turned, xc_ev, xc_used, split, spread_b, spread_c, dts, dx_ready, delta_ready = ({} for _ in range(10))
            exps, b_mm, db, scans, c_mm, c_ev, prods, sums, y_ev, stores = ({} for _ in range(10))
            before_loads, before_used = {}, {}
            pr_free = [None, None]

            def line(g, i):
                tile = (TILES - 1 - g) - it * PER_BODY if backwards else it * PER_BODY + g
                return tile * (T // SIDE) + i

            def load(g):
                for i in range(T // SIDE):
                    loads[g] = b.dma("sync", lambda e, i=i: e.dma_start(
                        xt[:, g % 2, i * JB:(i + 1) * JB, :], src[line(g, i)]), [turned.get(g - 2)], f"load{g % 2}")

            def prepare(g):
                s = g % 2
                both = lambda v: v.rearrange("p a t -> p (a t)")
                for half in range(HALVES):
                    def tr(e, half=half):
                        for j in range(SUBS):
                            last = e.transpose(pr[:, half, j * P:(j + 1) * P], xt[:, s, j, half * P:(half + 1) * P],
                                               const["eye"][:, :])
                        return last
                    turned[g] = b.do("tensor", tr, [loads.get(g), pr_free[half]], "prep")
                yield
                for half in range(HALVES):
                    xc_ev[g] = b.do("scalar", lambda e, half=half: e.copy(
                        xc[:, s, half, :], pr[:, half, :]), [turned[g], dx_ready.get(g - 2), xc_used.get(g - 2)], "prep_act")
                yield
                for which, name in enumerate(("proj_b", "proj_c")):
                    def mm(e, which=which, name=name):
                        rows = wts[name].shape[-1]
                        for half in range(HALVES):
                            last = e.matmul(pr[0:rows, which, :], wts[name][:, half, :], xc[:, s, half, :],
                                            start=(half == 0), stop=(half == HALVES - 1))
                        return last
                    t = b.do("tensor", mm, [xc_ev[g]], "prep")
                yield
                b.do("scalar", lambda e: e.copy(low[:, :], pr[96:96 + DT_RANK, 0, :]), [t, dts.get(g - 1)])
                up = b.do("scalar", lambda e: e.copy(both(parts[:, s]), both(pr[0:96])), [spread_c.get(g - 2)], "prep_act")
                yield
                re = b.do("vector", lambda e: e.tensor_tensor(both(rest[:, :, :]), both(pr[0:96]), both(parts[:, s]), ALU.subtract),
                          [up, split.get(g - 1)], "prep_dve")
                yield
                md = b.do("scalar", lambda e: e.copy(both(mid[:, :, :]), both(rest[:, :, :])), [re, split.get(g - 1)], "prep_act")
                for half in range(HALVES):
                    dts[g] = b.do("tensor", lambda e, half=half: e.matmul(
                        pr[:, half, :], wts["dt_w"][:, half * P:(half + 1) * P], low[:, :], start=True, stop=True),
                        [up, re], "prep")
                yield
                b.do("vector", lambda e: e.tensor_copy(parts[32:64, s], mid[32:64]), [md])
                split[g] = b.do("vector", lambda e: e.tensor_tensor(parts[64:96, s], rest[64:96], mid[64:96], ALU.subtract), [], "prep_dve")
                for half in range(HALVES):
                    rl = b.do("scalar", lambda e, half=half: e.activation(
                        e1[:, half, :], pr[:, half, :], ACT.Relu, bias=wts["guard_less_dt_b"][:, half:half + 1], scale=-1.0),
                        [dts[g], delta_ready.get(g - 1)], "prep_act")
                yield
                ex = b.do("scalar", lambda e: e.activation(e1[:, :, :], e1[:, :, :], ACT.Exp, scale=-1.0, bias=wts["guard"][:, 0:1]), [rl], "prep_act")
                yield
                ln = b.do("scalar", lambda e: e.activation(e1[:, :, :], e1[:, :, :], ACT.Ln, bias=1.0), [ex], "prep_act")
                yield
                for half in range(HALVES):
                    delta_ready[g] = pr_free[0] = pr_free[1] = b.do("vector", lambda e, half=half: e.scalar_tensor_tensor(
                        out=delta[:, s, half, :], in0=pr[:, half, :], scalar=wts["dt_b"][:, half:half + 1],
                        in1=e1[:, half, :], op0=ALU.add, op1=ALU.max), [ln, exps.get((g - 2, D_STATE - 1, 1))], "prep_dve")
                yield
                dx_ready[g] = b.do("vector", lambda e: e.tensor_tensor(
                    dx[:, s], delta[:, s], xc[:, s], ALU.mult), [delta_ready[g]], "prep_dve")
                yield

            def spread(g, n):
                s = g % 2
                b_mm[g, n] = b.do("tensor", lambda e: e.matmul(pb[:, n % 2, :], const["spread"][:, n, :],
                    parts[:, s, 0, :], start=True, stop=True),
                    [split.get(g), scans.get((g, n - 2, 1)) if n >= 2 else scans.get((g - 1, D_STATE + n - 2, 1))], "bmm")
                c_mm[g, n] = spread_c[g] = b.do("tensor", lambda e: e.matmul(pc[:, :], const["spread"][:, n, :],
                    parts[:, s, 1, :], start=True, stop=True),
                    [c_ev.get((g, n - 1)) or c_ev.get((g - 1, D_STATE - 1))], "cmm")
                at = n % NCB
                before = (g, n - NCB, 1) if n >= NCB else (g - 1, D_STATE + n - NCB, 1)
                c_ev[g, n] = b.do("scalar", lambda e: e.copy(cb[:, at, :], pc[:, :]), [c_mm[g, n], prods.get(before)], "cev")
                for half in range(HALVES):
                    slot = (2 * n + half) % NDA
                    before = (g, n - NDA // 2, half) if n >= NDA // 2 else (g - 1, D_STATE + n - NDA // 2, half)
                    exps[g, n, half] = b.do("scalar", lambda e, half=half, slot=slot: e.activation(
                        da[:, slot, :], delta[:, s, half, :], ACT.Exp, scale=wts["a_neg"][:, half, n:n + 1]),
                        [delta_ready.get(g), scans.get(before)], "exp")

            def state(g, n):
                s = g % 2
                dst_of = [pd[:, :], pb[:, n % 2, :]]
                for half in range(HALVES):
                    db[half] = b.do("vector", lambda e, half=half: e.tensor_tensor(
                        dst_of[half], pb[:, n % 2, :], dx[:, s, half, :], ALU.mult),
                        [b_mm[g, n], dx_ready.get(g), scans.get((g, n - 1, 0) if n else (g - 1, D_STATE - 1, 0))], "v")
                for half in range(HALVES):
                    slot = (2 * n + half) % NDA
                    scans[g, n, half] = b.do("vector", lambda e, half=half, slot=slot: e.tensor_tensor_scan(
                        h[:, half, n, flow], da[:, slot, flow], dst_of[half][:, flow], h[:, half, n, last_token:last_token + 1],
                        ALU.mult, ALU.add), [db[half], exps[g, n, half], prods.get((g - 1, n, half))], "v")
                at = n % NCB
                for half in range(HALVES):
                    slot = (2 * n + half) % NP_
                    before = (g, n - NP_ // 2, half) if n >= NP_ // 2 else (g - 1, D_STATE + n - NP_ // 2, half)
                    prods[g, n, half] = b.do("gpsimd", lambda e, half=half, slot=slot: e.tensor_tensor(
                        prod[:, slot, :], h[:, half, n, :], cb[:, at, :], ALU.mult),
                        [scans[g, n, half], c_ev[g, n], sums.get(before)], "prod")

            def total(g, n):
                for half in range(HALVES):
                    slot = (2 * n + half) % NP_
                    def mm(e, half=half, slot=slot):
                        for j in range(SUBS):
                            out = py[:, j // 2, (j % 2) * D_INNER + half * P:(j % 2) * D_INNER + (half + 1) * P]
                            first = n == 0 and half == 0 and j % 2 == 0
                            last = e.matmul(out, prod[:, slot, j * P:(j + 1) * P], const["eye"][:, :], start=first,
                                            stop=(n == D_STATE - 1), is_transpose=True, skip_group_check=True)
                        return last
                    sums[g, n, half] = b.do("tensor", mm, [prods[g, n, half], y_ev.get(g - 1) if n == 0 else None], "sum")

            def load_before(g):
                for i in range(T // SIDE):
                    before_loads[g] = b.dma("sync", lambda e, i=i: e.dma_start(
                        yb[:, g % 2, i * JB:(i + 1) * JB, :], before[line(g, i)]), [before_used.get(g - 2)], f"before{g % 2}")

            def add_before(g):
                def mm(e):
                    for j in range(SUBS):
                        last = e.matmul(py[:, j // 2, (j % 2) * D_INNER:(j % 2 + 1) * D_INNER], const["eye"][:, :],
                                        yb[:, g % 2, j, :], start=False, stop=False, skip_group_check=True)
                    return last
                before_used[g] = b.do("tensor", mm, [before_loads[g]], "before")

            def skip(g):
                def mm(e):
                    for j in range(SUBS):
                        for half in range(HALVES):
                            out = py[:, j // 2, (j % 2) * D_INNER + half * P:(j % 2) * D_INNER + (half + 1) * P]
                            last = e.matmul(out, xc[:, g % 2, half, j * P:(j + 1) * P], wts["d_diag"][:, half, :],
                                            start=False, stop=False, skip_group_check=True)
                    return last
                xc_used[g] = b.do("tensor", mm, [], "sum")

            def store(g):
                for bank in range(2):
                    y_ev[g] = b.do("scalar", lambda e, bank=bank: e.copy(
                        yt[:, g % 2, 2 * bank:2 * bank + 2, :].rearrange("p j d -> p (j d)"), py[:, bank, :]),
                        [sums[g, D_STATE - 1, 1], stores.get(g - 2)], "yev")
                for i in range(T // SIDE):
                    stores[g] = b.dma("sync", lambda e, i=i: e.dma_start(
                        dst[line(g, i)], yt[:, g % 2, i * JB:(i + 1) * JB, :]), [y_ev[g]], f"store{g % 2}")

            if first:
                load(0)
                for _ in prepare(0):
                    pass
                b.run()
                return
            LAG = 2
            order = [(g, n) for g in range(PER_BODY) for n in range(D_STATE)]
            summed = iter(order)

            def sum_next():
                g, n = next(summed)
                total(g, n)
                if n == 0 and k == 0:
                    skip(g)
                if n == D_STATE // 2 and k:
                    add_before(g)
                if n == D_STATE - 1:
                    store(g)

            spread(0, 0)
            load(1)
            if k:
                load_before(0)
            for i, (g, n) in enumerate(order):
                more = g + 1 < PER_BODY or not last
                if n == 0:
                    steps = prepare(g + 1) if more else iter(())
                if n == 4 and (g + 2 < PER_BODY or (g + 2 == PER_BODY and not last)):
                    load(g + 2)
                if n == 4 and k and g + 1 < PER_BODY:
                    load_before(g + 1)
                if i + 1 < len(order):
                    spread(*order[i + 1])
                state(g, n)
                if i >= LAG:
                    sum_next()
                next(steps, None)
            for _ in range(LAG):
                sum_next()
            b.do("sync", lambda e: e.nop(), [stores[PER_BODY - 1], stores[PER_BODY - 2]])
            b.run()

        turns = turns_limit or TILES // PER_BODY
        one_turn(0, first=True)
        with nc.Fori(0, turns - 1) as it:
            one_turn(it)
        one_turn(turns - 1, last=True)


def output_phase(nc, sems, y, x1, out, wts, const, scale_col, shift_col):
    K = 8
    PER_BODY = 16
    LOADS = 3
    with ExitStack() as stack:
        m = Memory(nc, stack)
        yt = m.sb("o_y", [P, LOADS, K, D_INNER])
        xt = m.sb("o_x", [P, LOADS, K, C])
        st = m.sb("o_st", [P, 2, K, 6])
        mv = m.sb("o_mv", [P, 2, K, 2])
        std = m.sb("o_std", [P, 2, K])
        rstd = m.sb("o_rstd", [P, 2, K])
        nmr = m.sb("o_nmr", [P, 2, K])
        gn = m.sb("o_gn", [P, 2, BANK])
        zs = m.sb("o_zs", [P, 2, HALVES, BANK])
        yn = m.sb("o_yn", [P, 2, HALVES, BANK])
        ot = m.sb("o_ot", [P, 2, K, C])
        tp = m.ps("o_tp", [P, BANK])
        zp = m.ps("o_zp", [P, 2, BANK])
        yp = m.ps("o_yp", [P, 2, BANK])
        op = m.ps("o_op", [P, 2, BANK])
        view = lambda t: t.rearrange("(i q p j) c -> i q p j c", q=PER_BODY, j=K, p=P)
        ysrc, xsrc, dst = view(y), view(x1), view(out)
        flat = lambda v: v.rearrange("p j d -> p (j d)")
        with nc.Fori(0, TOKENS // (K * P * PER_BODY)) as it:
            b = Body(nc, sems)
            ynt, tev, zmm, zev, zmul, yev, omm, oev, stored, loaded, normed, ytr = ({} for _ in range(12))

            def load(q):
                s = q % LOADS
                ly = b.dma("sync", lambda e: e.dma_start(yt[:, s], ysrc[it, q]), [ynt.get(q - LOADS)], f"ly{s}")
                lx = b.dma("sync", lambda e: e.dma_start(xt[:, s], xsrc[it, q]), [oev.get((q - LOADS, 1))], f"lx{s}")
                loaded[q] = (ly, lx)

            def normalize(q):
                s, l = q % 2, q % LOADS
                for j in range(K):
                    s0 = b.do("vector", lambda e, j=j: e.bn_stats(st[:, s, j, :], yt[:, l, j, :]), [loaded[q][0]], "v")
                for j in range(K):
                    s1 = b.do("vector", lambda e, j=j: e.bn_aggr(mv[:, s, j, :], st[:, s, j, :]), [s0], "v")
                v0 = b.do("vector", lambda e: e.tensor_scalar(std[:, s], mv[:, s, :, 1], 1e-5, None, ALU.add), [s1], "v")
                q0 = b.do("scalar", lambda e: e.activation(std[:, s], std[:, s], ACT.Sqrt), [v0], "sqrt")
                v1 = b.do("vector", lambda e: e.reciprocal(rstd[:, s], std[:, s]), [q0], "v")
                v2 = b.do("vector", lambda e: e.scalar_tensor_tensor(
                    out=nmr[:, s], in0=mv[:, s, :, 0], scalar=-1.0, in1=rstd[:, s], op0=ALU.mult, op1=ALU.mult), [v1], "v")
                for j in range(K):
                    normed[q] = b.do("vector", lambda e, j=j: e.tensor_scalar(
                        yt[:, l, j, :], yt[:, l, j, :], rstd[:, s, j:j + 1], nmr[:, s, j:j + 1], ALU.mult, ALU.add),
                        [v2], "v")

            def inner(q, f):
                i, l = q * 2 + f, q % LOADS
                def tr(e):
                    for j in range(4):
                        last = e.transpose(tp[:, j * P:(j + 1) * P], xt[:, l, 4 * f + j, :], const["eye"][:, :])
                    return last
                t = b.do("tensor", tr, [loaded[q][1], tev.get(i - 1)], "t")
                tev[i] = b.do("scalar", lambda e: e.activation(gn[:, i % 2, :], tp[:, :], ACT.Identity,
                              bias=shift_col[:, 0:1], scale=scale_col[:, 0:1]), [t, zmm.get(i - 2)], "gn")

            def outer(q, f):
                i, s, l = q * 2 + f, q % 2, q % LOADS
                for half in range(HALVES):
                    def ty(e, half=half):
                        for j in range(4):
                            last = e.transpose(yp[:, half, j * P:(j + 1) * P], yt[:, l, 4 * f + j, half * P:(half + 1) * P],
                                               const["eye"][:, :])
                        return last
                    ytr[half] = ynt[q] = b.do("tensor", ty, [normed[q], yev.get((i - 1, half))], "t")
                for half in range(HALVES):
                    yev[i, half] = b.do("scalar", lambda e, half=half: e.activation(
                        yn[:, i % 2, half, :], yp[:, half, :], ACT.Identity, bias=wts["ln_b"][:, half:half + 1],
                        scale=wts["ln_w"][:, half:half + 1]), [ytr[half], omm.get(i - 2)], "yn")
                for half in range(HALVES):
                    t = zmm[i] = b.do("tensor", lambda e, half=half: e.matmul(
                        zp[:, half, :], wts["w_in"][:, D_INNER + half * P:D_INNER + (half + 1) * P], gn[:, i % 2, :],
                        start=True, stop=True), [tev[i], zev.get((i - 1, half))], "t")
                    zev[i, half] = b.do("scalar", lambda e, half=half: e.activation(
                        zs[:, i % 2, half, :], zp[:, half, :], ACT.Silu), [t, zmul.get((i - 2, half))], "z")
                for half in range(HALVES):
                    zmul[i, half] = b.do("gpsimd" if half else "vector", lambda e, half=half: e.tensor_tensor(
                        yn[:, i % 2, half, :], yn[:, i % 2, half, :], zs[:, i % 2, half, :], ALU.mult),
                        [yev[i, half], zev[i, half]], f"zmul{half}")

            def product(q, f):
                i, s, l = q * 2 + f, q % 2, q % LOADS
                def mo(e):
                    for j in range(4):
                        for half in range(HALVES):
                            last = e.matmul(op[:, i % 2, j * P:(j + 1) * P], yn[:, i % 2, half, j * P:(j + 1) * P],
                                            wts["w_out"][:, half, :], start=(half == 0), stop=(half == HALVES - 1))
                    return last
                t = omm[i] = b.do("tensor", mo, [zmul[i, 0], zmul[i, 1], oev.get((q - 1, f))], "t")
                oev[q, f] = b.do("vector", lambda e: e.tensor_tensor(
                    flat(ot[:, s, 4 * f:4 * f + 4]), op[:, i % 2, :], flat(xt[:, l, 4 * f:4 * f + 4]), ALU.add),
                    [t, stored.get(q - 2)], "oev")
                if f == 1:
                    stored[q] = b.dma("sync", lambda e: e.dma_start(dst[it, q], ot[:, s]), [oev[q, 1]], f"store{s}")

            N = PER_BODY
            groups = [(q, f) for q in range(N) for f in range(2)]
            for q in range(LOADS - 1):
                load(q)
            normalize(0)
            inner(0, 0)
            for i, (q, f) in enumerate(groups):
                if f == 0 and q + 2 < N and q >= 1:
                    load(q + 1)
                if f == 0 and q + 1 < N:
                    if q + 1 >= 2 and q + 1 not in loaded:
                        load(q + 1)
                    normalize(q + 1)
                if i + 1 < len(groups):
                    inner(*groups[i + 1])
                outer(q, f)
                if i >= 1:
                    product(*groups[i - 1])
            product(*groups[-1])
            b.do("sync", lambda e: e.nop(), [stored[N - 1], stored[N - 2]])
            b.run()


_WEIGHTS = {
    "ln_scale": (P, 1), "ln_bias": (P, 1), "Wq": (C, C), "Wk": (C, C), "Wvg": (C, 2 * C), "Wb": (C, HEADS), "Wo": (C, C),
    "w_in": (C, 2 * D_INNER), "conv_w": (P, HALVES, 9), "conv_b": (P, HALVES),
    "proj_b": (DIRECTIONS, P, HALVES, 96 + DT_RANK), "proj_c": (DIRECTIONS, P, HALVES, 96),
    "dt_w": (DIRECTIONS, DT_RANK, D_INNER), "dt_b": (DIRECTIONS, P, HALVES), "A_logs": (DIRECTIONS, P, HALVES, D_STATE),
    "Ds": (P, HALVES, DIRECTIONS), "ln_w": (P, HALVES), "ln_b": (P, HALVES), "w_out": (P, HALVES, C),
}


def build(nc, x, dram, out, eye, mean, group_of, spread, phases="0123456789", outputs=None, scan_turns=None):
    f = lambda name, shape: (outputs or {}).get(name) or nc.dram_tensor(name, shape, F32).ap()
    zn_t = f("zn_t", (SIDE // 8, C, 8 * SIDE))
    bias_d = f("bias_d", (HEADS, TOKENS))
    x1 = f("x1", (TOKENS, C))
    xc_tok = f("xc_tok", (TOKENS, D_INNER))
    ys = [f(f"y{k}", (TOKENS, D_INNER)) for k in range(DIRECTIONS)]
    with ExitStack() as stack:
        m = Memory(nc, stack)
        sems = [stack.enter_context(nc.semaphore(f"s{i}")) for i in range(40)]
        assert all(b.num == a.num + 1 for a, b in zip(sems, sems[1:]))
        const = {"eye": m.sb("eye", [P, P]), "mean": m.sb("mean", [P, P]), "group_of": m.sb("group_of", [P, GROUPS]),
                 "spread": m.sb("spread", [96, D_STATE, P], BF16)}
        spread32 = m.sb("spread32", [96, D_STATE, P])
        scale_row, shift_row = m.sb("scale_row", [P, GROUPS]), m.sb("shift_row", [P, GROUPS])
        scale_col, shift_col = m.sb("scale_col", [P, 1]), m.sb("shift_col", [P, 1])
        per_direction = ("proj_b", "proj_c", "dt_w", "dt_b", "A_logs")
        wts = {}
        for name, shape in _WEIGHTS.items():
            if name in per_direction:
                wts[name] = [m.sb(f"w_{name}{k}", list(shape[1:])) for k in range(DIRECTIONS)]
            else:
                wts[name] = m.sb(f"w_{name}", list(shape))
        whole = lambda t: t[tuple(slice(None) for _ in t.shape)]
        wts["a_neg"] = [m.sb(f"a_neg{k}", [P, HALVES, D_STATE]) for k in range(DIRECTIONS)]
        wts["guard_less_dt_b"] = [m.sb(f"gdt{k}", [P, HALVES]) for k in range(DIRECTIONS)]
        guard = m.sb("guard", [P, 1])
        d_sum, d_diag = m.sb("d_sum", [P, HALVES]), m.sb("d_diag", [P, HALVES, P])

        b = Body(nc, sems)
        for tile, source in ((const["eye"], eye), (const["mean"], mean), (const["group_of"], group_of), (spread32, spread)):
            ld = b.dma("sync", lambda e, tile=tile, source=source: e.dma_start(whole(tile), source), [], "load")
        for name in _WEIGHTS:
            tiles = wts[name] if name in per_direction else [wts[name]]
            for k, tile in enumerate(tiles):
                source = dram[name][k] if name in per_direction else dram[name]
                ld = b.dma("sync", lambda e, tile=tile, source=source: e.dma_start(whole(tile), source), [], "load")
        b.do("vector", lambda e: e.memset(guard[:, :], 20.0))
        b.do("vector", lambda e: e.tensor_copy(const["spread"][:, :, :], spread32[:, :, :]), [ld])
        ds = b.do("vector", lambda e: e.tensor_reduce(d_sum[:, :], wts["Ds"][:, :, :], AX_X, ALU.add), [ld], "v")
        for half in range(HALVES):
            b.do("vector", lambda e, half=half: e.tensor_scalar(d_diag[:, half, :], const["eye"][:, :], d_sum[:, half:half + 1],
                 None, ALU.mult), [ds])
        for k in range(DIRECTIONS):
            b.do("vector", lambda e, k=k: e.tensor_scalar(wts["guard_less_dt_b"][k][:, :], wts["dt_b"][k][:, :], -1.0, 20.0,
                 ALU.mult, ALU.add), [ld])
            ex = b.do("scalar", lambda e, k=k: e.activation(wts["a_neg"][k][:, :, :], wts["A_logs"][k][:, :, :], ACT.Exp), [ld], "a")
            b.do("vector", lambda e, k=k: e.tensor_scalar(wts["a_neg"][k][:, :, :], wts["a_neg"][k][:, :, :], -1.0, None,
                 ALU.mult), [ex])
        b.run()

        if "0" in phases:
            group_stats(nc, sems, "g0", x, 1e-5, const, scale_row, shift_row)
        if "1" in phases:
            norm_phase(nc, sems, x, zn_t, bias_d, wts, const, scale_row, shift_row)
        if "2" in phases:
            attention_phase(nc, sems, x, zn_t, bias_d, x1, wts, const)
        if "3" in phases:
            group_stats(nc, sems, "g1", x1, 1e-5, const, scale_row, shift_row, (scale_col, shift_col))
        if "4" in phases:
            conv_phase(nc, sems, x1, xc_tok, wts, const, scale_col, shift_col)
        for k in range(DIRECTIONS):
            if str(5 + k) in phases:
                own = {n: wts[n][k] for n in per_direction + ("a_neg", "guard_less_dt_b")}
                scan_phase(nc, sems, k, xc_tok, ys[k - 1] if k else None, ys[k], {**wts, **own, "guard": guard, "d_diag": d_diag}, const, scan_turns)
        if "9" in phases:
            output_phase(nc, sems, ys[-1], x1, out, wts, const, scale_col, shift_col)


def laid_out(w):
    halves = lambda a: np.ascontiguousarray(np.moveaxis(a.reshape((HALVES, P) + a.shape[1:]), 0, 1))
    xp = w["L1_conv_x_proj_w"]
    proj_b = np.zeros((DIRECTIONS, D_INNER, 96 + DT_RANK), np.float32)
    proj_c = np.zeros((DIRECTIONS, D_INNER, 96), np.float32)
    for k in range(DIRECTIONS):
        for at in (0, 32, 64):
            proj_b[k, :, at:at + D_STATE] = xp[k, DT_RANK:DT_RANK + D_STATE].T
            proj_c[k, :, at:at + D_STATE] = xp[k, DT_RANK + D_STATE:].T
        proj_b[k, :, 96:] = xp[k, :DT_RANK].T
    each = lambda a: np.stack([halves(a[k]) for k in range(DIRECTIONS)])
    return {
        "ln_scale": w["L0_conv_ln_scale"].reshape(P, 1), "ln_bias": w["L0_conv_ln_bias"].reshape(P, 1),
        "Wq": w["L0_conv_Wq"], "Wk": w["L0_conv_Wk"], "Wvg": np.concatenate([w["L0_conv_Wv"], w["L0_conv_Wg"]], 1),
        "Wb": w["L0_conv_Wb"], "Wo": w["L0_conv_Wo"], "w_in": w["L1_conv_w_in"].T,
        "conv_w": halves(w["L1_conv_conv_w"].reshape(D_INNER, 9)), "conv_b": halves(w["L1_conv_conv_b"]),
        "proj_b": each(proj_b), "proj_c": each(proj_c), "dt_w": np.moveaxis(w["L1_conv_dt_w"], 1, 2),
        "dt_b": each(w["L1_conv_dt_b"]), "A_logs": each(w["L1_conv_A_logs"].reshape(DIRECTIONS, D_INNER, D_STATE)),
        "Ds": halves(w["L1_conv_Ds"].reshape(DIRECTIONS, D_INNER).T), "ln_w": halves(w["L1_conv_ln_w"]),
        "ln_b": halves(w["L1_conv_ln_b"]), "w_out": halves(w["L1_conv_w_out"].T),
    }


def constants():
    spread = np.zeros((96, D_STATE, P), np.float32)
    for n in range(D_STATE):
        for at in (0, 32, 64):
            spread[at + n, n, :] = 1.0
    return {"eye": np.eye(P, dtype=np.float32), "mean": np.full((P, P), 1.0 / P, np.float32),
            "group_of": np.repeat(np.eye(GROUPS, dtype=np.float32), PER_GROUP, axis=0), "spread": spread}


def kernel(**inputs):
    import concourse.bacc as bacc
    from concourse.bass_utils import run_bass_kernel_spmd

    w = {n: np.asarray(a) for n, a in inputs.items()}
    arrays = {"x": np.ascontiguousarray(w["x"]).reshape(TOKENS, C)}
    arrays.update({n: np.ascontiguousarray(a) for n, a in laid_out(w).items()})
    arrays.update(constants())
    nc = bacc.Bacc("TRN2", target_bir_lowering=False, num_devices=1)
    dram = {n: nc.dram_tensor(f"in_{n}", a.shape, F32, kind="ExternalInput").ap() for n, a in arrays.items()}
    out = nc.dram_tensor("out", (TOKENS, C), F32, kind="ExternalOutput").ap()
    build(nc, dram["x"], dram, out, dram["eye"], dram["mean"], dram["group_of"], dram["spread"])
    r = run_bass_kernel_spmd(nc, [{f"in_{n}": a for n, a in arrays.items()}], core_ids=[0])
    return r.results[0]["out"].reshape(1, SIDE, SIDE, C)
```

```python
from contextlib import ExitStack

import numpy as np
import concourse.bass as bass
from concourse import mybir

F32 = mybir.dt.float32
BF16 = mybir.dt.bfloat16
ALU = mybir.AluOpType
ACT = mybir.ActivationFunctionType
AX_X = mybir.AxisListType.X

P = 128
SIDE = 256
TOKENS = SIDE * SIDE
C = 128
GROUPS = 32
PER_GROUP = C // GROUPS
HEADS, HEAD_DIM = 4, 32
JB = SIDE // P
D_INNER = 256
HALVES = D_INNER // P
D_STATE = 16
DT_RANK = 8
DIRECTIONS = 4
BANK = 512

ENGINES = ("tensor", "vector", "scalar", "gpsimd", "sync")


class Body:

    def __init__(self, nc, semaphores):
        self.nc, self.semaphores = nc, semaphores
        self.named, self.counts, self.owner = {}, {}, {}
        self.queues = {e: [] for e in ENGINES}

    def do(self, engine, issue, after=(), signal=None):
        mark, step = None, 1
        if signal is not None:
            if signal not in self.named:
                self.named[signal] = self.semaphores[len(self.named)]
                self.counts[signal], self.owner[signal] = 0, engine
            assert self.owner[signal] == engine
            self.counts[signal] += 1
            mark = (signal, self.counts[signal])
        self.queues[engine].append((issue, [m for m in after if m], signal, step))
        return mark

    def dma(self, engine, issue, after=(), signal=None):
        mark = self.do(engine, issue, after, signal)
        queue = self.queues[engine]
        queue[-1] = queue[-1][:3] + (16,)
        return (mark[0], mark[1] * 16)

    def run(self):
        nc = self.nc
        with nc.Block() as block:
            for name in ENGINES:
                def program(engine, queue=self.queues[name]):
                    for issue, after, signal, step in queue:
                        for what, count in after:
                            engine.wait_ge(self.named[what], count)
                        last = issue(engine)
                        if signal is not None:
                            last.then_inc(self.named[signal], step)
                start = {"tensor": block.tensor, "vector": block.vector, "scalar": block.scalar,
                         "gpsimd": block.gpsimd, "sync": block.sync}
                start[name](program)
        first = self.semaphores[0].num
        nc.vector.sem_clear(range(first, first + len(self.semaphores)))
        nc.all_engine_barrier()


class Memory:

    def __init__(self, nc, stack):
        self.nc, self.stack = nc, stack

    def sb(self, name, shape, dtype=F32):
        return self.stack.enter_context(self.nc.sbuf_tensor(name, shape, dtype))

    def ps(self, name, shape, dtype=F32):
        return self.stack.enter_context(self.nc.psum_tensor(name, shape, dtype))


def group_stats(nc, sems, name, x, eps, const, scale_row, shift_row, columns=None):
    CHUNK = BANK // PER_GROUP
    per_part = TOKENS // P
    chunks = per_part // CHUNK
    with ExitStack() as stack:
        m = Memory(nc, stack)
        xt = m.sb(f"{name}_x", [P, 2, CHUNK, C])
        st = m.sb(f"{name}_st", [P, GROUPS, chunks, 6])
        mv = m.sb(f"{name}_mv", [P, GROUPS, 2])
        avg = m.sb(f"{name}_avg", [P, GROUPS, 2])
        dev = m.sb(f"{name}_dev", [P, GROUPS])
        var = m.sb(f"{name}_var", [P, GROUPS])
        std = m.sb(f"{name}_std", [P, GROUPS])
        pick = m.sb(f"{name}_pick", [P, 2, GROUPS])
        total = m.ps(f"{name}_total", [P, 2, BANK])
        src = x.rearrange("(p j k) c -> j p k c", p=P, k=CHUNK)
        b = Body(nc, sems)
        stats = [None] * chunks
        for j in range(chunks):
            loaded = b.dma("sync", lambda e, j=j: e.dma_start(xt[:, j % 2], src[j]),
                           [stats[j - 2] if j >= 2 else None], f"load{j % 2}")
            for g in range(GROUPS):
                stats[j] = b.do("vector", lambda e, j=j, g=g: e.bn_stats(
                    st[:, g, j, :], xt[:, j % 2, :, g * PER_GROUP:(g + 1) * PER_GROUP]), [loaded], "stats")
        for g in range(GROUPS):
            aggr = b.do("vector", lambda e, g=g: e.bn_aggr(mv[:, g, :], st[:, g]), [stats[-1]], "aggr")
        t0 = b.do("tensor", lambda e: e.matmul(total[:, 0, 0:2 * GROUPS], const["mean"][:, :],
                  mv[:, :, :].rearrange("p g s -> p (g s)"), start=True, stop=True), [aggr], "t")
        a0 = b.do("vector", lambda e: e.tensor_copy(avg[:, :, :].rearrange("p g s -> p (g s)"),
                  total[:, 0, 0:2 * GROUPS]), [t0], "v")
        d0 = b.do("vector", lambda e: e.tensor_tensor(dev[:, :], mv[:, :, 0], avg[:, :, 0], ALU.subtract), [a0], "v")
        d1 = b.do("vector", lambda e: e.tensor_tensor(dev[:, :], dev[:, :], dev[:, :], ALU.mult), [d0], "v")
        t1 = b.do("tensor", lambda e: e.matmul(total[:, 1, 0:GROUPS], const["mean"][:, :], dev[:, :],
                  start=True, stop=True), [d1], "t")
        v0 = b.do("vector", lambda e: e.tensor_tensor(var[:, :], avg[:, :, 1], total[:, 1, 0:GROUPS], ALU.add), [t1], "v")
        v1 = b.do("vector", lambda e: e.tensor_scalar(var[:, :], var[:, :], eps, None, ALU.add), [v0], "v")
        s0 = b.do("scalar", lambda e: e.activation(std[:, :], var[:, :], ACT.Sqrt), [v1], "s")
        r0 = b.do("vector", lambda e: e.reciprocal(scale_row[:, :], std[:, :]), [s0], "v")
        r1 = b.do("vector", lambda e: e.scalar_tensor_tensor(out=shift_row[:, :], in0=avg[:, :, 0], scalar=-1.0,
                  in1=scale_row[:, :], op0=ALU.mult, op1=ALU.mult), [r0], "v")
        if columns:
            for i, (row, column) in enumerate(zip((scale_row, shift_row), columns)):
                p0 = b.do("vector", lambda e, i=i, row=row: e.tensor_tensor(
                    pick[:, i, :], row[:, :], const["group_of"][:, :], ALU.mult), [r1], "v")
                b.do("vector", lambda e, i=i, column=column: e.tensor_reduce(
                    column[:, 0:1], pick[:, i, :], AX_X, ALU.add), [p0], "v")
        b.run()


def norm_phase(nc, sems, x, zn_t, bias_d, wts, const, scale_row, shift_row):
    ROWS = 8
    CT = ROWS * SIDE
    BLOCKS = CT // P
    PER_BODY = 8
    with ExitStack() as stack:
        m = Memory(nc, stack)
        xt = m.sb("n_x", [P, 2, BLOCKS, C])
        gt = m.sb("n_g", [P, 2, BLOCKS, C])
        st = m.sb("n_st", [P, 2, BLOCKS, 6])
        mv = m.sb("n_mv", [P, 2, BLOCKS, 2])
        std = m.sb("n_std", [P, 2, BLOCKS])
        rstd = m.sb("n_rstd", [P, 2, BLOCKS])
        nmr = m.sb("n_nmr", [P, 2, BLOCKS])
        zt = m.sb("n_zt", [P, 2, CT])
        bt = m.sb("n_bt", [HEADS, 2, CT])
        tp = m.ps("n_tp", [P, 4, BANK])
        bp = m.ps("n_bp", [P, 2, BANK])
        src = x.rearrange("(i q b p) c -> i q p b c", q=PER_BODY, b=BLOCKS, p=P)
        dst = zn_t.rearrange("(i q) c t -> i q c t", q=PER_BODY)
        bdst = bias_d.rearrange("h (i q t) -> i q h t", q=PER_BODY, t=CT)
        four = lambda v: v.rearrange("p b (g c) -> p b g c", c=PER_GROUP)
        row = lambda v: v[:, :].unsqueeze(1).unsqueeze(3).to_broadcast([P, BLOCKS, GROUPS, PER_GROUP])
        with nc.Fori(0, TOKENS // (CT * PER_BODY)) as it:
            b = Body(nc, sems)
            turned, evac, bevac, stored, bstored, loaded, normed, pb = ({} for _ in range(8))

            def load(q):
                s = q % 2
                for half in (slice(0, BLOCKS // 2), slice(BLOCKS // 2, BLOCKS)):
                    loaded[q] = b.dma("sync", lambda e, half=half: e.dma_start(xt[:, s, half], src[it, q, :, half]),
                                      [turned.get(q - 2)], f"load{s}")

            def normalize(q):
                s = q % 2
                g0 = b.do("vector", lambda e: e.tensor_tensor(four(gt[:, s]), four(xt[:, s]), row(scale_row),
                          ALU.mult), [loaded[q], turned.get(q - 2)], "v")
                g1 = b.do("vector", lambda e: e.tensor_tensor(four(gt[:, s]), four(gt[:, s]), row(shift_row),
                          ALU.add), [g0], "v")
                for j in range(BLOCKS):
                    s0 = b.do("vector", lambda e, j=j: e.bn_stats(st[:, s, j, :], gt[:, s, j, :]), [g1], "v")
                for j in range(BLOCKS):
                    s1 = b.do("vector", lambda e, j=j: e.bn_aggr(mv[:, s, j, :], st[:, s, j, :]), [s0], "v")
                v0 = b.do("vector", lambda e: e.tensor_scalar(std[:, s], mv[:, s, :, 1], 1e-5, None, ALU.add), [s1], "v")
                q0 = b.do("scalar", lambda e: e.activation(std[:, s], std[:, s], ACT.Sqrt), [v0], "s")
                v1 = b.do("vector", lambda e: e.reciprocal(rstd[:, s], std[:, s]), [q0], "v")
                v2 = b.do("vector", lambda e: e.scalar_tensor_tensor(
                    out=nmr[:, s], in0=mv[:, s, :, 0], scalar=-1.0, in1=rstd[:, s], op0=ALU.mult, op1=ALU.mult), [v1], "v")
                for j in range(BLOCKS):
                    normed[q] = b.do("vector", lambda e, j=j: e.tensor_scalar(
                        gt[:, s, j, :], gt[:, s, j, :], rstd[:, s, j:j + 1], nmr[:, s, j:j + 1], ALU.mult, ALU.add),
                        [v2], "v")

            def turn(q, f):
                k, s = q * 4 + f, q % 2
                def tr(e):
                    for j in range(4):
                        last = e.transpose(tp[:, f, j * P:(j + 1) * P], gt[:, s, 4 * f + j, :], const["eye"][:, :])
                    return last
                turned[q] = b.do("tensor", tr, [normed[q], evac.get(k - 4)], "turn")
                evac[k] = b.do("scalar", lambda e: e.activation(
                    zt[:, s, f * BANK:(f + 1) * BANK], tp[:, f, :], ACT.Identity, bias=wts["ln_bias"][:, 0:1],
                    scale=wts["ln_scale"][:, 0:1]), [turned[q], stored.get(q - 2)], "evac")

            def pair_bias(q, f):
                k, s = q * 4 + f, q % 2
                t = b.do("tensor", lambda e: e.matmul(
                    bp[0:HEADS, f % 2, :], wts["Wb"][:, :], zt[:, s, f * BANK:(f + 1) * BANK], start=True, stop=True),
                    [evac[k], bevac.get(k - 2)], "pb")
                bevac[k] = b.do("scalar", lambda e: e.copy(
                    bt[:, s, f * BANK:(f + 1) * BANK], bp[0:HEADS, f % 2, :]), [t, bstored.get(q - 2)], "bevac")

            N = PER_BODY
            load(0)
            load(1)
            normalize(0)
            for q in range(N):
                s = q % 2
                for f in range(4):
                    turn(q, f)
                if q + 2 < N:
                    load(q + 2)
                for f in range(4):
                    pair_bias(q, f)
                if q + 1 < N:
                    normalize(q + 1)
                stored[q] = b.dma("sync", lambda e, q=q, s=s: e.dma_start(dst[it, q], zt[:, s]), [evac[4 * q + 3]], f"st{s}")
                bstored[q] = b.dma("sync", lambda e, q=q, s=s: e.dma_start(bdst[it, q], bt[:, s]), [bevac[4 * q + 3]], f"bst{s}")
            b.do("sync", lambda e: e.nop(), [stored[N - 1], stored[N - 2], bstored[N - 1], bstored[N - 2]])
            b.run()


def attention_phase(nc, sems, x, zn_t, bias_d, x1, wts, const):
    ROWS = 128
    CHUNK = zn_t.shape[2] // SIDE
    SLOTS = 4
    SCALE = float(HEAD_DIM) ** -0.5
    V1 = HEAD_DIM + 1
    with ExitStack() as stack:
        m = Memory(nc, stack)
        zt = m.sb("a_zt", [P, SLOTS * CHUNK, SIDE])
        xt = m.sb("a_xt", [P, SLOTS * CHUNK, JB, C])
        bias = m.sb("a_bias", [P, JB, HEADS, SIDE])
        qk = m.sb("a_qk", [P, 2, 2, SIDE])
        v1 = m.sb("a_v1", [P, 4, JB, HEADS, V1])
        gate = m.sb("a_gate", [P, 4, JB, C])
        sc = m.sb("a_sc", [P, 3, HEADS, JB, SIDE])
        top = m.sb("a_top", [P, 3, HEADS, JB])
        ntop = m.sb("a_ntop", [P, 3, HEADS, JB])
        pt = m.sb("a_pt", [P, 2, HEADS, JB, SIDE])
        den = m.sb("a_den", [P, 2, JB, HEADS])
        rden = m.sb("a_rden", [P, 2, JB, HEADS])
        go = m.sb("a_go", [P, 2, JB, C])
        gt = m.sb("a_gt", [P, 2, SIDE])
        scores = m.ps("a_scores", [P, HEADS, BANK])
        proj = m.ps("a_proj", [P, BANK])
        turn = m.ps("a_turn", [P, 2, BANK])
        mix = m.ps("a_mix", [P, BANK])
        xsrc = x.rearrange("(i r b p) c -> i p r b c", r=ROWS, b=JB, p=P)
        xdst = x1.rearrange("(i r b p) c -> i p r b c", r=ROWS, b=JB, p=P)
        zsrc = zn_t.rearrange("(i q) c (r t) -> i q c r t", q=ROWS // CHUNK, t=SIDE)

        b = Body(nc, sems)
        bsrc = bias_d.rearrange("h (b j k) -> b j h k", b=JB, j=P)
        for jb in range(JB):
            ld = b.dma("sync", lambda e, jb=jb: e.dma_start(bias[:, jb], bsrc[jb]), [], "bias")
        b.do("sync", lambda e: e.nop(), [ld])
        b.do("vector", lambda e: e.memset(v1[:, :, :, :, :].rearrange("p s b h v -> p (s b h v)"), 1.0))
        b.run()

        with nc.Fori(0, SIDE // ROWS) as it:
            b = Body(nc, sems)
            N = ROWS
            zl, xl, stores, z_used = {}, {}, {}, {}
            at = lambda r: r % (SLOTS * CHUNK)

            def load(q):
                slot, first = q % SLOTS, q % SLOTS * CHUNK
                zl[q] = b.dma("sync", lambda e: e.dma_start(zt[:, first:first + CHUNK], zsrc[it, q]),
                              [z_used.get(q - SLOTS)], f"loadz{slot}")
                for part in range(2):
                    here, there = first + part * CHUNK // 2, q * CHUNK + part * CHUNK // 2
                    xl[q] = b.dma("sync", lambda e, here=here, there=there: e.dma_start(
                        xt[:, here:here + CHUNK // 2], xsrc[it, :, there:there + CHUNK // 2]),
                        [stores.get(q - SLOTS)], f"loadx{slot}")

            for q in range(SLOTS):
                load(q)
            qk_ev, v_ev, exps, t_last, t_ev, pv, gated, gt_ev, y_mm, y_ev, s_mm, s_ev, neg = ({} for _ in range(13))

            def project(r):
                def qk_mm(e):
                    e.matmul(proj[:, 0:SIDE], wts["Wq"][:, :], zt[:, at(r), :], start=True, stop=True)
                    return e.matmul(proj[:, SIDE:], wts["Wk"][:, :], zt[:, at(r), :], start=True, stop=True)
                t = b.do("tensor", qk_mm, [zl[r // CHUNK], v_ev.get(r - 1)], "proj")
                qk_ev[r] = b.do("scalar", lambda e: e.copy(
                    qk[:, r % 2].rearrange("p a t -> p (a t)"), proj[:, :]), [t, s_mm.get(r - 2)], "qkev")

            def values(r):
                def vg_mm(e):
                    for jb in range(JB):
                        last = e.matmul(proj[:, jb * SIDE:(jb + 1) * SIDE], zt[:, at(r), jb * P:(jb + 1) * P],
                                        wts["Wvg"][:, :], start=True, stop=True)
                    return last
                t = z_used[r // CHUNK] = b.do("tensor", vg_mm, [qk_ev[r]], "proj")
                pv_view = proj[:, :].rearrange("p (b a n) -> p b a n", b=JB, a=2)
                tan = b.do("scalar", lambda e: e.activation(gate[:, r % 4], pv_view[:, :, 1, :], ACT.Tanh, scale=0.5),
                           [t, gated.get(r - 4)], "gate")
                v_ev[r] = b.do("vector", lambda e: e.tensor_copy(
                    v1[:, r % 4, :, :, 0:HEAD_DIM], pv_view[:, :, 0, :].rearrange("p b (h d) -> p b h d", h=HEADS)),
                    [tan, pv.get(r - 4)], "vev")

            def score(r, h):
                def mm(e):
                    rows = slice(h * HEAD_DIM, (h + 1) * HEAD_DIM)
                    for jb in range(JB):
                        last = e.matmul(scores[:, h, jb * SIDE:(jb + 1) * SIDE],
                                        qk[rows, r % 2, 0, jb * P:(jb + 1) * P], qk[rows, r % 2, 1, :],
                                        start=True, stop=True)
                    return last
                s_mm[r] = t = b.do("tensor", mm, [qk_ev[r], s_ev.get((r - 1, h))], "score")
                s_ev[r, h] = b.do("vector", lambda e, h=h: e.scalar_tensor_tensor(
                    out=sc[:, r % 3, h, :, :], in0=scores[:, h, :].rearrange("p (b k) -> p b k", b=JB), scalar=SCALE,
                    in1=bias[:, :, h, :], op0=ALU.mult, op1=ALU.add), [t, t_last.get(r - 3)], "sev")

            def maximum(r):
                mx = b.do("vector", lambda e: e.tensor_reduce(
                    top[:, r % 3], sc[:, r % 3], AX_X, ALU.max), [s_ev[r, HEADS - 1]], "v")
                neg[r] = b.do("vector", lambda e: e.tensor_scalar(ntop[:, r % 3], top[:, r % 3], -1.0, None, ALU.mult),
                              [mx, exps.get((r - 3, HEADS - 1))], "v")

            def exponentials(r):
                for h in range(HEADS):
                    def ex(e, h=h):
                        for jb in range(JB):
                            last = e.activation(sc[:, r % 3, h, jb, :], sc[:, r % 3, h, jb, :], ACT.Exp,
                                                bias=ntop[:, r % 3, h, jb:jb + 1])
                        return last
                    exps[r, h] = b.do("scalar", ex, [neg[r]], "exp")

            def turn_weights(r, heads):
                for h in heads:
                    def tr(e, h=h):
                        for kb in range(JB):
                            for jb in range(JB):
                                last = e.transpose(turn[:, h % 2, kb * SIDE + jb * P:kb * SIDE + (jb + 1) * P],
                                                   sc[:, r % 3, h, jb, kb * P:(kb + 1) * P], const["eye"][:, :])
                        return last
                    t_last[r] = t = b.do("tensor", tr, [exps[r, h], t_ev.get((r, h - 2)), t_ev.get((r - 1, h + 2))], "turn")
                    who = "scalar" if h % 2 else "vector"
                    def ev(e, h=h):
                        dst, src = pt[:, r % 2, h].rearrange("p b k -> p (b k)"), turn[:, h % 2, :]
                        return e.copy(dst, src) if h % 2 else e.tensor_copy(dst, src)
                    t_ev[r, h] = b.do(who, ev, [t, pv.get(r - 2)], f"tev{h % 2}")

            def mix_values(r, h):
                def mm(e):
                    for jb in range(JB):
                        for kb in range(JB):
                            to = (jb * HEADS + h) * V1
                            last = e.matmul(mix[:, to:to + V1], pt[:, r % 2, h, kb, jb * P:(jb + 1) * P],
                                            v1[:, r % 4, kb, h, :], start=(kb == 0), stop=(kb == JB - 1))
                    return last
                pv[r] = b.do("tensor", mm, [t_ev[r, h], v_ev[r], y_ev.get(r - 1)], "pv")

            def weigh_out(r):
                o = mix[:, 0:JB * HEADS * V1].rearrange("p (b h v) -> p b h v", b=JB, h=HEADS)
                d0 = b.do("vector", lambda e: e.tensor_scalar(den[:, r % 2], o[:, :, :, HEAD_DIM], 2.0, None, ALU.mult), [pv[r]], "v")
                g0 = b.do("vector", lambda e: e.scalar_tensor_tensor(
                    out=go[:, r % 2].rearrange("p b (h d) -> p b h d", h=HEADS),
                    in0=gate[:, r % 4].rearrange("p b (h d) -> p b h d", h=HEADS), scalar=1.0,
                    in1=o[:, :, :, 0:HEAD_DIM], op0=ALU.add, op1=ALU.mult), [pv[r], gt_ev.get(r - 2)], "v")
                d1 = b.do("vector", lambda e: e.reciprocal(rden[:, r % 2], den[:, r % 2]), [d0], "v")
                gated[r] = b.do("vector", lambda e: e.tensor_tensor(
                    go[:, r % 2].rearrange("p b (h d) -> p b h d", h=HEADS),
                    go[:, r % 2].rearrange("p b (h d) -> p b h d", h=HEADS),
                    rden[:, r % 2].unsqueeze(3).broadcast_to([P, JB, HEADS, HEAD_DIM]), ALU.mult), [g0, d1], "v")

            def gate_turn(r):
                def tr(e):
                    for jb in range(JB):
                        last = e.transpose(mix[:, jb * P:(jb + 1) * P], go[:, r % 2, jb, :], const["eye"][:, :])
                    return last
                t = b.do("tensor", tr, [gated[r]], "mix")
                gt_ev[r] = b.do("scalar", lambda e: e.copy(gt[:, r % 2, :], mix[:, 0:SIDE]), [t, y_mm.get(r - 2)], "gtev")

            def output(r):
                def mm(e):
                    for jb in range(JB):
                        last = e.matmul(mix[:, SIDE + jb * P:SIDE + (jb + 1) * P], gt[:, r % 2, jb * P:(jb + 1) * P],
                                        wts["Wo"][:, :], start=True, stop=True)
                    return last
                y_mm[r] = b.do("tensor", mm, [gt_ev[r]], "ymm")
                y_ev[r] = b.do("vector", lambda e: e.tensor_tensor(
                    xt[:, at(r)].rearrange("p b c -> p (b c)"), mix[:, SIDE:2 * SIDE],
                    xt[:, at(r)].rearrange("p b c -> p (b c)"), ALU.add), [y_mm[r], xl[r // CHUNK]], "yev")

            for r in range(-3, N + 1):
                if 0 <= r < N:
                    turn_weights(r, (0, 1))
                if 0 <= r - 1:
                    gate_turn(r - 1)
                if 0 <= r + 2 < N:
                    score(r + 2, 0)
                if 0 <= r < N:
                    turn_weights(r, (2, 3))
                if 0 <= r - 1:
                    output(r - 1)
                    if r % CHUNK == 0:
                        q = r // CHUNK - 1
                        here, rows = q % SLOTS * CHUNK, slice(r - CHUNK, r)
                        stores[q] = b.dma("sync", lambda e, here=here, rows=rows: e.dma_start(
                            xdst[it, :, rows], xt[:, here:here + CHUNK]), [y_ev[r - 1]], f"store{q % SLOTS}")
                        if q + SLOTS < N // CHUNK:
                            load(q + SLOTS)
                if 0 <= r + 2 < N:
                    score(r + 2, 1)
                if 0 <= r + 1 < N:
                    exponentials(r + 1)
                if 0 <= r + 2 < N:
                    score(r + 2, 2)
                if r + 3 < N:
                    project(r + 3)
                if 0 <= r + 2 < N:
                    score(r + 2, 3)
                    maximum(r + 2)
                if 0 <= r < N:
                    for h in range(HEADS):
                        mix_values(r, h)
                    weigh_out(r)
                if r + 3 < N:
                    values(r + 3)
            b.do("sync", lambda e: e.nop(), [stores[q] for q in range(N // CHUNK - SLOTS, N // CHUNK)])
            b.run()


def conv_phase(nc, sems, x1, xc_tok, wts, const, scale_col, shift_col):
    ROWS = 32
    RING = 16
    PAIR = 2
    STRIP = 4
    WIDE = SIDE + 2
    PAIRS, STRIPS = ROWS // PAIR, ROWS // STRIP
    SHARED = (0, 2, 4, 6)
    with ExitStack() as stack:
        m = Memory(nc, stack)
        xt = m.sb("c_xt", [P, RING, JB, C])
        gn = m.sb("c_gn", [P, 2, BANK])
        xi = m.sb("c_xi", [P, HALVES, ROWS + 2, WIDE])
        acc = m.sb("c_acc", [P, 4, STRIP, SIDE])
        xc = m.sb("c_xc", [P, HALVES, RING, SIDE])
        ot = m.sb("c_ot", [P, RING, JB, D_INNER])
        tap = m.sb("c_tap", [P, 9, P])
        tp = m.ps("c_tp", [P, BANK])
        xp = m.ps("c_xp", [P, 2, BANK])
        cp = m.ps("c_cp", [P, 2, BANK])
        op = m.ps("c_op", [P, 2, BANK])
        src = x1.rearrange("(h b p) c -> p h b c", b=JB, p=P)
        dst = xc_tok.rearrange("(h b p) d -> p h b d", b=JB, p=P)

        def rows_of(ap, first, count):
            return ap[:, bass.ds(first, count)] if not isinstance(first, int) else ap[:, first:first + count]

        class Inner:

            def __init__(self, b, first, slot, rows, after=None):
                self.b, self.slot, self.rows, self.after = b, slot, rows, after
                self.first = first
                self.loads, self.turned, self.tev, self.xev, self.mm = {}, {}, {}, {}, {}
                for k in range(min((rows + 1) // PAIR, RING // PAIR)):
                    self.load(k)

            def load(self, k):
                count, here = min(PAIR, self.rows - PAIR * k), PAIR * k % RING
                self.loads[k] = self.b.dma("sync", lambda e: e.dma_start(
                    xt[:, here:here + count], rows_of(src, self.first + PAIR * k, count)),
                    [self.turned.get(k - RING // PAIR)], f"load{here // PAIR}")

            def pair(self, k):
                b = self.b
                count = min(PAIR, self.rows - PAIR * k)
                wide = count * SIDE
                def tr(e):
                    for j in range(count * JB):
                        last = e.transpose(tp[:, j * P:(j + 1) * P], xt[:, PAIR * k % RING + j // JB, j % JB, :], const["eye"][:, :])
                    return last
                t = self.turned[k] = b.do("tensor", tr, [self.loads[k], self.tev.get(k - 1)], "pe")
                self.tev[k] = b.do("scalar", lambda e: e.activation(gn[:, k % 2, 0:wide], tp[:, 0:wide], ACT.Identity,
                                   bias=shift_col[:, 0:1], scale=scale_col[:, 0:1]), [t, self.mm.get(k - 2)], "gn")

            def product(self, k):
                b = self.b
                count = min(PAIR, self.rows - PAIR * k)
                wide = count * SIDE
                for half in range(HALVES):
                    t = self.mm[k] = b.do("tensor", lambda e, half=half: e.matmul(
                        xp[:, half, 0:wide], wts["w_in"][:, half * P:(half + 1) * P], gn[:, k % 2, 0:wide], start=True, stop=True),
                        [self.tev[k], self.xev.get((k - 1, half))], "pe")
                    def ev(e, half=half):
                        d = xi[:, half, self.slot + PAIR * k:self.slot + PAIR * k + count, 1:1 + SIDE]
                        v = xp[:, half, 0:wide].rearrange("p (r w) -> p r w", r=count)
                        return e.copy(d, v)
                    self.xev[k, half] = b.do("scalar", ev, [t, self.after], f"xev{half}")

        def one_turn(h0, last):
            b = Body(nc, sems)
            rows = ROWS - 1 if last else ROWS
            zero = b.do("vector", lambda e: e.memset(xi[:, :, ROWS + 1, :], 0.0), [], "zero") if last else None
            inner = Inner(b, h0 + 1, 2, rows)
            cev, oev, mark = {}, {}, {}
            sev, turned, stores = {}, {}, {}

            strips = [(c, half) for c in range(STRIPS) for half in (1, 0) if half or c in SHARED]
            place = {key: i % 4 for i, key in enumerate(strips)}

            def strip(c, half):
                into, i = acc[:, place[c, half]], strips.index((c, half))
                for t9 in range(9):
                    dy, dx = t9 // 3, t9 % 3
                    window = xi[:, half, STRIP * c + dy:STRIP * c + dy + STRIP, dx:dx + SIDE]
                    w = wts["conv_w"][:, half, t9:t9 + 1]
                    if t9 == 0:
                        a = b.do("vector", lambda e, window=window, w=w: e.tensor_scalar(into, window, w, None, ALU.mult),
                                 [inner.xev[(STRIP * c + STRIP - 1) // PAIR, half], sev.get(strips[i - 4]) if i >= 4 else None,
                                  zero], "acc")
                    else:
                        a = b.do("vector", lambda e, window=window, w=w: e.scalar_tensor_tensor(
                            out=into, in0=window, scalar=w, in1=into, op0=ALU.mult, op1=ALU.add), [a], "acc")
                mark[c, half] = mark["dve"] = a

            def strip_silu(c, half):
                sev[c, half] = b.do("scalar", lambda e: e.activation(
                    xc[:, half, STRIP * c % RING:STRIP * c % RING + STRIP], acc[:, place[c, half]], ACT.Silu,
                    bias=wts["conv_b"][:, half:half + 1]), [mark[c, half], turned.get(STRIP * (c + 1) - 1 - RING)], "silu")

            def conv(k):
                def mm(e):
                    for t9 in range(9):
                        dy, dx = t9 // 3, t9 % 3
                        last = e.matmul(cp[:, k % 2, :].rearrange("p (r w) -> p r w", r=PAIR), tap[:, t9, :],
                                        xi[:, 0, PAIR * k + dy:PAIR * k + dy + PAIR, dx:dx + SIDE],
                                        start=(t9 == 0), stop=(t9 == 8))
                    return last
                mark["pe"] = t = b.do("tensor", mm, [inner.xev[k, 0], zero, cev.get(max((i for i in cev if i % 2 == k % 2), default=None))], "pe")
                cev[k] = b.do("scalar", lambda e: e.activation(
                    xc[:, 0, PAIR * k % RING:PAIR * k % RING + PAIR, :], cp[:, k % 2, :].rearrange("p (r w) -> p r w", r=PAIR),
                    ACT.Silu, bias=wts["conv_b"][:, 0:1]), [t, turned.get(PAIR * (k + 1) - 1 - RING)], "silu")

            def turn(r):
                def tr(e):
                    for jb in range(JB):
                        for half in range(HALVES):
                            last = e.transpose(op[:, r % 2, jb * D_INNER + half * P:jb * D_INNER + (half + 1) * P],
                                               xc[:, half, r % RING, jb * P:(jb + 1) * P], const["eye"][:, :])
                    return last
                t = turned[r] = b.do("tensor", tr, [sev[r // STRIP, 1], sev.get((r // STRIP, 0)), cev.get(r // PAIR), oev.get(r - 2)], "pe")
                def ev(e):
                    return e.copy(ot[:, r % RING].rearrange("p b d -> p (b d)"), op[:, r % 2, :])
                oev[r] = b.do("scalar", ev, [t, stores.get((r - RING) // 8)], "oev")

            LAG = 4
            inner.pair(0)
            for k in range(PAIRS + LAG):
                if k + 1 < PAIRS:
                    inner.pair(k + 1)
                if k < PAIRS:
                    inner.product(k)
                if 1 <= k <= PAIRS and PAIR * (k - 1) // STRIP not in SHARED:
                    conv(k - 1)
                if k < PAIRS and k % 2 == 1:
                    for half in (1, 0):
                        if (k // 2, half) in strips:
                            strip(k // 2, half)
                if k >= LAG and (k - LAG) % 2 == 0:
                    for half in (1, 0):
                        if ((k - LAG) // 2, half) in strips:
                            strip_silu((k - LAG) // 2, half)
                if k >= LAG:
                    for r in (PAIR * (k - LAG), PAIR * (k - LAG) + 1):
                        turn(r)
                    if r % 8 == 7:
                        here = r % RING - 7
                        stores[r // 8] = b.dma("sync", lambda e, r=r, here=here: e.dma_start(
                            rows_of(dst, h0 + (r - 7), 8), ot[:, here:here + 8]), [oev[r]], f"store{here // 8}")
                if k + RING // PAIR < (rows + 1) // PAIR:
                    inner.load(k + RING // PAIR)
            b.do("sync", lambda e: e.nop(), [stores[ROWS // 8 - 1], stores[ROWS // 8 - 2]])
            b.do("gpsimd", lambda e: e.tensor_copy(xi[:, :, 0:2, :], xi[:, :, ROWS:ROWS + 2, :]), [mark["pe"], mark["dve"]], None)
            b.run()

        b = Body(nc, sems)
        z = b.do("vector", lambda e: e.memset(xi[:, :, :, :].rearrange("p a r w -> p (a r w)"), 0.0), [], "zero")
        for t9 in range(9):
            b.do("vector", lambda e, t9=t9: e.tensor_scalar(tap[:, t9, :], const["eye"][:, :],
                 wts["conv_w"][:, 0, t9:t9 + 1], None, ALU.mult))
        top = Inner(b, 0, 1, 1, z)
        top.pair(0)
        top.product(0)
        b.run()
        turns = SIDE // ROWS
        with nc.Fori(0, turns - 1) as it:
            one_turn(it * ROWS, False)
        one_turn((turns - 1) * ROWS, True)


def scan_phase(nc, sems, k, xc_tok, y_before, y_k, wts, const, turns_limit=None):
    T = BANK
    SUBS = T // P
    TILES = TOKENS // T
    PER_BODY = 32
    NDA, NDB, NP_, NCB = 4, 4, 4, 6
    backwards = k >= 2
    by_column = k % 2 == 1
    GUARD = 20.0
    flow = slice(None, None, -1) if backwards else slice(None)
    tokens = slice(0, T) if backwards else slice(1, T + 1)
    restart = T if backwards else 0
    last_token = 0 if backwards else T
    with ExitStack() as stack:
        m = Memory(nc, stack)
        xt = m.sb(f"s{k}_xt", [P, SUBS, D_INNER])
        xc = m.sb(f"s{k}_xc", [P, 2, HALVES, T])
        mid = m.sb(f"s{k}_mid", [96, T], BF16)
        parts = m.sb(f"s{k}_parts", [96, 2, T], BF16)
        low = m.sb(f"s{k}_low", [DT_RANK, T])
        e1 = m.sb(f"s{k}_e1", [P, HALVES, T])
        rest = e1[0:96, 0, :]
        delta = m.sb(f"s{k}_delta", [P, 2, HALVES, T])
        dx = m.sb(f"s{k}_dx", [P, 2, HALVES, T])
        da = m.sb(f"s{k}_da", [P, NDA, HALVES, T + 1])
        h = m.sb(f"s{k}_h", [P, D_STATE, HALVES, T + 1])
        db = m.sb(f"s{k}_db", [P, NDB, HALVES, T + 1])
        cb = m.sb(f"s{k}_cb", [P, NCB, T])
        prod = m.sb(f"s{k}_prod", [P, NP_, HALVES, T])
        yt = m.sb(f"s{k}_yt", [P, SUBS, D_INNER])
        yb = m.sb(f"s{k}_yb", [P, SUBS, D_INNER]) if k else None
        pb = m.ps(f"s{k}_pb", [P, 2, BANK])
        pc = m.ps(f"s{k}_pc", [P, 2, BANK])
        py = m.ps(f"s{k}_py", [P, 2, BANK])
        pr = m.ps(f"s{k}_pr", [P, 2, BANK])

        if by_column:
            view = lambda t: t.rearrange("(b p w) d -> w p b d", b=JB, p=P)
        else:
            view = lambda t: t.rearrange("(i b p) d -> i p b d", b=JB, p=P)
        src, dst = view(xc_tok), view(y_k)
        before = view(y_before) if k else None

        b = Body(nc, sems)
        b.do("vector", lambda e: e.memset(h[:, :, :, last_token], 0.0))
        b.do("vector", lambda e: e.memset(da[:, :, :, restart], 0.0))
        b.do("scalar", lambda e: e.preload_act_table_set("natural_log_exp_and_others"))
        b.run()

        def one_turn(it, first=False, last=False):
            b = Body(nc, sems)
            loads, turned, xc_ev, xc_used, split, spread_b, spread_c, dts, dx_ready, delta_ready = ({} for _ in range(10))
            exps, b_mm, inputs, carried, scans, c_mm, c_ev, prods, sums, y_ev, stores = ({} for _ in range(11))
            before_loads, before_used, middle_part = {}, {}, {}
            pr_free = [None, None]

            def line(g, i):
                tile = (TILES - 1 - g) - it * PER_BODY if backwards else it * PER_BODY + g
                return tile * (T // SIDE) + i

            def load(g):
                for i in range(T // SIDE):
                    loads[g] = b.dma("sync", lambda e, i=i: e.dma_start(
                        xt[:, i * JB:(i + 1) * JB, :], src[line(g, i)]), [turned.get(g - 1)], f"load{g % 2}")

            def prepare(g):
                s = g % 2
                for half in range(HALVES):
                    def tr(e, half=half):
                        for j in range(SUBS):
                            last = e.transpose(pr[:, half, j * P:(j + 1) * P], xt[:, j, half * P:(half + 1) * P],
                                               const["eye"][:, :])
                        return last
                    turned[g] = b.do("tensor", tr, [loads.get(g), pr_free[half]], "prep")
                yield
                for half in range(HALVES):
                    xc_ev[g] = b.do("scalar", lambda e, half=half: e.copy(
                        xc[:, s, half, :], pr[:, half, :]), [turned[g], dx_ready.get(g - 2), xc_used.get(g - 2)], "prep_act")
                yield
                def mm(e):
                    for half in range(HALVES):
                        last = e.matmul(pr[0:96 + DT_RANK, 0, :], wts["proj"][:, half, :], xc[:, s, half, :],
                                        start=(half == 0), stop=(half == HALVES - 1))
                    return last
                t = b.do("tensor", mm, [xc_ev[g]], "prep")
                yield
                b.do("scalar", lambda e: e.copy(low[:, :], pr[96:96 + DT_RANK, 0, :]), [t, dts.get(g - 1)])
                up = b.do("scalar", lambda e: e.copy(parts[:, s], pr[0:96, 0, :]), [spread_c.get(g - 2)], "prep_act")
                yield
                re = b.do("vector", lambda e: e.tensor_tensor(rest, pr[0:96, 0, :], parts[:, s], ALU.subtract),
                          [up, split.get(g - 1), delta_ready.get(g - 1)], "prep_dve")
                yield
                md = b.do("scalar", lambda e: e.copy(mid[:, :], rest), [re, split.get(g - 1)], "prep_act")
                for half in range(HALVES):
                    dts[g] = b.do("tensor", lambda e, half=half: e.matmul(
                        pr[:, half, :], wts["dt_w"][:, half * P:(half + 1) * P], low[:, :], start=True, stop=True),
                        [up, re], "prep")
                yield
                middle_part[g] = b.do("scalar", lambda e: e.copy(parts[32:64, s], mid[32:64]), [md], "prep_act")
                split[g] = b.do("vector", lambda e: e.tensor_tensor(parts[64:96, s], rest[64:96], mid[64:96], ALU.subtract), [md], "prep_dve")
                for half in range(HALVES):
                    rl = b.do("scalar", lambda e, half=half: e.activation(
                        e1[:, half, :], pr[:, half, :], ACT.Relu, bias=wts["guard_less_dt_b"][:, half:half + 1], scale=-1.0),
                        [dts[g], split[g]], "prep_act")
                yield
                ex = b.do("scalar", lambda e: e.activation(e1[:, :, :], e1[:, :, :], ACT.Exp, scale=-1.0, bias=wts["guard"][:, 0:1]), [rl], "prep_act")
                yield
                ln = b.do("scalar", lambda e: e.activation(e1[:, :, :], e1[:, :, :], ACT.Ln, bias=1.0), [ex], "prep_act")
                yield
                for half in range(HALVES):
                    delta_ready[g] = pr_free[0] = pr_free[1] = b.do("vector", lambda e, half=half: e.scalar_tensor_tensor(
                        out=delta[:, s, half, :], in0=pr[:, half, :], scalar=wts["dt_b"][:, half:half + 1],
                        in1=e1[:, half, :], op0=ALU.add, op1=ALU.max), [ln, exps.get((g - 2, D_STATE - 1))], "prep_dve")
                yield
                dx_ready[g] = b.do("gpsimd", lambda e: e.tensor_tensor(
                    dx[:, s], delta[:, s], xc[:, s], ALU.mult), [delta_ready[g], inputs.get((g - 2, D_STATE - 1))], "prep_pool")
                yield

            def spread(g, n):
                s = g % 2
                b_mm[g, n] = b.do("tensor", lambda e: e.matmul(pb[:, n % 2, :], const["spread"][:, n, :],
                    parts[:, s, :], start=True, stop=True),
                    [split.get(g), middle_part.get(g), inputs.get((g, n - 2) if n >= 2 else (g - 1, D_STATE + n - 2))], "bmm")
                c_mm[g, n] = spread_c[g] = b.do("tensor", lambda e: e.matmul(pc[:, n % 2, :], const["spread"][:, D_STATE + n, :],
                    parts[:, s, :], start=True, stop=True),
                    [c_ev.get((g, n - 2) if n >= 2 else (g - 1, D_STATE + n - 2))], "cmm")
                slot = n % NDA
                before = (g, n - NDA) if n >= NDA else (g - 1, D_STATE + n - NDA)
                for half in range(HALVES):
                    exps[g, n] = b.do("scalar", lambda e, half=half: e.activation(
                        da[:, slot, half, tokens], delta[:, s, half, :], ACT.Exp, scale=wts["a_neg"][:, half, n:n + 1]),
                        [delta_ready.get(g), scans.get(before)], "exp")
                at = (g * D_STATE + n) % NCB
                before = (g, n - NCB) if n >= NCB else (g - 1, D_STATE + n - NCB)
                c_ev[g, n] = b.do("scalar", lambda e: e.copy(cb[:, at, :], pc[:, n % 2, :]), [c_mm[g, n], prods.get(before)], "cev")

            def enter(g, n):
                at = n % NDB
                before = (g, n - NDB) if n >= NDB else (g - 1, D_STATE + n - NDB)
                inputs[g, n] = b.do("vector", lambda e: e.tensor_tensor(
                    db[:, at, :, tokens], dx[:, g % 2], pb[:, n % 2, :].unsqueeze(1).to_broadcast([P, HALVES, T]), ALU.mult),
                    [b_mm[g, n], dx_ready.get(g), scans.get(before)], "v")
                carried[g, n] = b.do("scalar", lambda e: e.copy(db[:, at, :, restart], h[:, n, :, last_token]),
                    [scans.get(before)], "carry")

            def state(g, n):
                of_a, at = n % NDA, n % NDB
                line_of = lambda v: v.rearrange("p a t -> p (a t)")[:, flow]
                scans[g, n] = b.do("vector", lambda e: e.tensor_tensor_scan(
                    line_of(h[:, n]), line_of(da[:, of_a]), line_of(db[:, at]), 0.0, ALU.mult, ALU.add),
                    [inputs[g, n], carried[g, n], exps[g, n], prods.get((g - 1, n))], "v")
                of_c, slot = (g * D_STATE + n) % NCB, n % NP_
                before = (g, n - NP_, 1) if n >= NP_ else (g - 1, D_STATE + n - NP_, 1)
                prods[g, n] = b.do("gpsimd", lambda e: e.tensor_tensor(
                    prod[:, slot], h[:, n, :, tokens], cb[:, of_c, :].unsqueeze(1).to_broadcast([P, HALVES, T]), ALU.mult),
                    [scans[g, n], c_ev[g, n], sums.get(before)], "prod")

            def total(g, n):
                slot = n % NP_
                for half in range(HALVES):
                    def mm(e, half=half):
                        for j in range(SUBS):
                            out = py[:, j // 2, (j % 2) * D_INNER + half * P:(j % 2) * D_INNER + (half + 1) * P]
                            first = n == 0 and half == 0 and j % 2 == 0
                            last = e.matmul(out, prod[:, slot, half, j * P:(j + 1) * P], const["eye"][:, :], start=first,
                                            stop=(n == D_STATE - 1), is_transpose=True, skip_group_check=True)
                        return last
                    sums[g, n, half] = b.do("tensor", mm, [prods[g, n], y_ev.get(g - 1) if n == 0 else None], "sum")

            def load_before(g):
                for i in range(T // SIDE):
                    before_loads[g] = b.dma("sync", lambda e, i=i: e.dma_start(
                        yb[:, i * JB:(i + 1) * JB, :], before[line(g, i)]), [before_used.get(g - 1)], f"before{g % 2}")

            def add_before(g):
                def mm(e):
                    for j in range(SUBS):
                        last = e.matmul(py[:, j // 2, (j % 2) * D_INNER:(j % 2 + 1) * D_INNER], const["eye"][:, :],
                                        yb[:, j, :], start=False, stop=False, skip_group_check=True)
                    return last
                before_used[g] = b.do("tensor", mm, [before_loads[g]], "before")

            def skip(g):
                def mm(e):
                    for j in range(SUBS):
                        for half in range(HALVES):
                            out = py[:, j // 2, (j % 2) * D_INNER + half * P:(j % 2) * D_INNER + (half + 1) * P]
                            last = e.matmul(out, xc[:, g % 2, half, j * P:(j + 1) * P], wts["d_diag"][:, half, :],
                                            start=False, stop=False, skip_group_check=True)
                    return last
                xc_used[g] = b.do("tensor", mm, [], "sum")

            def store(g):
                for bank in range(2):
                    y_ev[g] = b.do("scalar", lambda e, bank=bank: e.copy(
                        yt[:, 2 * bank:2 * bank + 2, :].rearrange("p j d -> p (j d)"), py[:, bank, :]),
                        [sums[g, D_STATE - 1, 1], stores.get(g - 1)], "yev")
                for i in range(T // SIDE):
                    stores[g] = b.dma("sync", lambda e, i=i: e.dma_start(
                        dst[line(g, i)], yt[:, i * JB:(i + 1) * JB, :]), [y_ev[g]], f"store{g % 2}")

            if first:
                load(0)
                for _ in prepare(0):
                    pass
                b.run()
                return
            LAG = 3
            order = [(g, n) for g in range(PER_BODY) for n in range(D_STATE)]
            summed = iter(order)

            def sum_next():
                g, n = next(summed)
                total(g, n)
                if n == 0 and k == 0:
                    skip(g)
                if n == D_STATE // 2 and k:
                    add_before(g)
                if n == D_STATE - 1:
                    store(g)

            spread(0, 0)
            spread(0, 1)
            enter(0, 0)
            load(1)
            if k:
                load_before(0)
            for i, (g, n) in enumerate(order):
                more = g + 1 < PER_BODY or not last
                if n == 0:
                    steps = prepare(g + 1) if more else iter(())
                if n == 4 and (g + 2 < PER_BODY or (g + 2 == PER_BODY and not last)):
                    load(g + 2)
                if n == 12 and k and g + 1 < PER_BODY:
                    load_before(g + 1)
                if i + 2 < len(order):
                    spread(*order[i + 2])
                if i + 1 < len(order):
                    enter(*order[i + 1])
                state(g, n)
                if i >= LAG:
                    sum_next()
                next(steps, None)
            for _ in range(LAG):
                sum_next()
            b.do("sync", lambda e: e.nop(), [stores[PER_BODY - 1], stores[PER_BODY - 2]])
            b.run()

        turns = turns_limit or TILES // PER_BODY
        one_turn(0, first=True)
        with nc.Fori(0, turns - 1) as it:
            one_turn(it)
        one_turn(turns - 1, last=True)


def output_phase(nc, sems, y, x1, out, wts, const, scale_col, shift_col):
    K = 8
    PER_BODY = 16
    LOADS = 3
    with ExitStack() as stack:
        m = Memory(nc, stack)
        yt = m.sb("o_y", [P, LOADS, K, D_INNER])
        xt = m.sb("o_x", [P, LOADS, K, C])
        st = m.sb("o_st", [P, 2, K, 6])
        mv = m.sb("o_mv", [P, 2, K, 2])
        std = m.sb("o_std", [P, 2, K])
        rstd = m.sb("o_rstd", [P, 2, K])
        nmr = m.sb("o_nmr", [P, 2, K])
        gn = m.sb("o_gn", [P, 2, BANK])
        zs = m.sb("o_zs", [P, 2, HALVES, BANK])
        yn = m.sb("o_yn", [P, 2, HALVES, BANK])
        ot = m.sb("o_ot", [P, 2, K, C])
        tp = m.ps("o_tp", [P, BANK])
        zp = m.ps("o_zp", [P, 2, BANK])
        yp = m.ps("o_yp", [P, 2, BANK])
        op = m.ps("o_op", [P, 2, BANK])
        view = lambda t: t.rearrange("(i q p j) c -> i q p j c", q=PER_BODY, j=K, p=P)
        ysrc, xsrc, dst = view(y), view(x1), view(out)
        flat = lambda v: v.rearrange("p j d -> p (j d)")
        with nc.Fori(0, TOKENS // (K * P * PER_BODY)) as it:
            b = Body(nc, sems)
            ynt, tev, zmm, zev, zmul, yev, omm, oev, stored, loaded, normed, ytr = ({} for _ in range(12))

            def load(q):
                s = q % LOADS
                ly = b.dma("sync", lambda e: e.dma_start(yt[:, s], ysrc[it, q]), [ynt.get(q - LOADS)], f"ly{s}")
                lx = b.dma("sync", lambda e: e.dma_start(xt[:, s], xsrc[it, q]), [oev.get((q - LOADS, 1))], f"lx{s}")
                loaded[q] = (ly, lx)

            def normalize(q):
                s, l = q % 2, q % LOADS
                for j in range(K):
                    s0 = b.do("vector", lambda e, j=j: e.bn_stats(st[:, s, j, :], yt[:, l, j, :]), [loaded[q][0]], "v")
                for j in range(K):
                    s1 = b.do("vector", lambda e, j=j: e.bn_aggr(mv[:, s, j, :], st[:, s, j, :]), [s0], "v")
                v0 = b.do("vector", lambda e: e.tensor_scalar(std[:, s], mv[:, s, :, 1], 1e-5, None, ALU.add), [s1], "v")
                q0 = b.do("scalar", lambda e: e.activation(std[:, s], std[:, s], ACT.Sqrt), [v0], "sqrt")
                v1 = b.do("vector", lambda e: e.reciprocal(rstd[:, s], std[:, s]), [q0], "v")
                v2 = b.do("vector", lambda e: e.scalar_tensor_tensor(
                    out=nmr[:, s], in0=mv[:, s, :, 0], scalar=-1.0, in1=rstd[:, s], op0=ALU.mult, op1=ALU.mult), [v1], "v")
                for j in range(K):
                    normed[q] = b.do("vector", lambda e, j=j: e.tensor_scalar(
                        yt[:, l, j, :], yt[:, l, j, :], rstd[:, s, j:j + 1], nmr[:, s, j:j + 1], ALU.mult, ALU.add),
                        [v2], "v")

            def inner(q, f):
                i, l = q * 2 + f, q % LOADS
                def tr(e):
                    for j in range(4):
                        last = e.transpose(tp[:, j * P:(j + 1) * P], xt[:, l, 4 * f + j, :], const["eye"][:, :])
                    return last
                t = b.do("tensor", tr, [loaded[q][1], tev.get(i - 1)], "t")
                tev[i] = b.do("scalar", lambda e: e.activation(gn[:, i % 2, :], tp[:, :], ACT.Identity,
                              bias=shift_col[:, 0:1], scale=scale_col[:, 0:1]), [t, zmm.get(i - 2)], "gn")

            def outer(q, f):
                i, s, l = q * 2 + f, q % 2, q % LOADS
                for half in range(HALVES):
                    def ty(e, half=half):
                        for j in range(4):
                            last = e.transpose(yp[:, half, j * P:(j + 1) * P], yt[:, l, 4 * f + j, half * P:(half + 1) * P],
                                               const["eye"][:, :])
                        return last
                    ytr[half] = ynt[q] = b.do("tensor", ty, [normed[q], yev.get((i - 1, half))], "t")
                for half in range(HALVES):
                    yev[i, half] = b.do("scalar", lambda e, half=half: e.activation(
                        yn[:, i % 2, half, :], yp[:, half, :], ACT.Identity, bias=wts["ln_b"][:, half:half + 1],
                        scale=wts["ln_w"][:, half:half + 1]), [ytr[half], omm.get(i - 2)], "yn")
                for half in range(HALVES):
                    t = zmm[i] = b.do("tensor", lambda e, half=half: e.matmul(
                        zp[:, half, :], wts["w_in"][:, D_INNER + half * P:D_INNER + (half + 1) * P], gn[:, i % 2, :],
                        start=True, stop=True), [tev[i], zev.get((i - 1, half))], "t")
                    zev[i, half] = b.do("scalar", lambda e, half=half: e.activation(
                        zs[:, i % 2, half, :], zp[:, half, :], ACT.Silu), [t, zmul.get((i - 2, half))], "z")
                for half in range(HALVES):
                    zmul[i, half] = b.do("gpsimd" if half else "vector", lambda e, half=half: e.tensor_tensor(
                        yn[:, i % 2, half, :], yn[:, i % 2, half, :], zs[:, i % 2, half, :], ALU.mult),
                        [yev[i, half], zev[i, half]], f"zmul{half}")

            def product(q, f):
                i, s, l = q * 2 + f, q % 2, q % LOADS
                def mo(e):
                    for j in range(4):
                        for half in range(HALVES):
                            last = e.matmul(op[:, i % 2, j * P:(j + 1) * P], yn[:, i % 2, half, j * P:(j + 1) * P],
                                            wts["w_out"][:, half, :], start=(half == 0), stop=(half == HALVES - 1))
                    return last
                t = omm[i] = b.do("tensor", mo, [zmul[i, 0], zmul[i, 1], oev.get((q - 1, f))], "t")
                oev[q, f] = b.do("vector", lambda e: e.tensor_tensor(
                    flat(ot[:, s, 4 * f:4 * f + 4]), op[:, i % 2, :], flat(xt[:, l, 4 * f:4 * f + 4]), ALU.add),
                    [t, stored.get(q - 2)], "oev")
                if f == 1:
                    stored[q] = b.dma("sync", lambda e: e.dma_start(dst[it, q], ot[:, s]), [oev[q, 1]], f"store{s}")

            N = PER_BODY
            groups = [(q, f) for q in range(N) for f in range(2)]
            for q in range(LOADS - 1):
                load(q)
            normalize(0)
            inner(0, 0)
            for i, (q, f) in enumerate(groups):
                if f == 0 and q + 2 < N and q >= 1:
                    load(q + 1)
                if f == 0 and q + 1 < N:
                    if q + 1 >= 2 and q + 1 not in loaded:
                        load(q + 1)
                    normalize(q + 1)
                if i + 1 < len(groups):
                    inner(*groups[i + 1])
                outer(q, f)
                if i >= 1:
                    product(*groups[i - 1])
            product(*groups[-1])
            b.do("sync", lambda e: e.nop(), [stored[N - 1], stored[N - 2]])
            b.run()


_WEIGHTS = {
    "ln_scale": (P, 1), "ln_bias": (P, 1), "Wq": (C, C), "Wk": (C, C), "Wvg": (C, 2 * C), "Wb": (C, HEADS), "Wo": (C, C),
    "w_in": (C, 2 * D_INNER), "conv_w": (P, HALVES, 9), "conv_b": (P, HALVES),
    "proj": (DIRECTIONS, P, HALVES, 96 + DT_RANK),
    "dt_w": (DIRECTIONS, DT_RANK, D_INNER), "dt_b": (DIRECTIONS, P, HALVES), "A_logs": (DIRECTIONS, P, HALVES, D_STATE),
    "Ds": (P, HALVES, DIRECTIONS), "ln_w": (P, HALVES), "ln_b": (P, HALVES), "w_out": (P, HALVES, C),
}


def build(nc, x, dram, out, eye, mean, group_of, spread, phases="0123456789", outputs=None, scan_turns=None):
    f = lambda name, shape: (outputs or {}).get(name) or nc.dram_tensor(name, shape, F32).ap()
    zn_t = f("zn_t", (SIDE // 8, C, 8 * SIDE))
    bias_d = f("bias_d", (HEADS, TOKENS))
    x1 = f("x1", (TOKENS, C))
    xc_tok = f("xc_tok", (TOKENS, D_INNER))
    ys = [f(f"y{k}", (TOKENS, D_INNER)) for k in range(DIRECTIONS)]
    with ExitStack() as stack:
        m = Memory(nc, stack)
        sems = [stack.enter_context(nc.semaphore(f"s{i}")) for i in range(40)]
        assert all(b.num == a.num + 1 for a, b in zip(sems, sems[1:]))
        const = {"eye": m.sb("eye", [P, P]), "mean": m.sb("mean", [P, P]), "group_of": m.sb("group_of", [P, GROUPS]),
                 "spread": m.sb("spread", [96, 2 * D_STATE, P], BF16)}
        scale_row, shift_row = m.sb("scale_row", [P, GROUPS]), m.sb("shift_row", [P, GROUPS])
        scale_col, shift_col = m.sb("scale_col", [P, 1]), m.sb("shift_col", [P, 1])
        per_direction = ("proj", "dt_w", "dt_b", "A_logs")
        wts = {}
        for name, shape in _WEIGHTS.items():
            if name in per_direction:
                wts[name] = [m.sb(f"w_{name}{k}", list(shape[1:])) for k in range(DIRECTIONS)]
            else:
                wts[name] = m.sb(f"w_{name}", list(shape))
        whole = lambda t: t[tuple(slice(None) for _ in t.shape)]
        wts["a_neg"] = [m.sb(f"a_neg{k}", [P, HALVES, D_STATE]) for k in range(DIRECTIONS)]
        wts["guard_less_dt_b"] = [m.sb(f"gdt{k}", [P, HALVES]) for k in range(DIRECTIONS)]
        guard = m.sb("guard", [P, 1])
        d_sum, d_diag = m.sb("d_sum", [P, HALVES]), m.sb("d_diag", [P, HALVES, P])

        with ExitStack() as start:
            spread32 = Memory(nc, start).sb("spread32", [96, 2 * D_STATE, P])
            b = Body(nc, sems)
            for tile, source in ((const["eye"], eye), (const["mean"], mean), (const["group_of"], group_of), (spread32, spread)):
                ld = b.dma("sync", lambda e, tile=tile, source=source: e.dma_start(whole(tile), source), [], "load")
            for name in _WEIGHTS:
                tiles = wts[name] if name in per_direction else [wts[name]]
                for k, tile in enumerate(tiles):
                    source = dram[name][k] if name in per_direction else dram[name]
                    ld = b.dma("sync", lambda e, tile=tile, source=source: e.dma_start(whole(tile), source), [], "load")
            b.do("vector", lambda e: e.memset(guard[:, :], 20.0))
            b.do("vector", lambda e: e.tensor_copy(const["spread"][:, :, :], spread32[:, :, :]), [ld])
            ds = b.do("vector", lambda e: e.tensor_reduce(d_sum[:, :], wts["Ds"][:, :, :], AX_X, ALU.add), [ld], "v")
            for half in range(HALVES):
                b.do("vector", lambda e, half=half: e.tensor_scalar(d_diag[:, half, :], const["eye"][:, :], d_sum[:, half:half + 1],
                     None, ALU.mult), [ds])
            for k in range(DIRECTIONS):
                b.do("vector", lambda e, k=k: e.tensor_scalar(wts["guard_less_dt_b"][k][:, :], wts["dt_b"][k][:, :], -1.0, 20.0,
                     ALU.mult, ALU.add), [ld])
                ex = b.do("scalar", lambda e, k=k: e.activation(wts["a_neg"][k][:, :, :], wts["A_logs"][k][:, :, :], ACT.Exp), [ld], "a")
                b.do("vector", lambda e, k=k: e.tensor_scalar(wts["a_neg"][k][:, :, :], wts["a_neg"][k][:, :, :], -1.0, None,
                     ALU.mult), [ex])
            b.run()

        if "0" in phases:
            group_stats(nc, sems, "g0", x, 1e-5, const, scale_row, shift_row)
        if "1" in phases:
            norm_phase(nc, sems, x, zn_t, bias_d, wts, const, scale_row, shift_row)
        if "2" in phases:
            attention_phase(nc, sems, x, zn_t, bias_d, x1, wts, const)
        if "3" in phases:
            group_stats(nc, sems, "g1", x1, 1e-5, const, scale_row, shift_row, (scale_col, shift_col))
        if "4" in phases:
            conv_phase(nc, sems, x1, xc_tok, wts, const, scale_col, shift_col)
        for k in range(DIRECTIONS):
            if str(5 + k) in phases:
                own = {n: wts[n][k] for n in per_direction + ("a_neg", "guard_less_dt_b")}
                scan_phase(nc, sems, k, xc_tok, ys[k - 1] if k else None, ys[k], {**wts, **own, "guard": guard, "d_diag": d_diag}, const, scan_turns)
        if "9" in phases:
            output_phase(nc, sems, ys[-1], x1, out, wts, const, scale_col, shift_col)


def laid_out(w):
    halves = lambda a: np.ascontiguousarray(np.moveaxis(a.reshape((HALVES, P) + a.shape[1:]), 0, 1))
    xp = w["L1_conv_x_proj_w"]
    proj = np.zeros((DIRECTIONS, D_INNER, 96 + DT_RANK), np.float32)
    for k in range(DIRECTIONS):
        for at in (0, 32, 64):
            proj[k, :, at:at + 2 * D_STATE] = xp[k, DT_RANK:].T
        proj[k, :, 96:] = xp[k, :DT_RANK].T
    each = lambda a: np.stack([halves(a[k]) for k in range(DIRECTIONS)])
    return {
        "ln_scale": w["L0_conv_ln_scale"].reshape(P, 1), "ln_bias": w["L0_conv_ln_bias"].reshape(P, 1),
        "Wq": w["L0_conv_Wq"], "Wk": w["L0_conv_Wk"], "Wvg": np.concatenate([w["L0_conv_Wv"], w["L0_conv_Wg"]], 1),
        "Wb": w["L0_conv_Wb"], "Wo": w["L0_conv_Wo"], "w_in": w["L1_conv_w_in"].T,
        "conv_w": halves(w["L1_conv_conv_w"].reshape(D_INNER, 9)), "conv_b": halves(w["L1_conv_conv_b"]),
        "proj": each(proj), "dt_w": np.moveaxis(w["L1_conv_dt_w"], 1, 2),
        "dt_b": each(w["L1_conv_dt_b"]), "A_logs": each(w["L1_conv_A_logs"].reshape(DIRECTIONS, D_INNER, D_STATE)),
        "Ds": halves(w["L1_conv_Ds"].reshape(DIRECTIONS, D_INNER).T), "ln_w": halves(w["L1_conv_ln_w"]),
        "ln_b": halves(w["L1_conv_ln_b"]), "w_out": halves(w["L1_conv_w_out"].T),
    }


def constants():
    spread = np.zeros((96, 2 * D_STATE, P), np.float32)
    for n in range(2 * D_STATE):
        for at in (0, 32, 64):
            spread[at + n, n, :] = 1.0
    return {"eye": np.eye(P, dtype=np.float32), "mean": np.full((P, P), 1.0 / P, np.float32),
            "group_of": np.repeat(np.eye(GROUPS, dtype=np.float32), PER_GROUP, axis=0), "spread": spread}


def kernel(**inputs):
    import concourse.bacc as bacc
    from concourse.bass_utils import run_bass_kernel_spmd

    w = {n: np.asarray(a) for n, a in inputs.items()}
    arrays = {"x": np.ascontiguousarray(w["x"]).reshape(TOKENS, C)}
    arrays.update({n: np.ascontiguousarray(a) for n, a in laid_out(w).items()})
    arrays.update(constants())
    nc = bacc.Bacc("TRN2", target_bir_lowering=False, num_devices=1)
    dram = {n: nc.dram_tensor(f"in_{n}", a.shape, F32, kind="ExternalInput").ap() for n, a in arrays.items()}
    out = nc.dram_tensor("out", (TOKENS, C), F32, kind="ExternalOutput").ap()
    build(nc, dram["x"], dram, out, dram["eye"], dram["mean"], dram["group_of"], dram["spread"])
    r = run_bass_kernel_spmd(nc, [{f"in_{n}": a for n, a in arrays.items()}], core_ids=[0])
    return r.results[0]["out"].reshape(1, SIDE, SIDE, C)
```
